# Optimizing a Trainium2 kernel written in Bass

```python
import numpy as np
import jax
import jax.numpy as jnp

def _softmax(x, axis=-1):
    return jax.nn.softmax(x, axis=axis)

def _gelu(x):
    return jax.nn.gelu(x, approximate=True)

def _silu(x):
    return jax.nn.silu(x)

def _sigmoid(x):
    return jax.nn.sigmoid(x)

def _layernorm(x, axis=-1, eps=1e-05):
    m = jnp.mean(x, axis=axis, keepdims=True)
    v = jnp.var(x, axis=axis, keepdims=True)
    return (x - m) / jnp.sqrt(v + eps)

def _scatter_add(tgt, idx, src, axis=0):
    return tgt.at[idx].add(src)

def _segment_sum(src, seg, n):
    return jax.ops.segment_sum(src, seg, n)
kernel_name = 'mk_vit_tower_cls_d2_tok_img256_r4_11eb9c'

def setup_inputs(seed: int=0):
    np.random.seed(seed)
    _w = jnp.asarray

    def _rec_inputs():
        import jax
        import jax.numpy as jnp
        _rk = jax.random.key(seed)
        x = 7.22013e-05 + 1.00017 * jax.random.normal(jax.random.fold_in(_rk, 1), (2, 64, 64, 64), jnp.float32)
        cls_tok = 0.02 * jax.random.normal(jax.random.fold_in(_rk, 5), (1, 1, 64), jnp.float32)
        return (x, cls_tok)
    x, cls_tok = _rec_inputs()

    def _L0_tok_setup():
        import jax, jax.numpy as jnp
        import numpy as np
        K = 3
        PAD = (K - 1) // 2
        BN_EPS = 1e-05

        def _unfold(x):
            b, c, h, w = x.shape
            xp = jnp.pad(x, ((0, 0), (0, 0), (PAD, PAD), (PAD, PAD)))
            shifts = [xp[:, :, i:i + h, j:j + w] for i in range(K) for j in range(K)]
            return jnp.stack(shifts, axis=2)
        key = jax.random.key(seed)
        ks = jax.random.split(key, 4)
        b, c, h, w = (8, 64, 64, 64)
        cr = c // 4
        x = jax.random.normal(ks[0], (b, c, h, w), dtype=jnp.float32)
        conv1_w = jax.random.normal(ks[1], (cr, c), dtype=jnp.float32) * (1.0 / np.sqrt(c))
        conv1_b = jnp.zeros((cr,), dtype=jnp.float32)
        bn_gamma = jnp.ones((cr,), dtype=jnp.float32)
        bn_beta = jnp.zeros((cr,), dtype=jnp.float32)
        bn_mean = jnp.zeros((cr,), dtype=jnp.float32)
        bn_var = jnp.ones((cr,), dtype=jnp.float32)
        conv2_w = jax.random.normal(ks[2], (K * K, cr), dtype=jnp.float32) * (1.0 / np.sqrt(cr))
        conv2_b = jnp.zeros((K * K,), dtype=jnp.float32)
        return {'x': x, 'conv1_w': conv1_w, 'conv1_b': conv1_b, 'bn_gamma': bn_gamma, 'bn_beta': bn_beta, 'bn_mean': bn_mean, 'bn_var': bn_var, 'conv2_w': conv2_w, 'conv2_b': conv2_b}
    _L0_tok_all = _L0_tok_setup()
    _L0_tok_in = {k: v for k, v in _L0_tok_all.items() if k in ('conv1_w', 'conv1_b', 'bn_gamma', 'bn_beta', 'bn_mean', 'bn_var', 'conv2_w', 'conv2_b')}
    del _L0_tok_all

    def _L0_attn_setup():
        import jax, jax.numpy as jnp
        import numpy as np
        key = jax.random.key(seed)
        k1, k2, k3 = jax.random.split(key, 3)
        d = 64
        x = jax.random.normal(k1, (8, 512, d), dtype=jnp.float32)
        Wq = jax.random.normal(k2, (d, d), dtype=jnp.float32) * d ** (-0.5)
        Wk = jax.random.normal(k3, (d, d), dtype=jnp.float32) * d ** (-0.5)
        return {'x': x, 'Wq': Wq, 'Wk': Wk}
    _L0_attn_all = _L0_attn_setup()
    _L0_attn_in = {k: v for k, v in _L0_attn_all.items() if k in ('Wq', 'Wk')}
    del _L0_attn_all

    def _L0_ffn_setup():
        import jax, jax.numpy as jnp
        import numpy as np
        B, T, C = (64, 96, 64)
        NH, NKV = (4, 2)
        HD = C // NH
        NREP = NH // NKV
        NE, TOPK = (8, 2)
        HID = int(8 / 3 * C)
        EPS_RMS = 1e-06

        def _rope_tables(t_len):
            inv_freq = 1.0 / 10000.0 ** (np.arange(0, HD, 2, dtype=np.float32) / HD)
            t = np.arange(t_len, dtype=np.float32)
            freqs = np.outer(t, inv_freq)
            emb = np.concatenate([freqs, freqs], axis=-1)
            return (jnp.asarray(np.cos(emb)), jnp.asarray(np.sin(emb)))

        def _rotate_half(x):
            h = x.shape[-1] // 2
            return jnp.concatenate([-x[..., h:], x[..., :h]], axis=-1)

        def _rmsnorm(v, w):
            return v * jax.lax.rsqrt(jnp.mean(v * v, axis=-1, keepdims=True) + EPS_RMS) * w
        key = jax.random.key(seed)
        ks = jax.random.split(key, 10)
        s = lambda k, shape: jax.random.normal(k, shape, jnp.float32) * 0.02
        return {'x': jax.random.normal(ks[0], (B, T, C), jnp.float32), 'ln1_w': jnp.ones((C,), jnp.float32), 'ln2_w': jnp.ones((C,), jnp.float32), 'wq': s(ks[1], (NH * HD, C)), 'wk': s(ks[2], (NKV * HD, C)), 'wv': s(ks[3], (NKV * HD, C)), 'wo': s(ks[4], (C, C)), 'router_w': s(ks[5], (NE, C)), 'w1': s(ks[6], (NE, HID, C)), 'w2': s(ks[7], (NE, C, HID)), 'w3': s(ks[8], (NE, HID, C))}
    _L0_ffn_all = _L0_ffn_setup()
    _L0_ffn_in = {k: v for k, v in _L0_ffn_all.items() if k in ('ln1_w', 'ln2_w', 'wq', 'wk', 'wv', 'wo', 'router_w', 'w1', 'w2', 'w3')}
    del _L0_ffn_all

    def _L1_attn_setup():
        import jax, jax.numpy as jnp
        import numpy as np
        B_SZ, L, H, P = (16, 1024, 64, 64)
        STEP_SCALE = 1.0
        key = jax.random.key(seed)
        ks = jax.random.split(key, 8)
        x = jax.random.normal(ks[0], (B_SZ, L, H), jnp.float32)
        Lambda_re = jax.random.uniform(ks[1], (P,), jnp.float32, 0.2, 1.0)
        Lambda_im = jax.random.normal(ks[2], (P,), jnp.float32) * np.float32(np.pi)
        B_re = jax.random.normal(ks[3], (P, H), jnp.float32) / np.float32(np.sqrt(H))
        B_im = jax.random.normal(ks[4], (P, H), jnp.float32) / np.float32(np.sqrt(H))
        C_re = jax.random.normal(ks[5], (H, P), jnp.float32) / np.float32(np.sqrt(P))
        C_im = jax.random.normal(ks[6], (H, P), jnp.float32) / np.float32(np.sqrt(P))
        log_step = jax.random.uniform(ks[7], (P,), jnp.float32, np.float32(np.log(0.001)), np.float32(np.log(0.1)))
        return {'x': x, 'Lambda_re': Lambda_re, 'Lambda_im': Lambda_im, 'B_re': B_re, 'B_im': B_im, 'C_re': C_re, 'C_im': C_im, 'log_step': log_step}
    _L1_attn_all = _L1_attn_setup()
    _L1_attn_in = {k: v for k, v in _L1_attn_all.items() if k in ('Lambda_re', 'Lambda_im', 'B_re', 'B_im', 'C_re', 'C_im', 'log_step')}
    del _L1_attn_all

    def _L1_ffn_setup():
        import math
        import jax, jax.numpy as jnp
        import numpy as np
        CAPACITY_FACTOR = 1.25
        key = jax.random.key(seed)
        ks = jax.random.split(key, 5)
        B, L, D, F, E = (8, 2048, 64, 256, 8)
        h = jax.random.normal(ks[0], (B, L, D), dtype=jnp.float32)
        gate_w = jax.random.normal(ks[1], (D, E), dtype=jnp.float32) * 0.02
        gate_b = jnp.zeros((E,), dtype=jnp.float32)
        w1 = jax.random.normal(ks[2], (E, D, F), dtype=jnp.float32) * (1.0 / math.sqrt(D))
        b1 = jnp.zeros((E, F), dtype=jnp.float32)
        w2 = jax.random.normal(ks[3], (E, F, D), dtype=jnp.float32) * (1.0 / math.sqrt(F))
        b2 = jnp.zeros((E, D), dtype=jnp.float32)
        return {'h': h, 'gate_w': gate_w, 'gate_b': gate_b, 'w1': w1, 'b1': b1, 'w2': w2, 'b2': b2}
    _L1_ffn_all = _L1_ffn_setup()
    _L1_ffn_in = {k: v for k, v in _L1_ffn_all.items() if k in ('gate_w', 'gate_b', 'w1', 'b1', 'w2', 'b2')}
    del _L1_ffn_all
    return {'x': x, 'cls_tok': cls_tok, 'L0_tok_conv1_w': _L0_tok_in['conv1_w'], 'L0_tok_conv1_b': _L0_tok_in['conv1_b'], 'L0_tok_bn_gamma': _L0_tok_in['bn_gamma'], 'L0_tok_bn_beta': _L0_tok_in['bn_beta'], 'L0_tok_bn_mean': _L0_tok_in['bn_mean'], 'L0_tok_bn_var': _L0_tok_in['bn_var'], 'L0_tok_conv2_w': _L0_tok_in['conv2_w'], 'L0_tok_conv2_b': _L0_tok_in['conv2_b'], 'L0_attn_Wq': _L0_attn_in['Wq'], 'L0_attn_Wk': _L0_attn_in['Wk'], 'L0_ffn_ln1_w': _L0_ffn_in['ln1_w'], 'L0_ffn_ln2_w': _L0_ffn_in['ln2_w'], 'L0_ffn_wq': _L0_ffn_in['wq'], 'L0_ffn_wk': _L0_ffn_in['wk'], 'L0_ffn_wv': _L0_ffn_in['wv'], 'L0_ffn_wo': _L0_ffn_in['wo'], 'L0_ffn_router_w': _L0_ffn_in['router_w'], 'L0_ffn_w1': _L0_ffn_in['w1'], 'L0_ffn_w2': _L0_ffn_in['w2'], 'L0_ffn_w3': _L0_ffn_in['w3'], 'L1_attn_Lambda_re': _L1_attn_in['Lambda_re'], 'L1_attn_Lambda_im': _L1_attn_in['Lambda_im'], 'L1_attn_B_re': _L1_attn_in['B_re'], 'L1_attn_B_im': _L1_attn_in['B_im'], 'L1_attn_C_re': _L1_attn_in['C_re'], 'L1_attn_C_im': _L1_attn_in['C_im'], 'L1_attn_log_step': _L1_attn_in['log_step'], 'L1_ffn_gate_w': _L1_ffn_in['gate_w'], 'L1_ffn_gate_b': _L1_ffn_in['gate_b'], 'L1_ffn_w1': _L1_ffn_in['w1'], 'L1_ffn_b1': _L1_ffn_in['b1'], 'L1_ffn_w2': _L1_ffn_in['w2'], 'L1_ffn_b2': _L1_ffn_in['b2']}

def reference(x, cls_tok, L0_tok_conv1_w, L0_tok_conv1_b, L0_tok_bn_gamma, L0_tok_bn_beta, L0_tok_bn_mean, L0_tok_bn_var, L0_tok_conv2_w, L0_tok_conv2_b, L0_attn_Wq, L0_attn_Wk, L0_ffn_ln1_w, L0_ffn_ln2_w, L0_ffn_wq, L0_ffn_wk, L0_ffn_wv, L0_ffn_wo, L0_ffn_router_w, L0_ffn_w1, L0_ffn_w2, L0_ffn_w3, L1_attn_Lambda_re, L1_attn_Lambda_im, L1_attn_B_re, L1_attn_B_im, L1_attn_C_re, L1_attn_C_im, L1_attn_log_step, L1_ffn_gate_w, L1_ffn_gate_b, L1_ffn_w1, L1_ffn_b1, L1_ffn_w2, L1_ffn_b2):
    import jax
    import jax.numpy as jnp

    def _L0_tok_ref(x, conv1_w, conv1_b, bn_gamma, bn_beta, bn_mean, bn_var, conv2_w, conv2_b):
        import jax, jax.numpy as jnp
        import numpy as np
        K = 3
        PAD = (K - 1) // 2
        BN_EPS = 1e-05

        def _unfold(x):
            b, c, h, w = x.shape
            xp = jnp.pad(x, ((0, 0), (0, 0), (PAD, PAD), (PAD, PAD)))
            shifts = [xp[:, :, i:i + h, j:j + w] for i in range(K) for j in range(K)]
            return jnp.stack(shifts, axis=2)
        b, c, h, w = x.shape
        y = jnp.einsum('oc,bchw->bohw', conv1_w, x) + conv1_b[None, :, None, None]
        y = (y - bn_mean[None, :, None, None]) * (bn_gamma[None, :, None, None] * jax.lax.rsqrt(bn_var + BN_EPS)[None, :, None, None]) + bn_beta[None, :, None, None]
        y = jax.nn.relu(y)
        wdyn = jnp.einsum('ok,bkhw->bohw', conv2_w, y) + conv2_b[None, :, None, None]
        patches = _unfold(x)
        out = jnp.einsum('bckhw,bkhw->bchw', patches, wdyn)
        return out.reshape(b, h * w, c)

    def _L0_attn_ref(x, Wq, Wk):
        import jax, jax.numpy as jnp
        import numpy as np
        d = x.shape[-1]
        scale = d ** (-0.5)
        q = jnp.einsum('bnd,ed->bne', x, Wq)
        k = jnp.einsum('bnd,ed->bne', x, Wk)
        sim = jnp.einsum('bid,bjd->bij', q, k) * scale
        attn = jax.nn.softmax(sim, axis=-1)
        out = jnp.einsum('bij,bjd->bid', attn, x)
        return out

    def _L0_ffn_ref(x, ln1_w, ln2_w, wq, wk, wv, wo, router_w, w1, w2, w3):
        import jax, jax.numpy as jnp
        import numpy as np
        B, T, C = (64, 96, 64)
        NH, NKV = (4, 2)
        HD = C // NH
        NREP = NH // NKV
        NE, TOPK = (8, 2)
        HID = int(8 / 3 * C)
        EPS_RMS = 1e-06

        def _rope_tables(t_len):
            inv_freq = 1.0 / 10000.0 ** (np.arange(0, HD, 2, dtype=np.float32) / HD)
            t = np.arange(t_len, dtype=np.float32)
            freqs = np.outer(t, inv_freq)
            emb = np.concatenate([freqs, freqs], axis=-1)
            return (jnp.asarray(np.cos(emb)), jnp.asarray(np.sin(emb)))

        def _rotate_half(x):
            h = x.shape[-1] // 2
            return jnp.concatenate([-x[..., h:], x[..., :h]], axis=-1)

        def _rmsnorm(v, w):
            return v * jax.lax.rsqrt(jnp.mean(v * v, axis=-1, keepdims=True) + EPS_RMS) * w
        Bx, Tx, Cx = x.shape
        h = _rmsnorm(x, ln1_w)
        q = (h @ wq.T).reshape(Bx, Tx, NH, HD).transpose(0, 2, 1, 3)
        k = (h @ wk.T).reshape(Bx, Tx, NKV, HD).transpose(0, 2, 1, 3)
        v = (h @ wv.T).reshape(Bx, Tx, NKV, HD).transpose(0, 2, 1, 3)
        cos, sin = _rope_tables(Tx)
        cos, sin = (cos[None, None], sin[None, None])
        q = q * cos + _rotate_half(q) * sin
        k = k * cos + _rotate_half(k) * sin
        k = jnp.repeat(k, NREP, axis=1)
        v = jnp.repeat(v, NREP, axis=1)
        scores = jnp.einsum('bhtd,bhsd->bhts', q, k) / jnp.sqrt(jnp.float32(HD))
        causal = jnp.tril(jnp.ones((Tx, Tx), dtype=bool))
        scores = jnp.where(causal[None, None], scores, jnp.float32(-1e+30))
        att = jax.nn.softmax(scores, axis=-1)
        y = jnp.einsum('bhts,bhsd->bhtd', att, v).transpose(0, 2, 1, 3).reshape(Bx, Tx, Cx)
        x = x + y @ wo.T
        flat = _rmsnorm(x, ln2_w).reshape(-1, Cx)
        probs = jax.nn.softmax(flat @ router_w.T, axis=-1)
        tp, ti = jax.lax.top_k(probs, TOPK)
        tp = tp / (jnp.sum(tp, axis=-1, keepdims=True) + 1e-09)
        weights = jnp.sum(tp[..., None] * jax.nn.one_hot(ti, NE, dtype=flat.dtype), axis=1)
        out = jnp.zeros_like(flat)
        for e in range(NE):
            hh = jax.nn.silu(flat @ w1[e].T) * (flat @ w3[e].T)
            out = out + weights[:, e:e + 1] * (hh @ w2[e].T)
        return x + out.reshape(Bx, Tx, Cx)

    def _L1_attn_ref(x, Lambda_re, Lambda_im, B_re, B_im, C_re, C_im, log_step):
        import jax, jax.numpy as jnp
        import numpy as np
        B_SZ, L, H, P = (16, 1024, 64, 64)
        STEP_SCALE = 1.0
        step = STEP_SCALE * jnp.exp(log_step)
        Lam = -jnp.abs(Lambda_re) + 1j * Lambda_im
        Lam_bar = jnp.exp(Lam * step)
        gamma = (Lam_bar - 1.0) / Lam
        Bc = (B_re + 1j * B_im) * gamma[:, None]
        Bu = jnp.einsum('blh,ph->blp', x, Bc.real) + 1j * jnp.einsum('blh,ph->blp', x, Bc.imag)
        A_el = jnp.broadcast_to(Lam_bar, Bu.shape)

        def binop(a, b):
            Aa, ba = a
            Ab, bb = b
            return (Ab * Aa, Ab * ba + bb)
        _, states = jax.lax.associative_scan(binop, (A_el, Bu), axis=1)
        y = jnp.einsum('blp,hp->blh', states.real, C_re) - jnp.einsum('blp,hp->blh', states.imag, C_im)
        return jax.nn.relu(y) + x

    def _L1_ffn_ref(h, gate_w, gate_b, w1, b1, w2, b2):
        import math
        import jax, jax.numpy as jnp
        import numpy as np
        CAPACITY_FACTOR = 1.25
        B, L, D = h.shape
        E = gate_w.shape[1]
        T = B * L
        C = max(1, math.ceil(CAPACITY_FACTOR * T / E))
        x = h.reshape(T, D)
        logits = x @ gate_w + gate_b
        probs = jax.nn.softmax(logits, axis=-1)
        idx = jnp.argmax(probs, axis=-1)
        prb = jnp.take_along_axis(probs, idx[:, None], axis=1)[:, 0]
        one_hot = jax.nn.one_hot(idx, E, dtype=jnp.float32)
        pos = (jnp.cumsum(one_hot, axis=0) * one_hot).sum(-1).astype(jnp.int32) - 1
        kept = pos < C
        pos_safe = jnp.where(kept, pos, C)
        buf = jnp.zeros((E, C, D), dtype=h.dtype).at[idx, pos_safe].set(x, mode='drop')
        hmid = jax.nn.relu(jnp.einsum('ecd,edf->ecf', buf, w1) + b1[:, None, :])
        ybuf = jnp.einsum('ecf,efd->ecd', hmid, w2) + b2[:, None, :]
        pos_g = jnp.minimum(pos, C - 1)
        y_tok = ybuf[idx, pos_g] * (prb * kept)[:, None]
        y = y_tok.reshape(B, L, D)
        y = jnp.nan_to_num(y, nan=0.0, posinf=10000.0, neginf=-10000.0)
        return y
    h = _L0_tok_ref(x, L0_tok_conv1_w, L0_tok_conv1_b, L0_tok_bn_gamma, L0_tok_bn_beta, L0_tok_bn_mean, L0_tok_bn_var, L0_tok_conv2_w, L0_tok_conv2_b)
    h = jnp.concatenate([jnp.broadcast_to(cls_tok, (h.shape[0], 1, h.shape[2])), h], axis=1)
    h = h + _L0_attn_ref(_layernorm(h, axis=-1), L0_attn_Wq, L0_attn_Wk)
    h = h + _L0_ffn_ref(_layernorm(h, axis=-1), L0_ffn_ln1_w, L0_ffn_ln2_w, L0_ffn_wq, L0_ffn_wk, L0_ffn_wv, L0_ffn_wo, L0_ffn_router_w, L0_ffn_w1, L0_ffn_w2, L0_ffn_w3)
    h = h + _L1_attn_ref(_layernorm(h, axis=-1), L1_attn_Lambda_re, L1_attn_Lambda_im, L1_attn_B_re, L1_attn_B_im, L1_attn_C_re, L1_attn_C_im, L1_attn_log_step)
    h = h + _L1_ffn_ref(_layernorm(h, axis=-1), L1_ffn_gate_w, L1_ffn_gate_b, L1_ffn_w1, L1_ffn_b1, L1_ffn_w2, L1_ffn_b2)
    return h

_drawn_inputs = setup_inputs


def setup_inputs(seed=0):
    import zlib

    import numpy as np

    out = dict(_drawn_inputs(seed))
    spreads = {'L0_tok_conv1_b': (0.0, 0.1),
     'L0_tok_bn_gamma': (1.0, 0.2),
     'L0_tok_bn_beta': (0.0, 0.1),
     'L0_tok_bn_mean': (0.0, 0.1),
     'L0_tok_bn_var': (1.0, 0.2),
     'L0_tok_conv2_b': (0.0, 0.1),
     'L0_ffn_ln1_w': (1.0, 0.6),
     'L0_ffn_ln2_w': (1.0, 0.6),
     'L1_ffn_gate_b': (0.0, 0.402),
     'L1_ffn_b1': (0.0, 2.0),
     'L1_ffn_b2': (0.0, 2.0)}
    factors = {'cls_tok': 7.409,
     'L0_ffn_wq': 8.0,
     'L0_ffn_wk': 8.0,
     'L0_ffn_wv': 8.0,
     'L0_ffn_wo': 8.0,
     'L0_ffn_router_w': 8.0,
     'L0_ffn_w1': 8.0,
     'L0_ffn_w2': 8.0,
     'L0_ffn_w3': 8.0,
     'L1_attn_Lambda_re': 200.0,
     'L1_ffn_w1': 2.699,
     'L1_attn_Lambda_im': 52.24,
     'L1_attn_B_re': 51.92,
     'L1_attn_B_im': 54.2,
     'L1_attn_C_re': 43.216,
     'L1_attn_C_im': 52.376,
     'L1_attn_log_step': 53.08}
    for name, (base, spread) in spreads.items():
        noise = np.random.default_rng([zlib.crc32(name.encode()), seed]).standard_normal(out[name].shape)
        drawn = base * np.exp(spread * noise) if base else spread * noise
        out[name] = jnp.asarray(drawn.astype(out[name].dtype))
    for name, factor in factors.items():
        out[name] = (out[name] * factor).astype(out[name].dtype)
    return out
```

```python
from contextlib import ExitStack

import numpy as np

import concourse.bass as bass
from concourse import mybir

F32 = mybir.dt.float32
BF16 = mybir.dt.bfloat16
ALU = mybir.AluOpType
ACT = mybir.ActivationFunctionType
AX = mybir.AxisListType

P = 128
B = 2
D = 64
IMG = 64
TAPS = 9
CR = 16
N = IMG * IMG + 1
TPG = 3
GW = TPG * P
NG = -(-N // GW)
NT = NG * TPG
NP = NT * P
GT = B * NG
TT = B * NT
TOK = B * NP
EPS = 1e-5
BIG = -1e30
F1 = 256


class Stage:
    pass


def tower(nc, I, out):
    ctx = ExitStack()
    with ctx:
        def sb(name, shape, dt=F32):
            return ctx.enter_context(nc.sbuf_tensor(name, shape, dt))

        def sem(name):
            return ctx.enter_context(nc.semaphore(name))

        scratch = nc.dram_tensor("tokens_scratch", (B, IMG * IMG, D), F32, kind="Internal").ap()

        PS = ctx.enter_context(nc.psum_tensor("PS", [P, 8, 512], F32))

        def bank16(k):
            return PS[:, k, :].bitcast(BF16)

        H = sb("H", [P, TT, D])
        XN = sb("XN", [P, TT, D])
        stat = sb("stat", [P, 4, TT])
        A0 = sb("A0", [P, TT * 256], BF16)
        A1 = sb("A1", [P, 2 * TOK], BF16)
        A2 = sb("A2", [P, 2 * TOK], BF16)
        A3 = sb("A3", [P, TT * 65])
        A4 = sb("A4", [P, TT * D])
        ident = sb("ident", [P, P])
        ident16 = sb("ident16", [P, P], BF16)
        valid = sb("valid", [P, TT])
        epsc = sb("epsc", [P, 2])

        xstr = A0[:, :].rearrange("p (t n) -> p t n", n=256)
        W = A1[:, :].rearrange("p (w n) -> p w n", w=2)

        A5 = sb("A5", [P, 4 * NP], BF16)

        def places(arena, start):
            at = [start]

            def place(shape, dt=F32):
                n = int(np.prod(shape[1:])) * (2 if dt is F32 else 1)
                at[0] += at[0] % 2
                v = arena[0:shape[0], at[0]:at[0] + n]
                at[0] += n
                assert at[0] <= arena.shape[1], (at[0], arena.shape)
                v = v.bitcast(F32) if dt is F32 else v
                names = "abcd"[:len(shape) - 1]
                if len(shape) > 2:
                    v = v.rearrange("p (%s) -> p %s" % (" ".join(names), " ".join(names)), **dict(zip(names[1:], shape[2:])))
                return v
            return place

        early = places(A5, 0)
        n_ln = [0]
        n_pool = [0]
        p_ch = sem("pool_chain")

        c_in = sem("constants_loaded")
        c_id = sem("ident16_ready")

        block = ctx.enter_context(nc.Block())

        x_pad = A1[:, 0:2 * 66 * 66].bitcast(F32).rearrange("p (h w) -> p h w", w=66)
        conv = A2[:, 0:2 * IMG * IMG].bitcast(F32)
        c1w = early([P, B * CR])
        bnp = early([B * CR, 5])
        bns = early([B * CR, 4])
        c2w = A3[0:B * CR, 0:TAPS * P].rearrange("p (k n) -> p k n", k=TAPS)
        b2 = early([P, TAPS])
        yv = early([B * CR, 2, 512])
        tapp = early([P, 3, 512])
        t_in = sem("conv_inputs_loaded")
        t_std = sem("bn_std")
        t_bn = sem("bn_folded")
        t_ch = sem("bn_chain")
        t_y = sem("conv1_product")
        t_ys = sem("conv1_relu")
        t_w = sem("dynamic_weights")
        t_p = sem("tap_product")
        t_a = sem("tap_added")
        t_out = sem("conv_stored")
        h_in = sem("tokens_loaded")

        RG = 8
        SLOT = 3

        ln_ch = sem("vector_chain")
        ln_var = sem("ln_variance")
        ln_std = sem("ln_std")
        x_str = sem("x_strings")
        x_t = sem("x_transposed")
        x_w = sem("x_stacks")

        qk2 = early([D, 2, D])
        qkc = early([D, 2, P])
        qks = early([D, 2])
        MS = early([P, 3, D], BF16)
        mres = early([P, D])
        VA = A3[:, 0:TT * D].rearrange("p (t n) -> p t n", n=D)
        Q2 = A4[:, :].rearrange("p (t n) -> p t n", n=D)
        QP = A2[:, :].rearrange("p (w n) -> p w n", w=2)
        QT = A0[:, 0:3 * NP].rearrange("p (w n) -> p w n", w=3)
        MX = early([P, TPG, NG])
        mm = early([P, 2, TPG])
        qtm = early([P, TPG, D])
        QTS = early([P, TPG, 5, D], BF16)
        PT = early([P, 6, GW])
        VS = early([P, 6, D])
        OT = sb("OT", [P, GW])
        NPAIR = (NT + 1) // 2
        orec = early([P, TPG])
        ot = early([P, TPG, P])
        a_m = sem("a_projection_matrix")
        a_ms = sem("a_projection_stacks")
        a_ch = sem("a_chain")
        a_q = sem("a_queries_product")
        a_qe = sem("a_queries_kept")
        a_qstr = sem("a_query_strings")
        a_qpt = sem("a_query_transposed")
        a_qp = sem("a_query_stacks")
        a_s1 = sem("a_max_scores")
        a_s1f = sem("a_max_scores_read")
        a_str = sem("a_shifted_strings")
        a_tq = sem("a_shifted_transposed")
        a_qt = sem("a_shifted_stacks")
        a_s2 = sem("a_scores")
        a_ex = sem("a_exponentials")
        a_pv = sem("a_value_products")
        a_vs = sem("a_values_staged")
        a_ot = sem("a_output_kept")
        a_ft = sem("a_output_transposed")
        a_o = sem("a_output_added")
        a_pc = sem("a_prep_chain")
        o_out = sem("output_stored")
        o_ch = sem("a_output_chain")

        QR = TT // 3

        def b3(ap, n):
            return ap.unsqueeze(2).to_broadcast([P, ap.shape[1], n])

        def transposes(pe, ready, done, freed, strings=None):
            pe.wait_ge(ready, 1)
            pe.wait_ge(c_id, 1)
            with pe.Fori(0, GT // 2) as i:
                for h in range(2):
                    pe.wait_ge(freed, i * 2 + h + 1)
                    for w in range(2):
                        for u in range(TPG):
                            ins = nc.tensor.transpose(bank16(6 + h)[:, (w * TPG + u) * P:(w * TPG + u + 1) * P],
                                                      (xstr if strings is None else strings)[:, bass.ds((i * 2 + h) * TPG + u, 1), w * P:(w + 1) * P], ident16[:, :])
                    ins.then_inc(done, 1)

        def stack_copies(act, done, freed, dst):
            act.sem_inc(freed, 2)
            with act.Fori(0, GT // 2) as i:
                for h in range(2):
                    act.wait_ge(done, i * 2 + h + 1)
                    nc.scalar.copy(dst[:, :, bass.ds((i * 2 + h) * GW, GW)],
                                   bank16(6 + h)[:, 0:2 * GW].rearrange("p (w n) -> p w n", w=2)).then_inc(freed, 1)

        def link(e, s, count, ins):
            count[0] += 1
            ins.then_inc(s, 1)
            e.wait_ge(s, count[0])

        def layer_norm(dve, count, ready):
            ch = lambda ins: link(dve, ln_ch, count, ins)
            ch(nc.vector.tensor_reduce(stat[:, 0, :], H[:, :, :], AX.X, ALU.add))
            ch(nc.vector.tensor_scalar(stat[:, 0, :], stat[:, 0, :], -1.0 / D, None, ALU.mult))
            ch(nc.vector.tensor_tensor(XN[:, :, :], H[:, :, :], b3(stat[:, 0, :], D), ALU.add))
            ch(nc.vector.tensor_tensor(Q2, XN[:, :, :], XN[:, :, :], ALU.mult))
            nc.vector.tensor_reduce(stat[:, 1, :], Q2, AX.X, ALU.add).then_inc(ready, 1)

        def finish_norm(dve, count):
            ch = lambda ins: link(dve, ln_ch, count, ins)
            ch(nc.vector.reciprocal(stat[:, 3, :], stat[:, 2, :]))
            ch(nc.vector.tensor_tensor(XN[:, :, :], XN[:, :, :], b3(stat[:, 3, :], D), ALU.mult))

        def split_x(dve, count, src, res, ready, value, strings=None):
            ch = lambda ins: link(dve, ln_ch, count, ins)
            s = (xstr if strings is None else strings).rearrange("p t (a n) -> p t a n", n=D)
            ch(nc.vector.tensor_copy(s[:, :, 0, :], src))
            ch(nc.vector.tensor_copy(s[:, :, 3, :], s[:, :, 0, :]))
            ch(nc.vector.tensor_tensor(res, src, s[:, :, 0, :], ALU.subtract))
            ch(nc.vector.tensor_copy(s[:, :, 1, :], res))
            ch(nc.vector.tensor_tensor(res, res, s[:, :, 1, :], ALU.subtract))
            nc.vector.tensor_copy(s[:, :, 2, :], res).then_inc(ready, 1)
            dve.wait_ge(ready, value)

        def split_w(dve, s, count, w, st, ready, value):
            ch = lambda ins: link(dve, s, count, ins)
            ch(nc.vector.tensor_copy(st[:, 0, :], w))
            ch(nc.vector.tensor_copy(st[0:D, 1, :], st[0:D, 0, :]))
            ch(nc.vector.tensor_tensor(w, w, st[:, 0, :], ALU.subtract))
            ch(nc.vector.tensor_copy(st[:, 2, :], w))
            ch(nc.vector.tensor_tensor(w, w, st[:, 2, :], ALU.subtract))
            nc.vector.tensor_copy(st[D:P, 1, :], w[D:P, :]).then_inc(ready, 1)
            dve.wait_ge(ready, value)

        def project(pe, stacks, n, done, freed):
            with pe.Fori(0, GT // 2) as i:
                for h in range(2):
                    pe.wait_ge(freed, i * 2 + h + 1)
                    for u in range(TPG):
                        tile = bass.ds((i * 2 + h) * GW + u * P, P)
                        for k, w in enumerate((0, 1, 0)):
                            ins = nc.tensor.matmul(PS[:, 6 + h, u * n:(u + 1) * n], W[:, w, tile], stacks[:, k, :],
                                                   start=(k == 0), stop=(k == 2))
                    ins.then_inc(done, 1)

        def project_copies(act, n, done, freed, dst):
            act.sem_inc(freed, 2)
            with act.Fori(0, GT // 2) as i:
                for h in range(2):
                    act.wait_ge(done, i * 2 + h + 1)
                    nc.scalar.copy(dst[:, bass.ds((i * 2 + h) * TPG, TPG), :],
                                   PS[:, 6 + h, 0:TPG * n].rearrange("p (t n) -> p t n", n=n)).then_inc(freed, 1)


        NH, NKV, HD = 4, 2, 16
        PARTS = 6
        KR = PARTS * HD
        HH = HD // 2
        UN = TPG * NH
        QKV = A2[:, :].bitcast(F32).rearrange("p (t n) -> p t n", n=P)
        late = places(A3[:, :].bitcast(BF16), 2 * TT * NKV * (HD + 1))
        QB = [A5[:, :].rearrange("p (h n) -> p h n", h=NH), A2[:, :].rearrange("p (h n) -> p h n", h=NH)]
        KB = A1[:, :].rearrange("p (h n) -> p h n", h=NKV)
        qs_ = A0[:, 0:NT * NH * KR].rearrange("p (x a n) -> p x a n", a=PARTS, n=HD)
        ks_ = A4[:, :].bitcast(BF16)[:, 0:NT * NKV * KR].rearrange("p (x a n) -> p x a n", a=PARTS, n=HD)
        rt = A0[:, 0:8 * NT * 48].bitcast(F32).rearrange("p (k t h n) -> p k t h n", k=4, t=NT, n=HH)
        VB = A3[:, 0:TT * NKV * (HD + 1)].rearrange("p (t h n) -> p t h n", h=NKV, n=HD + 1)
        YB = A4[:, :].rearrange("p (t n) -> p t n", n=D)
        wf = late([P, P])
        lnw = late([P, 2])
        wqkv = late([P, 3, P], BF16)
        wof = late([P, D])
        wos = late([P, 3, D], BF16)
        cs = late([P, 2, NT, HH])
        neg = late([P, GW])
        MXB = late([P, UN, NG])
        mB = late([P, UN])
        mstr = late([P, UN, 3], BF16)
        MT = late([UN, GW], BF16)
        PB = A0[:, 0:2 * UN * GW].bitcast(F32).rearrange("p (k n) -> p k n", k=UN)
        VSB = sb("VSB", [P, TPG, NKV, HD + 1])
        tmask = sb("tmask", [P, GW])
        obr = sb("obr", [P, TPG, NH])
        b_ystr = sem("b_output_strings")
        b_in = sem("b_weights_loaded")
        b_var = sem("b_square_sums")
        b_std = sem("b_rms")
        b_w = sem("b_weight_stacks")
        b_str = sem("b_strings")
        b_t = sem("b_transposed")
        b_st = sem("b_stacks")
        b_q = sem("b_qkv_product")
        b_qe = sem("b_qkv_kept")
        b_hs = sem("b_head_strings")
        b_ht = sem("b_heads_transposed")
        b_hk = sem("b_head_stacks")
        b_one = sem("b_ones_rows")
        b_s1 = sem("b_max_scores")
        b_s1f = sem("b_max_scores_read")
        b_s2 = sem("b_scores")
        b_ex = sem("b_exponentials")
        b_sel = sem("b_causal_selected")
        b_pv = sem("b_value_products")
        b_vs = sem("b_values_staged")
        b_ot = sem("b_output_kept")
        b_ft = sem("b_output_transposed_back")
        b_o = sem("b_output_scaled")
        b_oc = sem("b_output_chain")
        b_ms = sem("b_maximum_strings")
        b_mt = sem("b_maxima_transposed")
        b_mc = sem("b_maxima_copied")
        b_mr = sem("b_maximum_rows")
        b_dc = sem("b_diagonal_chain")

        def u1(b, g):
            return UN * (b * NG * (NG + 1) // 2 + g * (g + 1) // 2)

        def b_sp(sp):
            sp.wait_ge(a_o, GT + 1)
            sp.dma_start(wf[:, :], I["wqkv"]).then_inc(b_in, 16)
            sp.dma_start(wof[:, :], I["wo"]).then_inc(b_in, 16)
            sp.dma_start(lnw[:, :], I["lnw"]).then_inc(b_in, 16)
            sp.dma_start(cs[:, :, :, :], I["rope"]).then_inc(b_in, 16)
            sp.dma_start(neg[:, :], I["neg"]).then_inc(b_in, 16)

        def b_sp_rows(sp):
            for b in range(B):
                for g in range(NG):
                    sp.wait_ge(b_mc, b * NG + g + 1)
                    for h in range(NH):
                        sp.dma_start(QB[b][KR:KR + 3, h, g * GW:(g + 1) * GW], MT[3 * h:3 * h + 3, :]).then_inc(b_mr, 16)

        def b_pe(pe):
            pe.wait_ge(a_o, GT + 1)
            transposes(pe, b_str, b_t, b_st)
            pe.wait_ge(b_st, GT + 2)
            pe.wait_ge(b_w, 1)
            project(pe, wqkv, P, b_q, b_qe)
            n = 0
            for b in range(B):
                pe.wait_ge(b_hs, b + 1)
                if b == 0:
                    pe.wait_ge(b_qe, GT + 2)
                with pe.Fori(0, NG) as g:
                    for c in range(3):
                        pe.wait_ge(b_hk, b * NG * 3 + g * 3 + c + 1)
                        for y in range(2):
                            for u in range(TPG):
                                if c < 2:
                                    src = qs_[:, bass.ds(g * UN + u * NH + 2 * c + y, 1), :, :]
                                else:
                                    src = ks_[:, bass.ds(g * TPG * NKV + u * NKV + y, 1), :, :]
                                ins = nc.tensor.transpose(bank16(c)[0:KR, (y * TPG + u) * P:(y * TPG + u + 1) * P],
                                                          src.rearrange("p x a n -> p (x a n)"), ident16[:, :])
                        ins.then_inc(b_ht, 1)
            pe.wait_ge(b_hk, B * NG * 3 + 3)
            pe.wait_ge(b_one, 2)
            pe.sem_inc(b_pv, 3)

            def qk(b, g, j, h, lo, k, n2):
                pe.wait_ge(b_ex, n2 + 1)
                nc.tensor.matmul(PS[:, k % 3, lo:GW], KB[0:KR + 3, h // 2, bass.ds(b * NP + j * P, P)],
                                 QB[b][0:KR + 3, h, g * GW + lo:(g + 1) * GW], start=True, stop=True).then_inc(b_s2, 1)

            def mx(b, g, a, h, key, width, k, n1):
                pe.wait_ge(b_s1f, n1 + 1)
                nc.tensor.matmul(PS[:, 3 + k % 3, 0:width], QB[b][0:KR, h, (g * TPG + a) * P:(g * TPG + a + 1) * P],
                                 KB[0:KR, h // 2, bass.ds(b * NP + key, width)], start=True, stop=True).then_inc(b_s1, 1)

            def triple(b, g, p1, jj, first, q0):
                n2 = u1(b, g) + jj * UN
                n1 = u1(b, g + p1) + jj * UN if p1 else 0
                for k in range(UN):
                    qk(b, g, jj * TPG + k // NH, k % NH, 0, k, n2 + k)
                    if p1:
                        mx(b, g + p1, k // NH, k % NH, jj * GW, GW, k, n1 + k)
                    if k == 1 and not first:
                        pvq(n2 - UN, q0 - TPG, 2, 0, False)
                    if k == 5 and first:
                        pe.wait_ge(b_ot, b * NG + g + 1)
                    if k in (5, 9):
                        pvq(n2, q0, k // NH - 1, 0, first and k == 5)

            def pvq(n2, q0, u, lo, first, sel=0):
                pe.wait_ge(b_ex, n2 + 4 * u + 4 + 3)
                pe.wait_ge(b_vs, q0 + u + 1)
                if sel:
                    pe.wait_ge(b_sel, sel)
                for h in range(NH):
                    ins = nc.tensor.matmul(PS[32 * h:32 * h + HD + 1, 6, lo:GW], VSB[:, u, h // 2, :], PB[:, NH * u + h, lo:GW],
                                           start=first, stop=True, skip_group_check=True)
                ins.then_inc(b_pv, 1)

            def maxima(b, g, lo, hi):
                if hi > lo:
                    with pe.Fori(lo, hi) as jj:
                        for k in range(UN):
                            mx(b, g, k // NH, k % NH, jj * GW, GW, k, u1(b, g) + jj * UN + k)

            def diagonal(b, g, p1):
                n2 = u1(b, g) + g * UN
                q0 = n2 // NH
                for k in range(UN + 4):
                    if k < UN and p1 != "only":
                        qk(b, g, g * TPG + k // NH, k % NH, k // NH * P, k, n2 + k)
                    if k < UN and p1:
                        q = g if p1 == "only" else g + p1
                        mx(b, q, k // NH, k % NH, q * GW, (k // NH + 1) * P, k, u1(b, q) + q * UN + k)
                    if k in (5, 9, 13) and p1 != "only":
                        u = k // NH - 1
                        if g == 0 and u == 0:
                            pe.wait_ge(b_ot, b * NG + g + 1)
                        pvq(n2, q0, u, u * P, g == 0 and u == 0, (b * NG + g) * UN + 4 * u + 4)

            def fin(gi):
                pe.wait_ge(b_ot, gi + 2)
                for a in range(TPG):
                    ins = nc.tensor.transpose(PS[:, 7, a * P:(a + 1) * P], OT[:, a * P:(a + 1) * P], ident[:, :])
                ins.then_inc(b_ft, 1)

            def prep(b, g):
                gi = b * NG + g
                pe.wait_ge(b_ms, gi + 1)
                if gi:
                    pe.wait_ge(b_mc, gi)
                if gi > 1:
                    pe.wait_ge(b_o, gi - 1)
                for a in range(TPG):
                    ins = nc.tensor.transpose(bank16(7)[0:UN, a * P:(a + 1) * P],
                                              mstr[:, a * NH:(a + 1) * NH, :].rearrange("p h n -> p (h n)"), ident16[:, :])
                ins.then_inc(b_mt, 1)

            for b in range(B):
                diagonal(b, 0, "only")
                prep(b, 0)
                maxima(b, 1, 0, 1)
                diagonal(b, 1, "only")
                for g in range(NG):
                    p1 = 2 if g + 2 < NG else 0
                    gi = b * NG + g
                    q0 = u1(b, g) // NH
                    pe.wait_ge(b_mr, 64 * (gi + 1))
                    if g:
                        triple(b, g, p1, 0, True, q0)
                    if gi:
                        fin(gi - 1)
                    if g > 1:
                        with pe.Fori(1, g) as jj:
                            triple(b, g, p1, jj, False, q0 + jj * TPG)
                    if g:
                        pvq(u1(b, g) + (g - 1) * UN, q0 + (g - 1) * TPG, 2, 0, False)
                    if g + 1 < NG:
                        prep(b, g + 1)
                    if p1:
                        maxima(b, g + 2, g, g + 2)
                    diagonal(b, g, p1)
            fin(GT - 1)

        def b_act(act):
            act.wait_ge(b_var, 1)
            nc.scalar.activation(stat[:, 2, :], stat[:, 1, :], ACT.Sqrt, bias=epsc[:, 1:2], scale=1.0 / D).then_inc(b_std, 1)
            stack_copies(act, b_t, b_st, W)
            project_copies(act, P, b_q, b_qe, QKV)
            act.sem_inc(b_hk, 3)
            for b in range(B):
                with act.Fori(0, NG) as g:
                    for c in range(3):
                        act.wait_ge(b_ht, b * NG * 3 + g * 3 + c + 1)
                        if c < 2:
                            dst = QB[b][0:KR, 2 * c:2 * c + 2, bass.ds(g * GW, GW)]
                        else:
                            dst = KB[0:KR, :, bass.ds(b * NP + g * GW, GW)]
                        nc.scalar.copy(dst, bank16(c)[0:KR, 0:2 * GW].rearrange("p (h n) -> p h n", h=2)).then_inc(b_hk, 1)
            act.sem_inc(b_ex, 3)

            def exps(n2, q0, lo=0):
                for k in range(UN):
                    act.wait_ge(b_s2, n2 + k + 1)
                    if k % NH == 0:
                        act.wait_ge(b_pv, q0 + k // NH + 1)
                    c = k // NH * P if lo else 0
                    nc.scalar.activation(PB[:, k, c:GW], PS[:, k % 3, c:GW], ACT.Exp).then_inc(b_ex, 1)

            def prep(b, g):
                gi = b * NG + g
                act.wait_ge(b_mt, gi + 1)
                if gi:
                    act.wait_ge(b_mr, 64 * gi)
                nc.scalar.copy(MT[:, :], bank16(7)[0:UN, 0:GW]).then_inc(b_mc, 1)

            for b in range(B):
                prep(b, 0)
                for g in range(NG):
                    if g:
                        with act.Fori(0, g) as jj:
                            exps(u1(b, g) + jj * UN, u1(b, g) // NH + jj * TPG)
                    if g + 1 < NG:
                        prep(b, g + 1)
                    exps(u1(b, g) + g * UN, u1(b, g) // NH + g * TPG, 1)

        def b_pool(pool):
            def stage(b, j, u, q):
                pool.wait_ge(b_one, 2)
                pool.wait_ge(b_pv, q + u + 1)
                nc.gpsimd.tensor_copy(VSB[:, u:u + 1, :, :], VB[:, bass.ds(b * NT + j + u, 1), :, :]).then_inc(b_vs, 1)

            for b in range(B):
                for g in range(NG):
                    q0 = u1(b, g) // NH
                    if g:
                        with pool.Fori(0, g) as jj:
                            for u in range(TPG):
                                stage(b, jj * TPG, u, q0 + jj * TPG)
                    for k in range(UN):
                        if k % NH == 0:
                            stage(b, g * TPG, k // NH, q0 + g * TPG)
                        pool.wait_ge(b_ex, u1(b, g) + g * UN + k + 4)
                        c = k // NH * P
                        v = PB[:, k, c:c + P]
                        nc.gpsimd.affine_select(out=v, in_=v, compare_op=ALU.is_ge, fill=0.0, base=0,
                                                pattern=[[1, P]], channel_multiplier=-1).then_inc(b_sel, 1)

        def b_dve(dve):
            dve.wait_ge(a_o, GT + 1)
            dve.wait_ge(b_in, 5 * 16)
            n_w = [0]
            ch = lambda ins: link(dve, ln_ch, n_ln, ins)
            ch(nc.vector.tensor_scalar(wf[:, :], wf[:, :], lnw[:, 0:1], None, ALU.mult))
            ch(nc.vector.tensor_scalar(wf[:, 0:D], wf[:, 0:D], float(HD) ** -0.5, None, ALU.mult))
            split_w(dve, ln_ch, n_ln, wf[:, :], wqkv, b_w, 1)
            split_w(dve, ln_ch, n_ln, wof[:, :], wos, b_w, 2)
            layer_norm(dve, n_ln, ln_var)
            dve.wait_ge(ln_std, 2)
            finish_norm(dve, n_ln)
            link(dve, ln_ch, n_ln, nc.vector.tensor_tensor(Q2, XN[:, :, :], XN[:, :, :], ALU.mult))
            nc.vector.tensor_reduce(stat[:, 1, :], Q2, AX.X, ALU.add).then_inc(b_var, 1)
            dve.wait_ge(b_std, 1)
            link(dve, ln_ch, n_ln, nc.vector.reciprocal(stat[:, 3, :], stat[:, 2, :]))
            link(dve, ln_ch, n_ln, nc.vector.tensor_tensor(Q2, XN[:, :, :], b3(stat[:, 3, :], D), ALU.mult))
            split_x(dve, n_ln, Q2, Q2, b_str, 1)
            n_h = [0]
            ch = lambda ins: link(dve, ln_ch, n_ln, ins)
            dve.wait_ge(b_qe, GT + 2)
            ch(nc.vector.memset(VB[:, :, :, :], 1.0))
            ch(nc.vector.tensor_copy(VB[:, :, :, 0:HD], QKV[:, :, 96:128].rearrange("p t (h n) -> p t h n", h=NKV)))
            for b in range(B):
                if b:
                    dve.wait_ge(b_hk, b * NG * 3 + 3)
                v = QKV[:, b * NT:(b + 1) * NT, 0:96].rearrange("p t (h c n) -> p t h c n", c=2, n=HH)
                lo, hi = v[:, :, :, 0, :], v[:, :, :, 1, :]
                co = cs[:, 0, :, :].unsqueeze(2).to_broadcast([P, NT, NH + NKV, HH])
                si = cs[:, 1, :, :].unsqueeze(2).to_broadcast([P, NT, NH + NKV, HH])
                ch(nc.vector.tensor_tensor(rt[:, 0, :, :, :], lo, co, ALU.mult))
                ch(nc.vector.tensor_tensor(rt[:, 1, :, :, :], hi, si, ALU.mult))
                ch(nc.vector.tensor_tensor(rt[:, 2, :, :, :], hi, co, ALU.mult))
                ch(nc.vector.tensor_tensor(rt[:, 3, :, :, :], lo, si, ALU.mult))
                ch(nc.vector.tensor_tensor(lo, rt[:, 0, :, :, :], rt[:, 1, :, :, :], ALU.subtract))
                ch(nc.vector.tensor_tensor(hi, rt[:, 2, :, :, :], rt[:, 3, :, :, :], ALU.add))
                for z, (st, c0, nh, where) in enumerate(((qs_, 0, NH, ((0, 1, 2), (3, 4), (5,))), (ks_, D, NKV, ((0, 3, 5), (1, 4), (2,))))):
                    x = QKV[:, b * NT:(b + 1) * NT, c0:c0 + nh * HD].rearrange("p t (h n) -> p t h n", n=HD)
                    for part, at in enumerate(where):
                        first = st[:, :, at[0], :].rearrange("p (t h) n -> p t h n", h=nh)
                        last = z == 1 and part == 2
                        ins = nc.vector.tensor_copy(first, x)
                        if last:
                            ins.then_inc(b_hs, 1)
                            dve.wait_ge(b_hs, b + 1)
                        else:
                            ch(ins)
                        for c in at[1:]:
                            ch(nc.vector.tensor_copy(st[:, :, c, :], st[:, :, at[0], :]))
                        if part < 2:
                            ch(nc.vector.tensor_tensor(x, x, first, ALU.subtract))
            dve.wait_ge(b_hk, B * NG * 3 + 3)
            nc.vector.memset(KB[96:99, 0, :], 1.0).then_inc(b_one, 1)
            nc.vector.memset(KB[96:99, 1, :], 1.0).then_inc(b_one, 1)
            dve.sem_inc(b_s1f, 3)
            dve.sem_inc(b_ot, 1)

            def maxima(b, g, lo, hi):
                if hi > lo:
                    with dve.Fori(lo, hi) as jj:
                        for k in range(UN):
                            dve.wait_ge(b_s1, u1(b, g) + jj * UN + k + 1)
                            nc.vector.tensor_reduce(MXB[:, k, bass.ds(jj, 1)], PS[:, 3 + k % 3, 0:GW], AX.X, ALU.max).then_inc(b_s1f, 1)

            def diagonal(b, g):
                for k in range(UN):
                    w = (k // NH + 1) * P
                    n = (b * NG + g) * UN + k
                    dve.wait_ge(b_s1, u1(b, g) + g * UN + k + 1)
                    if n:
                        dve.wait_ge(b_dc, n)
                    nc.vector.tensor_tensor(tmask[:, 0:w], PS[:, 3 + k % 3, 0:w], neg[:, GW - w:GW], ALU.add).then_inc(b_s1f, 1)
                    dve.wait_ge(b_s1f, u1(b, g) + g * UN + k + 1 + 3)
                    nc.vector.tensor_reduce(MXB[:, k, g:g + 1], tmask[:, 0:w], AX.X, ALU.max).then_inc(b_dc, 1)

            n_p = [0]

            def prep(b, g):
                gi = b * NG + g
                chp = lambda ins: link(dve, ln_ch, n_ln, ins)
                dve.wait_ge(b_dc, (gi + 1) * UN)
                dve.wait_ge(b_s1f, u1(b, g) + (g + 1) * UN + 3)
                chp(nc.vector.tensor_reduce(mB[:, :], MXB[:, :, 0:g + 1], AX.X, ALU.max, negate=True))
                if gi:
                    dve.wait_ge(b_mt, gi)
                chp(nc.vector.tensor_copy(mstr[:, :, 0], mB[:, :]))
                chp(nc.vector.tensor_tensor(mB[:, :], mB[:, :], mstr[:, :, 0], ALU.subtract))
                chp(nc.vector.tensor_copy(mstr[:, :, 1], mB[:, :]))
                chp(nc.vector.tensor_tensor(mB[:, :], mB[:, :], mstr[:, :, 1], ALU.subtract))
                nc.vector.tensor_copy(mstr[:, :, 2], mB[:, :]).then_inc(b_ms, 1)
                dve.wait_ge(b_ms, gi + 1)

            def keep(b, g):
                gi = b * NG + g
                dve.wait_ge(b_pv, (u1(b, g) + (g + 1) * UN) // NH + 3)
                for h in range(NH):
                    ins = nc.vector.tensor_copy(OT[32 * h:32 * h + HD + 1, :], PS[32 * h:32 * h + HD + 1, 6, 0:GW])
                ins.then_inc(b_ot, 1)

            def fin(gi):
                O = PS[:, 7, 0:GW].rearrange("p (t h n) -> p t h n", h=NH, n=32)
                dve.wait_ge(b_ft, gi + 1)
                nc.vector.reciprocal(obr[:, :, :], O[:, :, :, HD]).then_inc(b_oc, 1)
                dve.wait_ge(b_oc, gi + 1)
                nc.vector.tensor_tensor(YB[:, gi * TPG:(gi + 1) * TPG, :].rearrange("p t (h n) -> p t h n", h=NH), O[:, :, :, 0:HD],
                                        obr[:, :, :].unsqueeze(3).to_broadcast([P, TPG, NH, HD]), ALU.mult).then_inc(b_o, 1)
                dve.wait_ge(b_o, gi + 1)

            for b in range(B):
                diagonal(b, 0)
                prep(b, 0)
                maxima(b, 1, 0, 1)
                diagonal(b, 1)
                for g in range(NG):
                    gi = b * NG + g
                    more = g + 2 < NG
                    if g + 1 < NG:
                        prep(b, g + 1)
                    if more and g:
                        maxima(b, g + 2, 0, 1)
                    if gi:
                        fin(gi - 1)
                    if more:
                        maxima(b, g + 2, 1 if g else 0, g + 2)
                        diagonal(b, g + 2)
                    keep(b, g)
            fin(GT - 1)
            split_x(dve, n_ln, YB, YB, b_ystr, 1)


        b_yt = sem("b_output_transposed")
        b_yst = sem("b_output_stacks")
        b_yp = sem("b_output_product")
        b_yk = sem("b_output_added")

        def bo_pe(pe):
            transposes(pe, b_ystr, b_yt, b_yst)
            pe.wait_ge(b_yst, GT + 2)
            pe.wait_ge(b_w, 2)
            project(pe, wos, D, b_yp, b_yk)

        def bo_act(act):
            stack_copies(act, b_yt, b_yst, W)

        def bo_dve(dve):
            dve.sem_inc(b_yk, 2)
            with dve.Fori(0, GT // 2) as i:
                for h in range(2):
                    dve.wait_ge(b_yp, i * 2 + h + 1)
                    x = XN[:, bass.ds((i * 2 + h) * TPG, TPG), :]
                    nc.vector.tensor_tensor(x, PS[:, 6 + h, 0:TPG * D].rearrange("p (t n) -> p t n", n=D), x,
                                            ALU.add).then_inc(b_yk, 1)
            dve.wait_ge(b_yk, GT + 2)

        NE = 8
        WR = 3 * NE
        RN = 8
        S2 = A2[:, :].rearrange("p (t n) -> p t n", n=256)

        def experts(tag, HT, ring, gated, place_w, place_r, place_t, hh, raw):
            m = Stage()
            m.HT, m.ring, m.gated, m.hh = HT, ring, gated, hh
            m.PP, m.CR = (HT + 1) // 2, (ring + 1) // 2
            m.inp = sem(tag + "_weights_loaded")
            m.raw_in = sem(tag + "_selection_loaded")
            m.wst = sem(tag + "_weight_stacks")
            m.rsp = sem(tag + "_router_stacks")
            m.str = sem(tag + "_strings")
            m.xt = sem(tag + "_transposed")
            m.xw = sem(tag + "_stacks")
            m.lp = sem(tag + "_logits_product")
            m.lk = sem(tag + "_logits_kept")
            m.sh = sem(tag + "_logits_shifted")
            m.ex = sem(tag + "_logits_exponentials")
            m.ws = sem(tag + "_token_weight_strings")
            m.wt = sem(tag + "_token_weights_transposed")
            m.wk = sem(tag + "_token_weights_kept")
            m.a = sem(tag + "_hidden_product")
            m.b = sem(tag + "_hidden_second_product")
            m.s = sem(tag + "_hidden_activated")
            m.tc = sem(tag + "_hidden_chain")
            m.h = sem(tag + "_hidden_ready")
            m.o = sem(tag + "_output_products")
            m.ot = sem(tag + "_output_kept")
            m.ft = sem(tag + "_output_transposed")
            m.fc = sem(tag + "_output_chain")
            m.add = sem(tag + "_output_added")
            m.done = sem(tag + "_finished")
            m.w1 = place_w([P, 3, HT * P], BF16)
            m.w3 = place_w([P, 3, HT * P], BF16) if gated else None
            m.raw1 = raw or place_w([P, HT * P])
            m.raw3 = place_w([P, HT * P]) if gated else None
            m.w2 = place_w([P, HT, D])
            m.sel = place_w([WR, HT * P], BF16)
            m.rst = place_r([P, 3, RN], BF16)
            m.rw = place_r([P, RN + 1 + RN])
            m.LG = place_r([P, TT, NE])
            m.OH = place_r([P, TT, NE])
            m.KEY = place_r([P, TT, NE])
            m.t1 = place_r([P, TT])
            m.t2 = place_r([P, TT])
            m.t3 = place_r([P, TT])
            m.WSF = place_r([P, TT * WR + P - WR], BF16)
            m.WS = m.WSF[:, 0:TT * WR].rearrange("p (t a n) -> p t a n", a=3, n=NE)
            m.WT = place_t([WR, TOK], BF16)
            return m

        def experts_weights(pool, m, sp_raw, scale=None):
            def ch(ins):
                link(pool, p_ch, n_pool, ins)

            for w, st in ((m.raw1, m.w1),) + (((m.raw3, m.w3),) if m.gated else ()):
                if scale is not None:
                    ch(nc.gpsimd.tensor_tensor(w, w, scale.to_broadcast([P, m.HT * P]), ALU.mult))
                ch(nc.gpsimd.tensor_copy(st[:, 0, :], w))
                ch(nc.gpsimd.tensor_copy(st[0:D, 1, :], st[0:D, 0, :]))
                ch(nc.gpsimd.tensor_tensor(w, w, st[:, 0, :], ALU.subtract))
                ch(nc.gpsimd.tensor_copy(st[:, 2, :], w))
                ch(nc.gpsimd.tensor_tensor(w, w, st[:, 2, :], ALU.subtract))
                ch(nc.gpsimd.tensor_copy(st[D:P, 1, :], w[D:P, :]))
            pool.sem_inc(m.wst, 1)
            pool.wait_ge(m.raw_in, 16)
            nc.gpsimd.tensor_copy(m.sel[:, :], m.raw1[0:WR, :]).then_inc(m.wst, 1)

        def experts_pe_pre(pe, m, strings):
            transposes(pe, m.str, m.xt, m.xw, strings)
            pe.wait_ge(m.xw, GT + 2)
            pe.wait_ge(m.rsp, 1)
            project(pe, m.rst, NE, m.lp, m.lk)

        def experts_act_pre(act, m):
            stack_copies(act, m.xt, m.xw, W)
            project_copies(act, NE, m.lp, m.lk, m.LG)
            act.wait_ge(m.sh, 1)
            nc.scalar.activation(m.LG, m.LG, ACT.Exp).then_inc(m.ex, 1)

        def softmax8(dve, m, bias=None):
            ch = lambda ins: link(dve, ln_ch, n_ln, ins)
            dve.wait_ge(m.lk, GT + 2)
            if bias is not None:
                ch(nc.vector.tensor_tensor(m.LG, m.LG, bias.unsqueeze(1).to_broadcast([P, TT, NE]), ALU.add))
            ch(nc.vector.tensor_reduce(m.t1, m.LG, AX.X, ALU.max))
            nc.vector.tensor_tensor(m.LG, m.LG, b3(m.t1, NE), ALU.subtract).then_inc(m.sh, 1)
            dve.wait_ge(m.ex, 1)
            ch(nc.vector.tensor_reduce(m.t1, m.LG, AX.X, ALU.add))
            ch(nc.vector.reciprocal(m.t1, m.t1))
            ch(nc.vector.tensor_tensor(m.LG, m.LG, b3(m.t1, NE), ALU.mult))

        def first_max(dve, m, top, oh, key, tmp):
            ch = lambda ins: link(dve, ln_ch, n_ln, ins)
            ch(nc.vector.tensor_reduce(top, m.LG, AX.X, ALU.max))
            ch(nc.vector.tensor_tensor(key, m.LG, b3(top, NE), ALU.is_equal))
            ch(nc.vector.tensor_tensor(key, key, m.rw[:, RN + 1:2 * RN + 1].unsqueeze(1).to_broadcast([P, TT, NE]), ALU.mult))
            ch(nc.vector.tensor_reduce(tmp, key, AX.X, ALU.max))
            ch(nc.vector.tensor_tensor(oh, key, b3(tmp, NE), ALU.is_equal))

        def weight_strings(dve, m, w):
            ch = lambda ins: link(dve, ln_ch, n_ln, ins)
            ch(nc.vector.memset(m.WSF[:, TT * WR:], 0.0))
            ch(nc.vector.tensor_copy(m.WS[:, :, 0, :], w))
            ch(nc.vector.tensor_tensor(w, w, m.WS[:, :, 0, :], ALU.subtract))
            ch(nc.vector.tensor_copy(m.WS[:, :, 1, :], w))
            ch(nc.vector.tensor_tensor(w, w, m.WS[:, :, 1, :], ALU.subtract))
            nc.vector.tensor_copy(m.WS[:, :, 2, :], w).then_inc(m.ws, 1)

        def experts_pe(pe, m, b2s=None):
            HT, PP = m.HT, m.PP
            pe.wait_ge(m.ws, 1)
            with pe.Fori(0, GT // 2) as i:
                for h in range(2):
                    pe.wait_ge(m.wk, i * 2 + h + 1)
                    for u in range(TPG):
                        ins = nc.tensor.transpose(bank16(6 + h)[:, u * P:(u + 1) * P],
                                                  m.WSF[:, bass.ds(((i * 2 + h) * TPG + u) * WR, P)], ident16[:, :])
                    ins.then_inc(m.wt, 1)
            pe.wait_ge(m.wk, GT + 2)
            pe.wait_ge(m.wst, 2)
            pe.sem_inc(m.o, m.CR)

            def hidden(gi, h, k):
                n, ba = gi * HT + k, (h * HT + k) % 2
                tok = bass.ds(gi * GW, GW)
                pe.wait_ge(m.h, n + 1)
                for p, w in enumerate((0, 1, 0)):
                    ins = nc.tensor.matmul(PS[:, ba, 0:GW], m.w1[:, p, k * P:(k + 1) * P], W[:, w, tok],
                                           start=(p == 0), stop=(p == 2))
                ins.then_inc(m.a, 1)
                if m.gated:
                    for p, w in enumerate((0, 1, 0)):
                        nc.tensor.matmul(PS[:, 2 + ba, 0:GW], m.w3[:, p, k * P:(k + 1) * P], W[:, w, tok],
                                         start=(p == 0), stop=(p == 2))
                nc.tensor.matmul(PS[:, 4 + ba, 0:GW], m.sel[:, k * P:(k + 1) * P], m.WT[:, tok],
                                 start=True, stop=True).then_inc(m.b, 1)

            def second(gi, j):
                both = 2 * j + 1 < HT
                pe.wait_ge(m.h, gi * HT + 2 * j + both + 3)
                if j == 0:
                    pe.wait_ge(m.ot, gi + 1)
                for y in range(1 + both):
                    k = 2 * j + y
                    ins = nc.tensor.matmul(PS[y * D:(y + 1) * D, 6, 0:GW], m.w2[:, k, :], m.hh[:, k % m.ring, :],
                                           start=(j == 0), stop=True, skip_group_check=True)
                if j == PP - 1 and b2s is not None:
                    for p in range(3):
                        ins = nc.tensor.matmul(PS[:, 6, 0:GW], b2s[:, p, :], m.WT[:, bass.ds(gi * GW, GW)],
                                               start=False, stop=True, skip_group_check=True)
                ins.then_inc(m.o, 1)

            def back(gi):
                pe.wait_ge(m.ot, gi + 2)
                pe.wait_ge(m.add, gi + 1)
                for a in range(TPG):
                    ins = nc.tensor.transpose(PS[:, 7, a * P:(a + 1) * P], OT[:, a * P:(a + 1) * P], ident[:, :])
                ins.then_inc(m.ft, 1)

            rest = list(range((HT - 2) // 2, PP))
            with pe.Fori(0, GT // 2) as i:
                for h in range(2):
                    gi = i * 2 + h
                    for k in range(HT):
                        hidden(gi, h, k)
                        if h and k < len(rest):
                            second(gi - 1, rest[k])
                        if k >= 3 and k % 2 and (k - 3) // 2 not in rest:
                            second(gi, (k - 3) // 2)
                        if h and k == 5:
                            back(gi - 1)
                for j in rest:
                    second(i * 2 + 1, j)
                back(i * 2 + 1)

        def experts_act(act, m, SL, func, bias=None):
            HT, PP = m.HT, m.PP
            act.sem_inc(m.wk, 2)
            with act.Fori(0, GT // 2) as i:
                for h in range(2):
                    act.wait_ge(m.wt, i * 2 + h + 1)
                    nc.scalar.copy(m.WT[:, bass.ds((i * 2 + h) * GW, GW)], bank16(6 + h)[0:WR, 0:GW]).then_inc(m.wk, 1)
            act.sem_inc(m.ot, 1)
            act.sem_inc(m.ft, 1)

            def keep(gi):
                act.wait_ge(m.o, (gi + 1) * PP + m.CR)
                act.wait_ge(m.ft, gi + 1)
                nc.scalar.copy(OT[:, :], PS[:, 6, 0:GW]).then_inc(m.ot, 1)

            with act.Fori(0, GT // 2) as i:
                for h in range(2):
                    gi = i * 2 + h
                    for k in range(HT):
                        n, ba = gi * HT + k, (h * HT + k) % 2
                        act.wait_ge(m.a, n + 1)
                        act.wait_ge(m.h, n + 1)
                        if bias is None:
                            nc.scalar.activation(SL[:, ba, :], PS[:, ba, 0:GW], func).then_inc(m.s, 1)
                        else:
                            nc.scalar.activation(SL[:, ba, :], PS[:, ba, 0:GW], func, bias=bias[:, k:k + 1]).then_inc(m.s, 1)
                        if h and k == 2:
                            keep(gi - 1)
                keep(i * 2 + 1)

        def experts_dve(dve, m, SL, TM, dst):
            HT, PP = m.HT, m.PP
            dve.sem_inc(m.h, 2)
            dve.sem_inc(m.add, 1)

            def add(gi):
                O = PS[:, 7, 0:GW].rearrange("p (t n) -> p t n", n=P)
                v = dst[:, bass.ds(gi * TPG, TPG), :]
                dve.wait_ge(m.ft, gi + 2)
                nc.vector.tensor_tensor(v, O[:, :, 0:D], v, ALU.add).then_inc(m.fc, 1)
                dve.wait_ge(m.fc, gi + 1)
                nc.vector.tensor_tensor(v, O[:, :, D:P], v, ALU.add).then_inc(m.add, 1)

            with dve.Fori(0, GT // 2) as i:
                for h in range(2):
                    gi = i * 2 + h
                    for k in range(HT):
                        n, ba = gi * HT + k, (h * HT + k) % 2
                        src = SL[:, ba, :]
                        dve.wait_ge(m.s, n + 1)
                        dve.wait_ge(m.b, n + 1)
                        if m.gated:
                            nc.vector.tensor_tensor(TM[:, ba, :], PS[:, 2 + ba, 0:GW], src, ALU.mult).then_inc(m.tc, 1)
                            dve.wait_ge(m.tc, n + 1)
                            src = TM[:, ba, :]
                        dve.wait_ge(m.o, gi * PP + k // 2 + 1)
                        nc.vector.tensor_tensor(m.hh[:, k % m.ring, :], PS[:, 4 + ba, 0:GW], src, ALU.mult).then_inc(m.h, 1)
                        if h and k == 6:
                            add(gi - 1)
                add(i * 2 + 1)
            dve.wait_ge(m.add, GT + 1)

        HID0 = -(-NE * int(8 / 3 * D) // P)
        pl2, pl5, pl3 = places(A2, 0), places(A5, 0), places(A3[:, :].bitcast(BF16), 0)
        f = experts("f", HID0, HID0, True, pl2, pl3, pl5, A4[:, :].rearrange("p (k n) -> p k n", n=GW), None)
        f.var, f.std = sem("f_square_sums"), sem("f_rms")
        fSL, fTM = pl5([P, 2, GW]), pl5([P, 2, GW])
        fOH2 = pl3([P, TT, NE])

        def f_sp(sp):
            sp.wait_ge(b_o, GT)
            for dst, name in ((f.raw1, "f_w1"), (f.raw3, "f_w3"), (f.w2, "f_w2")):
                sp.dma_start(dst, I[name]).then_inc(f.inp, 16)
            sp.wait_ge(b_yk, GT + 2)
            sp.dma_start(f.rw, I["f_r"]).then_inc(f.inp, 16)
            sp.wait_ge(f.wst, 1)
            sp.dma_start(f.raw1[0:WR, :], I["f_sel"]).then_inc(f.raw_in, 16)

        def f_pool(pool):
            pool.wait_ge(f.inp, 4 * 16)
            experts_weights(pool, f, None, f.rw[:, RN:RN + 1])

        def f_dve(dve):
            ch = lambda ins: link(dve, ln_ch, n_ln, ins)
            ch(nc.vector.tensor_tensor(Q2, XN[:, :, :], XN[:, :, :], ALU.mult))
            nc.vector.tensor_reduce(stat[:, 1, :], Q2, AX.X, ALU.add).then_inc(f.var, 1)
            dve.wait_ge(f.std, 1)
            ch(nc.vector.reciprocal(stat[:, 3, :], stat[:, 2, :]))
            ch(nc.vector.tensor_tensor(Q2, XN[:, :, :], b3(stat[:, 3, :], D), ALU.mult))
            split_x(dve, n_ln, Q2, Q2, f.str, 1)
            dve.wait_ge(f.inp, 4 * 16)
            cr = lambda ins: link(dve, ln_ch, n_ln, ins)
            cr(nc.vector.tensor_tensor(f.rw[:, 0:RN], f.rw[:, 0:RN], f.rw[:, RN:RN + 1].to_broadcast([P, RN]), ALU.mult))
            split_w(dve, ln_ch, n_ln, f.rw[:, 0:RN], f.rst, f.rsp, 1)
            softmax8(dve, f)
            first_max(dve, f, f.t1, f.OH, f.KEY, f.t3)
            cr(nc.vector.scalar_tensor_tensor(f.LG, f.OH, -2.0, f.LG, ALU.mult, ALU.add))
            first_max(dve, f, f.t2, fOH2, f.KEY, f.t3)
            cr(nc.vector.tensor_tensor(f.t3, f.t1, f.t2, ALU.add))
            cr(nc.vector.tensor_scalar(f.t3, f.t3, 1e-9, None, ALU.add))
            cr(nc.vector.reciprocal(f.t3, f.t3))
            cr(nc.vector.tensor_tensor(f.t1, f.t1, f.t3, ALU.mult))
            cr(nc.vector.tensor_tensor(f.t2, f.t2, f.t3, ALU.mult))
            cr(nc.vector.tensor_tensor(f.OH, f.OH, b3(f.t1, NE), ALU.mult))
            cr(nc.vector.tensor_tensor(fOH2, fOH2, b3(f.t2, NE), ALU.mult))
            cr(nc.vector.tensor_tensor(f.OH, f.OH, fOH2, ALU.add))
            weight_strings(dve, f, f.OH)
            experts_dve(dve, f, fSL, fTM, XN)
            nc.vector.tensor_tensor(H[:, :, :], H[:, :, :], XN[:, :, :], ALU.add).then_inc(f.done, 1)
            dve.wait_ge(f.done, 1)

        def f_act(act):
            act.wait_ge(f.var, 1)
            nc.scalar.activation(stat[:, 2, :], stat[:, 1, :], ACT.Sqrt, bias=epsc[:, 1:2], scale=1.0 / D).then_inc(f.std, 1)
            experts_act_pre(act, f)
            experts_act(act, f, fSL, ACT.Silu)

        def f_pe(pe):
            experts_pe_pre(pe, f, None)
            experts_pe(pe, f)


        SC = 64
        NC_ = NP // SC
        lam = sb("lam", [P, 5])
        sp_ = sb("ssm_parameters", [P, 24])
        s_in = sem("s_parameters_loaded")
        s_x = sem("s_exponent_ready")
        s_e = sem("s_exponentials")
        s_a = sem("s_angle_ready")
        s_sn = sem("s_sines")
        col = lambda k: sp_[:, k:k + 1]
        STEP, MAG, TH, K, XM, E, EM1, SH, SN, CO, NR, NI, LR, DEN, AL, BE, TA, TB_, AN = range(19)

        def s_parameters(dve):
            n = [0]
            ch = lambda ins: link(dve, ln_ch, n_ln, ins)
            tt = lambda o, a, b, op: ch(nc.vector.tensor_tensor(o, a, b, op))
            ts = lambda o, a, x, op: ch(nc.vector.tensor_scalar(o, a, x, None, op))
            dve.wait_ge(s_e, 1)
            lre, lim, up, dn = lam[:, 0:1], lam[:, 1:2], lam[:, 3:4], lam[:, 4:5]
            ts(col(LR), lre, -1.0, ALU.mult)
            tt(col(LR), col(LR), lre, ALU.min)
            tt(col(MAG), col(LR), col(STEP), ALU.mult)
            nc.vector.tensor_scalar(col(XM), col(MAG), -1.0, None, ALU.max).then_inc(s_x, 1)
            dve.wait_ge(s_x, 1)
            tt(col(TH), lim, col(STEP), ALU.mult)
            ts(col(K), col(TH), 1.0 / (2 * np.pi), ALU.mult)
            ts(col(K), col(K), 1.5 * 2.0 ** 23, ALU.add)
            ts(col(K), col(K), -1.5 * 2.0 ** 23, ALU.add)
            c1 = 6.28125
            c2 = float(np.float32(np.float32((2 * np.pi - c1) * 2 ** 20).round() / 2 ** 20))
            for c in (c1, c2, 2 * np.pi - c1 - c2):
                ch(nc.vector.scalar_tensor_tensor(col(TH), col(K), -float(c), col(TH), ALU.mult, ALU.add))
            ts(col(TH), col(TH), 3.1415925, ALU.min)
            ts(col(AN), col(TH), -3.1415925, ALU.max)
            nc.vector.tensor_scalar(col(TA), col(AN), 0.5, None, ALU.mult).then_inc(s_a, 1)
            dve.wait_ge(s_a, 1)
            dve.wait_ge(s_e, 2)
            ts(col(EM1), col(XM), 1.0 / 24, ALU.mult)
            ts(col(EM1), col(EM1), 1.0 / 6, ALU.add)
            tt(col(EM1), col(EM1), col(XM), ALU.mult)
            ts(col(EM1), col(EM1), 0.5, ALU.add)
            tt(col(EM1), col(EM1), col(XM), ALU.mult)
            ts(col(EM1), col(EM1), 1.0, ALU.add)
            tt(col(EM1), col(EM1), col(XM), ALU.mult)
            ts(col(TB_), col(MAG), -0.01, ALU.is_ge)
            tt(col(EM1), col(EM1), col(TB_), ALU.mult)
            ts(col(TB_), col(TB_), -1.0, ALU.mult)
            ts(col(TB_), col(TB_), 1.0, ALU.add)
            ts(col(NR), col(E), -1.0, ALU.add)
            tt(col(NR), col(NR), col(TB_), ALU.mult)
            tt(col(EM1), col(EM1), col(NR), ALU.add)
            dve.wait_ge(s_sn, 2)
            tt(col(SH), col(SH), col(SH), ALU.mult)
            ts(col(SH), col(SH), -2.0, ALU.mult)
            ts(col(CO), col(SH), 1.0, ALU.add)
            tt(col(NR), col(E), col(SH), ALU.mult)
            tt(col(NR), col(NR), col(EM1), ALU.add)
            tt(col(NI), col(E), col(SN), ALU.mult)
            tt(col(DEN), col(LR), col(LR), ALU.mult)
            ch(nc.vector.scalar_tensor_tensor(col(DEN), lim, lim, col(DEN), ALU.mult, ALU.add))
            ch(nc.vector.reciprocal(col(DEN), col(DEN)))
            tt(col(TA), col(NR), col(LR), ALU.mult)
            ch(nc.vector.scalar_tensor_tensor(col(TA), col(NI), lim, col(TA), ALU.mult, ALU.add))
            tt(col(TA), col(TA), col(DEN), ALU.mult)
            tt(col(TB_), col(NI), col(LR), ALU.mult)
            tt(col(K), col(NR), lim, ALU.mult)
            tt(col(TB_), col(TB_), col(K), ALU.subtract)
            tt(col(TB_), col(TB_), col(DEN), ALU.mult)
            tt(col(AL), col(TB_), dn, ALU.mult)
            ch(nc.vector.scalar_tensor_tensor(col(AL), col(TA), up, col(AL), ALU.mult, ALU.add))
            tt(col(BE), col(TB_), up, ALU.mult)
            ch(nc.vector.scalar_tensor_tensor(col(BE), col(TA), dn, col(BE), ALU.mult, ALU.subtract))

        def s_parameters_act(act):
            act.wait_ge(s_in, 16)
            nc.scalar.activation(col(STEP), lam[:, 2:3], ACT.Exp).then_inc(s_e, 1)
            act.wait_ge(s_x, 1)
            nc.scalar.activation(col(E), col(MAG), ACT.Exp).then_inc(s_e, 1)
            act.wait_ge(s_a, 1)
            nc.scalar.activation(col(SN), col(AN), ACT.Sin).then_inc(s_sn, 1)
            nc.scalar.activation(col(SH), col(TA), ACT.Sin).then_inc(s_sn, 1)

        TAB = A0[:, :].bitcast(F32).rearrange("p (k n) -> p k n", k=2)
        ps3 = places(A3[:, :].bitcast(BF16), 2 * 3250)
        fin0 = ps3([P, 2, SC + 1])
        fin1 = ps3([P, 2, NC_])
        s_tab = sem("s_table_ready")

        def s_tables(pool):
            n = [0]
            ch = lambda ins: link(pool, p_ch, n_pool, ins)

            def double(T, total):
                at = 1
                while at < total - 1:
                    m = min(at, total - 1 - at)
                    bc = lambda k: T[:, k, at:at + 1].to_broadcast([P, m])
                    c, s_ = T[:, 0, 1:1 + m], T[:, 1, 1:1 + m]
                    co, so = T[:, 0, at + 1:at + 1 + m], T[:, 1, at + 1:at + 1 + m]
                    tmp = ptmp[:, 0:m]
                    ch(nc.gpsimd.tensor_tensor(tmp, s_, bc(1), ALU.mult))
                    ch(nc.gpsimd.tensor_tensor(co, c, bc(0), ALU.mult))
                    ch(nc.gpsimd.tensor_tensor(co, co, tmp, ALU.subtract))
                    ch(nc.gpsimd.tensor_tensor(tmp, c, bc(1), ALU.mult))
                    ch(nc.gpsimd.tensor_tensor(so, s_, bc(0), ALU.mult))
                    ch(nc.gpsimd.tensor_tensor(so, so, tmp, ALU.add))
                    at += m

            for T in (fin0, fin1):
                ch(nc.gpsimd.memset(T[:, 0, 0:1], 1.0))
                ch(nc.gpsimd.memset(T[:, 1, 0:1], 0.0))
            ch(nc.gpsimd.tensor_copy(fin0[:, 0, 1:2], col(CO)))
            ch(nc.gpsimd.tensor_copy(fin0[:, 1, 1:2], col(SN)))
            double(fin0, SC + 1)
            ch(nc.gpsimd.tensor_copy(fin1[:, :, 1:2], fin0[:, :, SC:SC + 1]))
            double(fin1, NC_)
            pool.wait_ge(f.xw, GT + 2)
            for hb in range(2):
                cs_ = slice(hb * NC_ // 2, (hb + 1) * NC_ // 2)
                sh = [P, NC_ // 2, SC]
                hi = lambda k: fin1[:, k, cs_].unsqueeze(2).to_broadcast(sh)
                lo = lambda k: fin0[:, k, 0:SC].unsqueeze(1).to_broadcast(sh)
                o = lambda k: TAB[:, k, hb * NP // 2:(hb + 1) * NP // 2].rearrange("p (c j) -> p c j", j=SC)
                t = big.rearrange("p (c j) -> p c j", j=SC)
                ch(nc.gpsimd.tensor_tensor(t, hi(1), lo(1), ALU.mult))
                ch(nc.gpsimd.tensor_tensor(o(0), hi(0), lo(0), ALU.mult))
                ch(nc.gpsimd.tensor_tensor(o(0), o(0), t, ALU.subtract))
                ch(nc.gpsimd.tensor_tensor(t, hi(1), lo(0), ALU.mult))
                ch(nc.gpsimd.tensor_tensor(o(1), hi(0), lo(1), ALU.mult))
                ch(nc.gpsimd.tensor_tensor(o(1), o(1), t, ALU.add))
            pool.sem_inc(s_tab, 1)

        ptmp = sb("table_product", [P, SC])
        big = pl5([P, NP // 2])
        pa4 = places(A4[:, :].bitcast(BF16), 0)
        m1, m2, uu, zz, zc, zs = (pa4([P, 2, GW]) if k < 5 else None for k in range(6))
        pa5 = places(A3[:, :].bitcast(BF16), 0)
        zs = pa5([P, 2, GW])
        sB = pa5([P, 2, D])
        sQ = pa5([P, 2, P])
        sQr = pa5([P, P])
        sW = [pa5([P, 3, P], BF16), pa5([P, 3, P], BF16)]
        sC = pa5([P, 2, D])
        sCz = pa5([P, 2, D])
        zlast = pa5([P, 1])
        rb = pa5([P, GW])
        yt = pa5([P, 2, TPG, D])
        S = Stage()
        S.w = sem("s_weights_loaded")
        S.q = sem("s_input_weights")
        S.qt = sem("s_input_weights_transposed")
        S.ws = sem("s_weight_stacks")
        S.str = sem("s_strings")
        S.xt = sem("s_transposed")
        S.xw = sem("s_stacks")
        S.p = sem("s_input_product")
        S.pf = sem("s_input_product_read")
        S.u = sem("s_sum_ready")
        S.z = sem("s_scanned")
        S.zc = sem("s_turned_back")
        S.o = sem("s_output_product")
        S.ot = sem("s_output_kept")
        S.ft = sem("s_output_transposed")
        S.oc = sem("s_output_chain")
        S.add = sem("s_output_added")
        S.xa = sem("s_normed_added")
        S.sc = sem("s_scan_chain")

        def s_sp(sp):
            sp.wait_ge(f.done, 1)
            sp.dma_start(sB, I["s_b"]).then_inc(S.w, 16)
            sp.dma_start(sC, I["s_c"]).then_inc(S.w, 16)

        def s_dve(dve):
            layer_norm(dve, n_ln, ln_var)
            dve.wait_ge(ln_std, 3)
            finish_norm(dve, n_ln)
            split_x(dve, n_ln, XN[:, :, :], Q2, S.str, 1, S2)
            n_w = [0]
            ch = lambda ins: link(dve, ln_ch, n_ln, ins)
            dve.wait_ge(S.w, 2 * 16)
            dve.wait_ge(s_tab, 1)
            for k, (a, c) in enumerate(((AL, BE), (BE, AL))):
                v = sQ[:, k, 0:D]
                ch(nc.vector.tensor_scalar(v, sB[:, 0, :], col(a), None, ALU.mult))
                if k:
                    ch(nc.vector.tensor_scalar(v, v, -1.0, None, ALU.mult))
                ch(nc.vector.scalar_tensor_tensor(v, sB[:, 1, :], col(c), v, ALU.mult, ALU.add))
                ins = nc.vector.tensor_copy(sQ[:, k, D:P], v)
                ins.then_inc(S.q, 1)
            ch(nc.vector.tensor_tensor(sp_[:, 20:21], lam[:, 3:4], lam[:, 4:5], ALU.subtract))
            ch(nc.vector.tensor_scalar(sCz[:, 0, :], sC[:, 0, :], sp_[:, 20:21], None, ALU.mult))
            ch(nc.vector.tensor_scalar(sCz[:, 1, :], sC[:, 1, :], -1.0, None, ALU.mult))
            ch(nc.vector.memset(rb, 1.0))
            ch(nc.vector.tensor_scalar(rb, rb, col(E), None, ALU.mult))
            for k in range(2):
                dve.wait_ge(S.qt, k + 1)
                ch(nc.vector.tensor_copy(sQr, PS[:, k, 0:P]))
                split_w(dve, ln_ch, n_ln, sQr, sW[k], S.ws, k + 1)
            nc.vector.tensor_tensor(H[:, :, :], H[:, :, :], XN[:, :, :], ALU.add).then_inc(S.xa, 1)
            dve.wait_ge(S.xa, 1)
            dve.sem_inc(S.pf, 2)
            dve.sem_inc(S.add, 2)
            dve.sem_inc(S.sc, 1)

            def turn(gi, g, s_):
                dve.wait_ge(S.p, gi + 1)
                dve.wait_ge(S.u, gi + 1)
                t = bass.ds(g * GW, GW)
                nc.vector.tensor_tensor(m1[:, s_, :], PS[:, 2 * s_, 0:GW], TAB[:, 0, t], ALU.mult)
                nc.vector.tensor_tensor(m2[:, s_, :], PS[:, 2 * s_ + 1, 0:GW], TAB[:, 1, t], ALU.mult).then_inc(S.pf, 1)

            def scan(gi, s_, first):
                dve.wait_ge(S.u, gi + 3)
                dve.wait_ge(S.zc, gi + 1)
                dve.wait_ge(S.z, gi + 1)
                nc.vector.tensor_tensor_scan(zz[:, s_, :], rb, uu[:, s_, :], 0.0 if first else zz[:, 1 - s_, GW - 1:GW],
                                             ALU.mult, ALU.add).then_inc(S.z, 1)

            def add(gi, s_):
                O = PS[:, 6 + s_, 0:GW].rearrange("p (t n) -> p t n", n=P)
                v = H[:, bass.ds(gi * TPG, TPG), :]
                y = yt[:, s_, :, :]
                dve.wait_ge(S.ft, gi + 2)
                dve.wait_ge(S.oc, gi * 2 + 1)
                nc.vector.tensor_copy(y, O[:, :, 0:D]).then_inc(S.oc, 1)
                dve.wait_ge(S.oc, gi * 2 + 2)
                nc.vector.tensor_tensor(y, O[:, :, D:P], y, ALU.add).then_inc(S.oc, 1)
                dve.wait_ge(S.oc, gi * 2 + 3)
                nc.vector.scalar_tensor_tensor(v, y, 0.0, v, ALU.max, ALU.add).then_inc(S.add, 1)

            dve.sem_inc(S.oc, 1)
            dve.sem_inc(S.z, 1)
            for b in range(B):
                turn(b * NG, 0, b)
                scan(b * NG, b, True)
                with dve.Fori(0, NG // 2) as i:
                    for h in range(2):
                        g = i * 2 + h + 1
                        gi = b * NG + g
                        turn(gi, g, (b + h + 1) % 2)
                        add(gi - 1, (b + h) % 2)
                        scan(gi, (b + h + 1) % 2, False)
                add(b * NG + NG - 1, b)
            dve.wait_ge(S.add, GT + 2)

        def s_pool(pool):
            pool.sem_inc(S.u, 2)
            pool.sem_inc(S.zc, 2)

            def sum_(gi, s_):
                pool.wait_ge(S.pf, gi + 3)
                pool.wait_ge(S.z, gi + 1)
                nc.gpsimd.tensor_tensor(uu[:, s_, :], m1[:, s_, :], m2[:, s_, :], ALU.add).then_inc(S.u, 1)

            def back(gi, g, s_):
                pool.wait_ge(S.z, gi + 2)
                pool.wait_ge(S.o, gi + 1)
                t = bass.ds(g * GW, GW)
                nc.gpsimd.tensor_tensor(zc[:, s_, :], zz[:, s_, :], TAB[:, 0, t], ALU.mult).then_inc(S.sc, 1)
                nc.gpsimd.tensor_tensor(zs[:, s_, :], zz[:, s_, :], TAB[:, 1, t], ALU.mult).then_inc(S.zc, 1)

            for b in range(B):
                sum_(b * NG, b)
                back(b * NG, 0, b)
                with pool.Fori(0, NG // 2) as i:
                    for h in range(2):
                        g = i * 2 + h + 1
                        gi = b * NG + g
                        sum_(gi, (b + h + 1) % 2)
                        back(gi, g, (b + h + 1) % 2)

        def s_act(act):
            act.wait_ge(ln_var, 3)
            nc.scalar.activation(stat[:, 2, :], stat[:, 1, :], ACT.Sqrt, bias=epsc[:, 0:1], scale=1.0 / D).then_inc(ln_std, 1)
            stack_copies(act, S.xt, S.xw, W)
            act.sem_inc(S.ft, 1)

            def keep(gi, s_):
                act.wait_ge(S.o, gi + 3)
                act.wait_ge(S.ft, gi + 1)
                nc.scalar.copy(OT[:, :], PS[:, 4 + s_, 0:GW]).then_inc(S.ot, 1)

            for b in range(B):
                keep(b * NG, b)
                with act.Fori(0, NG // 2) as i:
                    for h in range(2):
                        keep(b * NG + i * 2 + h + 1, (b + h + 1) % 2)

        def s_pe(pe):
            transposes(pe, S.str, S.xt, S.xw, S2)
            for k in range(2):
                pe.wait_ge(S.q, k + 1)
                nc.tensor.transpose(PS[:, k, 0:P], sQ[:, k, :], ident[:, :]).then_inc(S.qt, 1)
            pe.wait_ge(S.xw, GT + 2)
            pe.wait_ge(S.ws, 2)
            pe.sem_inc(S.o, 2)

            def inp(gi, s_):
                pe.wait_ge(S.pf, gi + 1)
                for k in range(2):
                    for p_, w in enumerate((0, 1, 0)):
                        ins = nc.tensor.matmul(PS[:, 2 * s_ + k, 0:GW], sW[k][:, p_, :], W[:, w, bass.ds(gi * GW, GW)],
                                               start=(p_ == 0), stop=(p_ == 2))
                ins.then_inc(S.p, 1)

            def outp(gi, s_):
                pe.wait_ge(S.zc, gi + 3)
                for y, z in enumerate((zc, zs)):
                    ins = nc.tensor.matmul(PS[y * D:(y + 1) * D, 4 + s_, 0:GW], sCz[:, y, :], z[:, s_, :],
                                           start=True, stop=True, skip_group_check=True)
                ins.then_inc(S.o, 1)

            def fin(gi, s_):
                pe.wait_ge(S.ot, gi + 1)
                pe.wait_ge(S.add, gi + 1)
                for a in range(TPG):
                    ins = nc.tensor.transpose(PS[:, 6 + s_, a * P:(a + 1) * P], OT[:, a * P:(a + 1) * P], ident[:, :])
                ins.then_inc(S.ft, 1)

            for b in range(B):
                inp(b * NG, b)
                with pe.Fori(0, NG // 2) as i:
                    for h in range(2):
                        gi = b * NG + i * 2 + h + 1
                        inp(gi, (b + h + 1) % 2)
                        outp(gi - 1, (b + h) % 2)
                        fin(gi - 1, (b + h) % 2)
                outp(b * NG + NG - 1, b)
                fin(b * NG + NG - 1, b)


        HID1 = NE * F1 // P
        CAP = -(-5 * B * N // (4 * NE))
        qa5, qa0, qa3 = places(A5, 0), places(A0, 0), places(A3[:, :].bitcast(BF16), 0)
        qa4 = places(A4[:, :].bitcast(BF16), 0)
        ghh = qa4([P, 8, GW])
        gSL = qa4([P, 2, GW])
        g_ = experts("g", HID1, 8, False, qa5, qa0, qa3, ghh, None)
        gb1 = qa5([P, HID1])
        gb2 = qa5([WR, D])
        gb2s = qa5([WR, 3, P], BF16)
        gbias = qa5([P, NE])
        upto = qa5([P, P])
        ones = qa5([P, P])
        TOTT = qa0([P, NE, TT])
        SCN = qa0([P, NE, TT])
        smask = qa5([P, NE, TT])
        wide = qa0([P, TT, D])
        limit = qa0([P, 2])
        g_.cum = sem("g_positions_counted")
        g_oh = sem("g_choice_ready")

        def g_sp(sp):
            sp.wait_ge(f.done, 1)
            sp.wait_ge(s_tab, 1)
            for dst, name in ((g_.raw1, "g_w1"), (g_.w2, "g_w2"), (gb1, "g_b1"), (gb2, "g_b2"), (gbias, "g_bias"), (upto, "upto")):
                sp.dma_start(dst, I[name]).then_inc(g_.inp, 16)
            sp.wait_ge(g_.wst, 1)
            sp.dma_start(g_.raw1[0:WR, :], I["g_sel"]).then_inc(g_.raw_in, 16)
            sp.wait_ge(S.add, GT + 2)
            sp.dma_start(g_.rw, I["g_r"]).then_inc(g_.inp, 16)

        def g_pool(pool):
            pool.wait_ge(g_.inp, 6 * 16)
            experts_weights(pool, g_, None)

        def g_dve(dve):
            layer_norm(dve, n_ln, ln_var)
            dve.wait_ge(ln_std, 4)
            finish_norm(dve, n_ln)
            split_x(dve, n_ln, XN[:, :, :], Q2, g_.str, 1, S2)
            cr = lambda ins: link(dve, ln_ch, n_ln, ins)
            dve.wait_ge(g_.inp, 7 * 16)
            split_w(dve, ln_ch, n_ln, g_.rw[:, 0:RN], g_.rst, g_.rsp, 1)
            cr(nc.vector.memset(XN[:, :, :], 0.0))
            cr(nc.vector.memset(ones, 1.0))
            cr(nc.vector.memset(gb2s, 0.0))
            cr(nc.vector.memset(smask, 1.0))
            cr(nc.vector.memset(smask[:, :, 0:1], 0.0))
            for k in range(3):
                cr(nc.vector.tensor_copy(gb2s[:, k, 0:D], gb2))
                if k < 2:
                    cr(nc.vector.tensor_tensor(gb2, gb2, gb2s[:, k, 0:D], ALU.subtract))
            softmax8(dve, g_, gbias)
            first_max(dve, g_, g_.t1, g_.OH, g_.KEY, g_.t3)
            nc.vector.tensor_tensor(g_.OH, g_.OH, b3(valid[:, :], NE), ALU.mult).then_inc(g_oh, 1)
            dve.wait_ge(g_.cum, 1)
            for k in range(2):
                v = PS[:, 2 + k, 0:NT * NE].rearrange("p (t e) -> p e t", e=NE)
                cr(nc.vector.tensor_copy(TOTT[:, :, k * NT:(k + 1) * NT], v))
            fl = lambda a: a.rearrange("p e t -> p (e t)")
            cr(nc.vector.tensor_tensor_scan(fl(SCN), fl(smask), fl(TOTT), 0.0, ALU.mult, ALU.add))
            cr(nc.vector.tensor_tensor(SCN, SCN, TOTT, ALU.subtract))
            for k in range(2):
                tl = slice(k * NT, (k + 1) * NT)
                cr(nc.vector.tensor_tensor(g_.KEY[:, tl, :], PS[:, k, 0:NT * NE].rearrange("p (t e) -> p t e", e=NE),
                                           SCN[:, :, tl].rearrange("p e t -> p t e"), ALU.add))
            cr(nc.vector.tensor_tensor(g_.KEY, g_.KEY, g_.OH, ALU.mult))
            cr(nc.vector.tensor_reduce(g_.t2, g_.KEY, AX.X, ALU.add))
            cr(nc.vector.tensor_scalar(g_.t2, g_.t2, float(CAP), None, ALU.is_le))
            cr(nc.vector.tensor_tensor(g_.t1, g_.t1, g_.t2, ALU.mult))
            cr(nc.vector.tensor_tensor(g_.OH, g_.OH, b3(g_.t1, NE), ALU.mult))
            weight_strings(dve, g_, g_.OH)
            experts_dve(dve, g_, gSL, None, XN)
            mask = wide.bitcast(mybir.dt.uint32)
            cr(nc.vector.memset(limit[:, 0:1], 1e4))
            cr(nc.vector.memset(limit[:, 1:2], -1e4))
            cr(nc.vector.memset(Q2, 0.0))
            cr(nc.vector.tensor_tensor(wide, XN[:, :, :], XN[:, :, :], ALU.is_equal))
            cr(nc.vector.copy_predicated(Q2, mask, XN[:, :, :]))
            for k, (bound, op) in enumerate(((3.4028235e38, ALU.is_gt), (-3.4028235e38, ALU.is_lt))):
                cr(nc.vector.tensor_scalar(wide, Q2, bound, None, op))
                cr(nc.vector.copy_predicated(Q2, mask, limit[:, k:k + 1].unsqueeze(2).to_broadcast([P, TT, D])))
            nc.vector.tensor_tensor(H[:, :, :], H[:, :, :], Q2, ALU.add).then_inc(g_.done, 1)

        def g_act(act):
            act.wait_ge(ln_var, 4)
            nc.scalar.activation(stat[:, 2, :], stat[:, 1, :], ACT.Sqrt, bias=epsc[:, 0:1], scale=1.0 / D).then_inc(ln_std, 1)
            experts_act_pre(act, g_)
            experts_act(act, g_, gSL, ACT.Relu, gb1)

        def g_pe(pe):
            experts_pe_pre(pe, g_, S2)
            pe.wait_ge(g_oh, 1)
            for m in range(2):
                for k in range(2):
                    ins = nc.tensor.matmul(PS[:, 2 * m + k, 0:NT * NE], (upto, ones)[m],
                                           g_.OH[:, k * NT:(k + 1) * NT, :].rearrange("p t e -> p (t e)"), start=True, stop=True)
            ins.then_inc(g_.cum, 1)
            experts_pe(pe, g_, gb2s)

        @block.sync
        def _(sp):
            sp.dma_start(x_pad, I["xpad"]).then_inc(t_in, 16)
            sp.dma_start(c1w[:, :], I["c1w"]).then_inc(t_in, 16)
            sp.dma_start(bnp[:, :], I["bnp"]).then_inc(t_in, 16)
            sp.dma_start(c2w, I["c2w"]).then_inc(t_in, 16)
            sp.dma_start(b2[:, :], I["b2"]).then_inc(t_in, 16)
            sp.dma_start(ident[:, :], I["ident"]).then_inc(c_in, 16)
            sp.dma_start(lam[:, :], I["lam"]).then_inc(s_in, 16)
            sp.dma_start(valid[:, :], I["valid"]).then_inc(c_in, 16)
            sp.dma_start(qk2[:, :, :], I["qk"]).then_inc(c_in, 16)
            sp.wait_ge(t_a, 8 * (IMG // RG))
            sp.dma_start(scratch.rearrange("b (c h) w -> (b c) (h w)", h=IMG), conv).then_inc(t_out, 16)
            sp.wait_ge(t_out, 16)
            for b in range(B):
                t0 = b * NT
                sp.dma_start(H[0:1, t0, :], I["cls"]).then_inc(h_in, 16)
                sp.dma_start(H[1:P, t0, :], scratch[b, 0:P - 1, :]).then_inc(h_in, 16)
                sp.dma_start(H[:, t0 + 1:t0 + NT - 1, :],
                             scratch[b, P - 1:P - 1 + (NT - 2) * P, :].rearrange("(t p) d -> p t d", p=P)).then_inc(h_in, 16)
                sp.dma_start(H[0:1, t0 + NT - 1, :], scratch[b, IMG * IMG - 1:IMG * IMG, :]).then_inc(h_in, 16)
                sp.dma_start(H[1:P, t0 + NT - 1, :], I["cls"].to_broadcast([P - 1, D])).then_inc(h_in, 16)
            b_sp(sp)
            b_sp_rows(sp)
            f_sp(sp)
            s_sp(sp)
            g_sp(sp)
            sp.wait_ge(g_.done, 1)
            for b in range(B):
                sp.dma_start(out[b, 0:N - 1, :].rearrange("(t p) d -> p t d", p=P), H[:, b * NT:(b + 1) * NT - 1, :]).then_inc(o_out, 16)
                sp.dma_start(out[b, N - 1:N, :], H[0:1, (b + 1) * NT - 1, :]).then_inc(o_out, 16)
            sp.wait_ge(o_out, 4 * 16)

        @block.tensor
        def _(pe):
            pe.wait_ge(t_in, 5 * 16)
            for r in range(IMG // RG):
                rows = x_pad[:, 1 + r * RG:1 + (r + 1) * RG, 1:1 + IMG]
                if r >= 2:
                    pe.wait_ge(t_ys, r - 1)
                nc.tensor.matmul(PS[0:B * CR, r % 2, :].rearrange("p (h w) -> p h w", w=IMG), c1w[:, :], rows,
                                 start=True, stop=True).then_inc(t_y, 1)
                pe.wait_ge(t_ys, r + 1)
                for k in range(TAPS):
                    n = r * TAPS + k
                    if n >= 4:
                        pe.wait_ge(t_p, n - 3)
                    nc.tensor.matmul(PS[:, 2 + n % 4, :], c2w[:, k, :], yv[:, r % 2, :],
                                     start=True, stop=True).then_inc(t_w, 1)
            transposes(pe, x_str, x_t, x_w)
            pe.wait_ge(x_w, GT + 2)
            pe.wait_ge(a_ch, 4)
            nc.tensor.matmul(PS[:, 2, 0:D], qkc[:, 0, :], qkc[:, 1, 0:D], start=True, stop=True).then_inc(a_m, 1)
            pe.wait_ge(a_ms, 1)
            project(pe, MS, D, a_q, a_qe)
            transposes(pe, a_qstr, a_qpt, a_qp)
            pe.wait_ge(a_qp, GT + 2)
            pe.sem_inc(a_pv, 2)

            def qk(b, g, m, k, n2):
                pe.wait_ge(a_ex, n2 + 1)
                for p, w in enumerate((0, 1, 0)):
                    ins = nc.tensor.matmul(PS[:, k % 3, 0:GW], W[:, w, bass.ds(b * NP + m * P, P)],
                                           QT[:, p, bass.ds(g * GW, GW)], start=(p == 0), stop=(p == 2))
                ins.then_inc(a_s2, 1)

            def mx(b, g, jj, u, n1):
                pe.wait_ge(a_s1f, n1 + 1)
                for p in range(2):
                    ins = nc.tensor.matmul(PS[:, 3 + u, 0:GW], QP[:, p, bass.ds((b * NG + g) * GW + u * P, P)],
                                           W[:, 0, bass.ds(b * NP + jj * GW, GW)], start=(p == 0), stop=(p == 1))
                ins.then_inc(a_s1, 1)

            def pv(n2, v, k, both, first):
                pe.wait_ge(a_ex, n2 + 4 + both)
                pe.wait_ge(a_vs, v)
                for y in range(1 + both):
                    ins = nc.tensor.matmul(PS[y * D:(y + 1) * D, 6, 0:GW], VS[:, k + y, :], PT[:, k + y, :],
                                           start=first, stop=True, skip_group_check=True)
                ins.then_inc(a_pv, 1)

            def fin(gi):
                pe.wait_ge(a_ot, gi + 2)
                for a in range(TPG):
                    ins = nc.tensor.transpose(PS[:, 7, a * P:(a + 1) * P], OT[:, a * P:(a + 1) * P], ident[:, :])
                ins.then_inc(a_ft, 1)

            def prep(gi, half, nofin=False):
                if half == 0:
                    pe.wait_ge(a_str, gi + 1)
                    if not nofin:
                        pe.wait_ge(a_o, gi)
                pe.wait_ge(a_qt, gi * 2 + half + 1)
                for w in ((0, 1), (2,))[half]:
                    for u in range(TPG):
                        o = (w % 2) * TPG + u
                        c = (0, 1, 3)[w] * D
                        ins = nc.tensor.transpose(bank16(7)[:, o * P:(o + 1) * P],
                                                  QTS[:, u, :, :].rearrange("p a n -> p (a n)")[:, c:c + P], ident16[:, :])
                ins.then_inc(a_tq, 1)

            def run(b, g, i6, n, p2, p1, first=False, last=False):
                gi = b * NG + g
                n2 = gi * NT + i6 * 6
                v0 = gi * NG + i6 * 2
                n1 = (gi + p1) * NT + i6 * 6 if p1 is not None else 0
                for k in range(n):
                    if p2:
                        qk(b, g, i6 * 6 + k, k, n2 + k)
                    if p1 is not None:
                        mx(b, g + p1, i6 * 2 + k // 3, k % 3, n1 + k)
                    if p2 and k == 1 and not first:
                        pv(n2 - 2, v0, 4, 1, False)
                    if p2 and k in (3, 5):
                        if first and k == 3:
                            pe.wait_ge(a_ot, gi + 1)
                        pv(n2 + k - 3, v0 + 1 + (k - 2) // 3, k - 3, 1, first and k == 3)
                if p2 and last:
                    pv(n2, v0 + 1, 0, 1, False)
                    pv(n2 + 2, v0 + 1, 2, 0, False)

            def step(b, g, p1, pr, before=True):
                gi = b * NG + g
                pe.wait_ge(a_qt, gi * 2 + 3)
                run(b, g, 0, 6, True, p1, first=True)
                if before:
                    fin(gi - 1)
                if pr is not None:
                    prep(gi + pr, 0)
                with pe.Fori(1, 3) as i6:
                    run(b, g, i6, 6, True, p1)
                if pr is not None:
                    prep(gi + pr, 1)
                with pe.Fori(3, 5) as i6:
                    run(b, g, i6, 6, True, p1)
                run(b, g, 5, 3, True, p1, last=True)

            for b in range(B):
                for g in range(2):
                    with pe.Fori(0, 5) as i6:
                        run(b, 0, i6, 6, False, g)
                    run(b, 0, 5, 3, False, g)
                    if g == 0:
                        prep(b * NG, 0, nofin=b == 0)
                        prep(b * NG, 1)
                step(b, 0, 2, 1, before=b > 0)
                with pe.Fori(1, NG - 2) as g:
                    step(b, g, 2, 1)
                step(b, NG - 2, None, 1)
                step(b, NG - 1, None, None)
            fin(GT - 1)
            b_pe(pe)
            bo_pe(pe)
            f_pe(pe)
            s_pe(pe)
            g_pe(pe)

        @block.scalar
        def _(act):
            s_parameters_act(act)
            act.wait_ge(t_in, 5 * 16)
            act.wait_ge(c_id, 1)
            nc.scalar.activation(bns[:, 0:1], bnp[:, 4:5], ACT.Sqrt, bias=epsc[0:B * CR, 0:1]).then_inc(t_std, 1)
            act.wait_ge(t_bn, 1)
            for r in range(IMG // RG):
                act.wait_ge(t_y, r + 1)
                if r >= 2:
                    act.wait_ge(t_w, (r - 1) * TAPS)
                nc.scalar.activation(yv[:, r % 2, :], PS[0:B * CR, r % 2, :], ACT.Relu, bias=bns[:, 3:4],
                                     scale=bns[:, 1:2]).then_inc(t_ys, 1)
            act.wait_ge(ln_var, 1)
            nc.scalar.activation(stat[:, 2, :], stat[:, 1, :], ACT.Sqrt, bias=epsc[:, 0:1], scale=1.0 / D).then_inc(ln_std, 1)
            stack_copies(act, x_t, x_w, W)
            project_copies(act, D, a_q, a_qe, Q2)
            stack_copies(act, a_qpt, a_qp, QP)
            act.sem_inc(a_ex, 3)
            act.sem_inc(a_qt, 1)

            def prep(gi, g, half):
                act.wait_ge(a_tq, gi * 2 + half + 1)
                ws = ((0, 2), (2, 3))[half]
                k = ws[1] - ws[0]
                nc.scalar.copy(QT[:, ws[0]:ws[1], bass.ds(g * GW, GW)],
                               bank16(7)[:, 0:k * GW].rearrange("p (w n) -> p w n", w=k)).then_inc(a_qt, 1)

            def run(gi, i6, n, need):
                for k in range(n):
                    n2 = gi * NT + i6 * 6 + k
                    act.wait_ge(a_s2, n2 + 1)
                    if k % 2 == 0:
                        act.wait_ge(a_pv, gi * NPAIR + i6 * 3 + need[k // 2] + 2)
                    nc.scalar.activation(PT[:, k, :], PS[:, k % 3, 0:GW], ACT.Exp).then_inc(a_ex, 1)

            def step(b, g, pr):
                gi = b * NG + g
                run(gi, 0, 6, (-1, 0, 0))
                if pr is not None:
                    prep(gi + pr, g + pr, 0)
                with act.Fori(1, 3) as i6:
                    run(gi, i6, 6, (-2, -1, 0))
                if pr is not None:
                    prep(gi + pr, g + pr, 1)
                with act.Fori(3, 5) as i6:
                    run(gi, i6, 6, (-2, -1, 0))
                run(gi, 5, 3, (-2, -1))

            for b in range(B):
                prep(b * NG, 0, 0)
                prep(b * NG, 0, 1)
                with act.Fori(0, NG - 2) as g:
                    step(b, g, 1)
                step(b, NG - 2, 1)
                step(b, NG - 1, None)
            act.wait_ge(ln_var, 2)
            nc.scalar.activation(stat[:, 2, :], stat[:, 1, :], ACT.Sqrt, bias=epsc[:, 0:1], scale=1.0 / D).then_inc(ln_std, 1)
            b_act(act)
            bo_act(act)
            f_act(act)
            s_act(act)
            g_act(act)

        @block.gpsimd
        def _(pool):
            for r in range(IMG // RG):
                acc = conv[:, r * 512:(r + 1) * 512]
                for k in range(1, TAPS):
                    n = r * (TAPS - 1) + k - 1
                    pool.wait_ge(t_p, r * TAPS + k + 1)
                    if n:
                        pool.wait_ge(t_a, n)
                    nc.gpsimd.tensor_tensor(acc, acc, tapp[:, n % SLOT, :], ALU.add).then_inc(t_a, 1)

            def stage(gi, b, i6, t, need):
                pool.wait_ge(x_str, 1)
                pool.wait_ge(a_pv, gi * NPAIR + i6 * 3 + need + 2)
                j = bass.ds(b * NT + i6 * 6 + 3 * t, 3)
                nc.gpsimd.tensor_tensor(VS[:, 3 * t:3 * t + 3, :], VA[:, j, :],
                                        valid[:, j].unsqueeze(2).to_broadcast([P, TPG, D]), ALU.mult).then_inc(a_vs, 1)

            for b in range(B):
                with pool.Fori(0, NG) as g:
                    gi = b * NG + g
                    stage(gi, b, 0, 0, 0)
                    stage(gi, b, 0, 1, 0)
                    with pool.Fori(1, 5) as i6:
                        stage(gi, b, i6, 0, -1)
                        stage(gi, b, i6, 1, 0)
                    stage(gi, b, 5, 0, -1)
            b_pool(pool)
            f_pool(pool)
            s_tables(pool)
            g_pool(pool)
            s_pool(pool)

        @block.vector
        def _(dve):
            nc.vector.memset(epsc[:, 0:1], EPS)
            nc.vector.memset(epsc[:, 1:2], 1e-6)
            s_parameters(dve)
            dve.wait_ge(c_in, 3 * 16)
            nc.vector.tensor_copy(ident16[:, :], ident[:, :]).then_inc(c_id, 1)
            n_bn = [0]
            dve.wait_ge(t_std, 1)
            link(dve, t_ch, n_bn, nc.vector.reciprocal(bns[:, 0:1], bns[:, 0:1]))
            link(dve, t_ch, n_bn, nc.vector.tensor_tensor(bns[:, 1:2], bnp[:, 1:2], bns[:, 0:1], ALU.mult))
            link(dve, t_ch, n_bn, nc.vector.tensor_tensor(bns[:, 2:3], bnp[:, 0:1], bnp[:, 3:4], ALU.subtract))
            nc.vector.scalar_tensor_tensor(bns[:, 3:4], bns[:, 2:3], bns[:, 1:2], bnp[:, 2:3], ALU.mult,
                                           ALU.add).then_inc(t_bn, 1)
            for r in range(IMG // RG):
                for k in range(TAPS):
                    n = r * TAPS + k
                    m = r * (TAPS - 1) + k - 1
                    di, dj = k // 3, k % 3
                    dve.wait_ge(t_w, n + 1)
                    if k:
                        if m >= SLOT:
                            dve.wait_ge(t_a, m - SLOT + 1)
                        dst = tapp[:, m % SLOT, :]
                    else:
                        dst = conv[:, r * 512:(r + 1) * 512]
                    nc.vector.scalar_tensor_tensor(dst.rearrange("p (h w) -> p h w", w=IMG),
                                                   PS[:, 2 + n % 4, :].rearrange("p (h w) -> p h w", w=IMG), b2[:, k:k + 1],
                                                   x_pad[:, r * RG + di:r * RG + di + RG, dj:dj + IMG],
                                                   ALU.add, ALU.mult).then_inc(t_p, 1)
            dve.wait_ge(h_in, 10 * 16)
            layer_norm(dve, n_ln, ln_var)
            dve.wait_ge(ln_std, 1)
            finish_norm(dve, n_ln)
            link(dve, ln_ch, n_ln, nc.vector.tensor_scalar(XN[:, :, :], XN[:, :, :], 1.0, None, ALU.add))
            link(dve, ln_ch, n_ln, nc.vector.tensor_copy(VA, XN[:, :, :]))
            split_x(dve, n_ln, XN[:, :, :], Q2, x_str, 1)
            n_a = [0]
            ch = lambda ins: link(dve, a_ch, n_a, ins)
            ch(nc.vector.tensor_reduce(qks[:, :], qk2[:, :, :], AX.X, ALU.add))
            ch(nc.vector.tensor_scalar(qks[:, :], qks[:, :], -1.0 / D, None, ALU.mult))
            ch(nc.vector.tensor_tensor(qkc[:, :, 0:D], qk2[:, :, :], qks[:, :].unsqueeze(2).to_broadcast([D, 2, D]), ALU.add))
            ch(nc.vector.tensor_copy(qkc[:, :, D:P], qkc[:, :, 0:D]))
            dve.wait_ge(a_m, 1)
            ch(nc.vector.tensor_scalar(mres[:, :], PS[:, 2, 0:D], float(D) ** -0.5, None, ALU.mult))
            split_w(dve, a_ch, n_a, mres[:, :], MS, a_ms, 1)
            dve.wait_ge(a_qe, GT + 2)
            dve.wait_ge(x_w, GT + 2)
            s = xstr.rearrange("p t (a n) -> p t a n", n=D)
            ch(nc.vector.tensor_copy(s[:, :, 0, :], Q2))
            ch(nc.vector.tensor_copy(s[:, :, 1, :], s[:, :, 0, :]))
            ch(nc.vector.tensor_tensor(XN[:, :, :], Q2, s[:, :, 0, :], ALU.subtract))
            ch(nc.vector.tensor_copy(s[:, :, 2, :], XN[:, :, :]))
            nc.vector.tensor_copy(s[:, :, 3, :], s[:, :, 2, :]).then_inc(a_qstr, 1)

            dve.sem_inc(a_s1f, 3)
            dve.sem_inc(a_ot, 1)
            dve.sem_inc(a_o, 1)

            def maxima(gi, lo=0, hi=NG):
                with dve.Fori(lo, hi) as jj:
                    for u in range(TPG):
                        dve.wait_ge(a_s1, gi * NT + jj * TPG + u + 1)
                        nc.vector.tensor_reduce(MX[:, u, bass.ds(jj, 1)], PS[:, 3 + u, 0:GW], AX.X, ALU.max).then_inc(a_s1f, 1)

            CH = 7

            def prep(gi, g, b):
                k = [gi * CH]

                def chn(ins):
                    ins.then_inc(a_pc, 1)
                    k[0] = k[0] + 1
                    dve.wait_ge(a_pc, k[0])

                dve.wait_ge(a_s1f, (gi + 1) * NT + 3)
                chn(nc.vector.tensor_reduce(mm[:, 0, :], MX[:, :, :], AX.X, ALU.max))
                chn(nc.vector.tensor_scalar(mm[:, 1, :], mm[:, 0, :], -1.0 / D, None, ALU.mult))
                chn(nc.vector.tensor_tensor(qtm[:, :, :], Q2[:, bass.ds(gi * TPG, TPG), :],
                                            mm[:, 1, :].unsqueeze(2).to_broadcast([P, TPG, D]), ALU.add))
                dve.wait_ge(a_tq, gi * 2)
                chn(nc.vector.tensor_copy(QTS[:, :, 0:2, :], qtm[:, :, :].unsqueeze(2).to_broadcast([P, TPG, 2, D])))
                chn(nc.vector.tensor_tensor(qtm[:, :, :], qtm[:, :, :], QTS[:, :, 0, :], ALU.subtract))
                chn(nc.vector.tensor_copy(QTS[:, :, 3:5, :], qtm[:, :, :].unsqueeze(2).to_broadcast([P, TPG, 2, D])))
                chn(nc.vector.tensor_tensor(qtm[:, :, :], qtm[:, :, :], QTS[:, :, 3, :], ALU.subtract))
                nc.vector.tensor_copy(QTS[:, :, 2, :], qtm[:, :, :]).then_inc(a_str, 1)

            def keep(gi):
                dve.wait_ge(a_pv, (gi + 1) * NPAIR + 2)
                dve.wait_ge(a_ft, gi) if isinstance(gi, int) and gi else None
                nc.vector.tensor_copy(OT[:, :], PS[:, 6, 0:GW]).then_inc(a_ot, 1)

            FC = 5

            def fin(gi):
                O = PS[:, 7, 0:GW].rearrange("p (t n) -> p t n", n=P)
                k = [gi * FC]

                def chf(ins):
                    ins.then_inc(o_ch, 1)
                    k[0] = k[0] + 1
                    dve.wait_ge(o_ch, k[0])

                dve.wait_ge(a_o, gi + 1)
                dve.wait_ge(a_ft, gi + 1)
                chf(nc.vector.tensor_reduce(orec[:, :], O, AX.X, ALU.add))
                chf(nc.vector.tensor_scalar(orec[:, :], orec[:, :], 1.0 / D, None, ALU.mult))
                chf(nc.vector.reciprocal(orec[:, :], orec[:, :]))
                r = orec[:, :].unsqueeze(2).to_broadcast([P, TPG, P])
                chf(nc.vector.tensor_tensor(ot[:, :, :], O, r, ALU.mult))
                chf(nc.vector.tensor_tensor(ot[:, :, 0:D], ot[:, :, 0:D], ot[:, :, D:P], ALU.add))
                hv = H[:, bass.ds(gi * TPG, TPG), :]
                nc.vector.scalar_tensor_tensor(hv, ot[:, :, 0:D], -1.0, hv, ALU.add, ALU.add).then_inc(a_o, 1)

            def step(b, g, p1, pr, before=True):
                gi = b * NG + g
                if pr is not None:
                    prep(gi + pr, g + pr, b)
                if p1 is not None:
                    maxima(gi + p1, 0, 2)
                if before:
                    fin(gi - 1)
                if p1 is not None:
                    maxima(gi + p1, 2, NG)
                keep(gi)

            for b in range(B):
                gb = b * NG
                maxima(gb)
                prep(gb, 0, b)
                maxima(gb + 1)
                step(b, 0, 2, 1, before=b > 0)
                with dve.Fori(1, NG - 2) as g:
                    step(b, g, 2, 1)
                step(b, NG - 2, None, 1)
                step(b, NG - 1, None, None)
            fin(GT - 1)
            b_dve(dve)
            bo_dve(dve)
            f_dve(dve)
            s_dve(dve)
            g_dve(dve)


def selection(rows, tiles):
    s = np.zeros((3, 8, tiles * P), np.float32)
    for e in range(8):
        s[:, e, e * rows:(e + 1) * rows] = 1.0
    return s.reshape(24, tiles * P)


def f_layout(L, f):
    hid = int(8 / 3 * D)
    tiles = -(-8 * hid // P)
    pad = tiles * P - 8 * hid
    first = 9 - np.arange(1, 9, dtype=np.float32)
    for n in ("w1", "w3"):
        w = f("L0_ffn_" + n).reshape(8 * hid, D).T
        L["f_" + n] = np.tile(np.pad(w, ((0, 0), (0, pad))), (2, 1))
    w2 = np.pad(f("L0_ffn_w2").transpose(0, 2, 1).reshape(8 * hid, D), ((0, pad), (0, 0)))
    L["f_w2"] = w2.reshape(tiles, P, D).transpose(1, 0, 2)
    L["f_sel"] = selection(hid, tiles)
    r = np.concatenate([f("L0_ffn_router_w").T, f("L0_ffn_ln2_w")[:, None], np.tile(first, (D, 1))], axis=1)
    L["f_r"] = np.tile(r, (2, 1))


def _layout(i):
    f = lambda n: np.ascontiguousarray(np.asarray(i[n], dtype=np.float32))
    L = {}
    x = f("x").reshape(B * D, IMG, IMG)
    L["xpad"] = np.pad(x, ((0, 0), (1, 1), (1, 1)))
    w1, w2 = f("L0_tok_conv1_w"), f("L0_tok_conv2_w")
    c1 = np.zeros((B * D, B * CR), np.float32)
    c2 = np.zeros((B * CR, TAPS, B * D), np.float32)
    for b in range(B):
        c1[b * D:(b + 1) * D, b * CR:(b + 1) * CR] = w1.T
        c2[b * CR:(b + 1) * CR, :, b * D:(b + 1) * D] = w2.T[:, :, None]
    L["c1w"], L["c2w"] = c1, c2
    L["bnp"] = np.tile(np.stack([f("L0_tok_conv1_b"), f("L0_tok_bn_gamma"), f("L0_tok_bn_beta"), f("L0_tok_bn_mean"),
                                 f("L0_tok_bn_var")], axis=1), (B, 1))
    L["b2"] = np.tile(f("L0_tok_conv2_b")[None, :], (P, 1))
    L["cls"] = f("cls_tok").reshape(1, D)
    L["qk"] = np.stack([f("L0_attn_Wq"), f("L0_attn_Wk")], axis=1)
    L["ident"] = np.eye(P, dtype=np.float32)
    twice = lambda w: np.tile(w.T, (2, 1))
    L["wqkv"] = np.concatenate([twice(f("L0_ffn_wq")), twice(f("L0_ffn_wk")), twice(f("L0_ffn_wv"))], axis=1)
    L["wo"] = twice(f("L0_ffn_wo"))
    L["lnw"] = np.tile(np.stack([f("L0_ffn_ln1_w"), f("L0_ffn_ln2_w")], axis=1), (2, 1))
    inv = 1.0 / 10000.0 ** (np.arange(0, 16, 2, dtype=np.float32) / 16)
    ang = np.outer(np.arange(NP, dtype=np.float32), inv)
    L["rope"] = np.stack([np.cos(ang), np.sin(ang)]).astype(np.float32).reshape(2, NT, P, 8).transpose(2, 0, 1, 3)
    L["neg"] = np.concatenate([np.zeros((P, 2 * P)), np.triu(np.full((P, P), BIG), 1)], axis=1).astype(np.float32)
    t = (np.arange(TT)[None, :] % NT) * P + np.arange(P)[:, None]
    f_layout(L, f)
    tiles = 8 * F1 // P
    L["g_w1"] = np.tile(f("L1_ffn_w1").transpose(1, 0, 2).reshape(D, 8 * F1), (2, 1))
    L["g_w2"] = f("L1_ffn_w2").reshape(tiles, P, D).transpose(1, 0, 2)
    L["g_b1"] = f("L1_ffn_b1").reshape(tiles, P).T
    L["g_b2"] = np.tile(f("L1_ffn_b2"), (3, 1))
    L["g_bias"] = np.tile(f("L1_ffn_gate_b")[None, :], (P, 1))
    L["g_sel"] = selection(F1, tiles)
    L["g_r"] = np.tile(np.concatenate([f("L1_ffn_gate_w"), np.zeros((D, 1), np.float32),
                                       np.tile(8 - np.arange(8, dtype=np.float32), (D, 1))], axis=1), (2, 1))
    L["upto"] = np.triu(np.ones((P, P), np.float32))
    up = np.repeat([1.0, 0.0], D).astype(np.float32)
    lam = [np.tile(f("L1_attn_" + n), 2) for n in ("Lambda_re", "Lambda_im", "log_step")]
    L["lam"] = np.stack(lam + [up, 1 - up], axis=1)
    L["s_b"] = np.tile(np.stack([f("L1_attn_B_re"), f("L1_attn_B_im")], axis=1), (2, 1, 1))
    cr, ci = f("L1_attn_C_re").T, f("L1_attn_C_im").T
    L["s_c"] = np.stack([np.concatenate([cr, ci]), np.concatenate([ci, cr])], axis=1)
    L["valid"] = (t < N).astype(np.float32)
    return {k: np.ascontiguousarray(v) for k, v in L.items()}


def kernel(**inputs):
    import concourse.bacc as _bacc
    from concourse import mybir as _mybir
    from concourse.bass_utils import run_bass_kernel_spmd as _run

    nc = _bacc.Bacc("TRN2", target_bir_lowering=False, num_devices=1)
    arrays = {"in_" + k: v for k, v in _layout(inputs).items()}
    I = {k[3:]: nc.dram_tensor(k, v.shape, _mybir.dt.from_np(v.dtype), kind="ExternalInput").ap() for k, v in arrays.items()}
    out = nc.dram_tensor("out_h", (B, N, D), _mybir.dt.float32, kind="ExternalOutput").ap()
    tower(nc, I, out)
    r = _run(nc, [arrays], core_ids=[0])
    return r.results[0]["out_h"]
```

```python
from contextlib import ExitStack

import numpy as np

import concourse.bass as bass
from concourse import mybir

F32 = mybir.dt.float32
BF16 = mybir.dt.bfloat16
ALU = mybir.AluOpType
ACT = mybir.ActivationFunctionType
AX = mybir.AxisListType

P = 128
B = 2
D = 64
IMG = 64
TAPS = 9
CR = 16
N = IMG * IMG + 1
TPG = 3
GW = TPG * P
NG = -(-N // GW)
NT = NG * TPG
NP = NT * P
GT = B * NG
TT = B * NT
TOK = B * NP
EPS = 1e-5
BIG = -1e30
F1 = 256


class Stage:
    pass


def tower(nc, I, out):
    ctx = ExitStack()
    with ctx:
        def sb(name, shape, dt=F32):
            return ctx.enter_context(nc.sbuf_tensor(name, shape, dt))

        def sem(name):
            return ctx.enter_context(nc.semaphore(name))

        scratch = nc.dram_tensor("tokens_scratch", (B, IMG * IMG, D), F32, kind="Internal").ap()

        PS = ctx.enter_context(nc.psum_tensor("PS", [P, 8, 512], F32))

        def bank16(k):
            return PS[:, k, :].bitcast(BF16)

        H = sb("H", [P, TT, D])
        XN = sb("XN", [P, TT, D])
        stat = sb("stat", [P, 4, TT])
        A0 = sb("A0", [P, TT * 256], BF16)
        A1 = sb("A1", [P, 2 * TOK], BF16)
        A2 = sb("A2", [P, 2 * TOK], BF16)
        A3 = sb("A3", [P, TT * 65])
        A4 = sb("A4", [P, TT * D])
        ident = sb("ident", [P, P])
        ident16 = sb("ident16", [P, P], BF16)
        valid = sb("valid", [P, TT])
        epsc = sb("epsc", [P, 2])

        xstr = A0[:, :].rearrange("p (t n) -> p t n", n=256)
        W = A1[:, :].rearrange("p (w n) -> p w n", w=2)

        A5 = sb("A5", [P, 4 * NP], BF16)

        def places(arena, start):
            at = [start]

            def place(shape, dt=F32):
                n = int(np.prod(shape[1:])) * (2 if dt is F32 else 1)
                at[0] += at[0] % 2
                v = arena[0:shape[0], at[0]:at[0] + n]
                at[0] += n
                assert at[0] <= arena.shape[1], (at[0], arena.shape)
                v = v.bitcast(F32) if dt is F32 else v
                names = "abcd"[:len(shape) - 1]
                if len(shape) > 2:
                    v = v.rearrange("p (%s) -> p %s" % (" ".join(names), " ".join(names)), **dict(zip(names[1:], shape[2:])))
                return v
            return place

        early = places(A5, 0)
        n_ln = [0]
        n_pool = [0]
        p_ch = sem("pool_chain")

        c_in = sem("constants_loaded")
        c_id = sem("ident16_ready")

        block = ctx.enter_context(nc.Block())

        x_pad = A1[:, 0:2 * 66 * 66].bitcast(F32).rearrange("p (h w) -> p h w", w=66)
        conv = A2[:, 0:2 * IMG * IMG].bitcast(F32)
        c1w = early([P, B * CR])
        bnp = early([B * CR, 5])
        bns = early([B * CR, 4])
        c2w = A3[0:B * CR, 0:TAPS * P].rearrange("p (k n) -> p k n", k=TAPS)
        b2 = early([P, TAPS])
        yv = early([B * CR, 2, 512])
        tapp = early([P, 3, 512])
        t_in = sem("conv_inputs_loaded")
        t_std = sem("bn_std")
        t_bn = sem("bn_folded")
        t_ch = sem("bn_chain")
        t_y = sem("conv1_product")
        t_ys = sem("conv1_relu")
        t_w = sem("dynamic_weights")
        t_p = sem("tap_product")
        t_a = sem("tap_added")
        t_out = sem("conv_stored")
        h_in = sem("tokens_loaded")

        RG = 8
        SLOT = 3

        ln_ch = sem("vector_chain")
        ln_var = sem("ln_variance")
        ln_std = sem("ln_std")
        x_str = sem("x_strings")
        x_t = sem("x_transposed")
        x_w = sem("x_stacks")

        qk2 = early([D, 2, D])
        qkc = early([D, 2, P])
        qks = early([D, 2])
        MS = early([P, 3, D], BF16)
        mres = early([P, D])
        VA = A3[:, 0:TT * D].rearrange("p (t n) -> p t n", n=D)
        Q2 = A4[:, :].rearrange("p (t n) -> p t n", n=D)
        QP = A2[:, :].rearrange("p (w n) -> p w n", w=2)
        QT = A0[:, 0:3 * NP].rearrange("p (w n) -> p w n", w=3)
        MX = early([P, TPG, NG])
        mm = early([P, 2, TPG])
        qtm = early([P, TPG, D])
        QTS = early([P, TPG, 5, D], BF16)
        PT = early([P, 6, GW])
        VS = early([P, 6, D])
        OT = sb("OT", [P, GW])
        NPAIR = (NT + 1) // 2
        orec = early([P, TPG])
        ot = early([P, TPG, P])
        a_m = sem("a_projection_matrix")
        a_ms = sem("a_projection_stacks")
        a_ch = sem("a_chain")
        a_q = sem("a_queries_product")
        a_qe = sem("a_queries_kept")
        a_qstr = sem("a_query_strings")
        a_qpt = sem("a_query_transposed")
        a_qp = sem("a_query_stacks")
        a_s1 = sem("a_max_scores")
        a_s1f = sem("a_max_scores_read")
        a_str = sem("a_shifted_strings")
        a_tq = sem("a_shifted_transposed")
        a_qt = sem("a_shifted_stacks")
        a_s2 = sem("a_scores")
        a_ex = sem("a_exponentials")
        a_pv = sem("a_value_products")
        a_vs = sem("a_values_staged")
        a_ot = sem("a_output_kept")
        a_ft = sem("a_output_transposed")
        a_o = sem("a_output_added")
        a_pc = sem("a_prep_chain")
        o_out = sem("output_stored")
        o_ch = sem("a_output_chain")

        QR = TT // 3

        def b3(ap, n):
            return ap.unsqueeze(2).to_broadcast([P, ap.shape[1], n])

        CHUNKS = [(0, 4), (4, 8), (8, GT // 2)]
        NCH = len(CHUNKS)

        def transposes(pe, c, ready, done, freed, strings=None):
            pe.wait_ge(ready, c + 1)
            pe.wait_ge(c_id, 1)
            with pe.Fori(*CHUNKS[c]) as i:
                for h in range(2):
                    pe.wait_ge(freed, i * 2 + h + 1)
                    for w in range(2):
                        for u in range(TPG):
                            ins = nc.tensor.transpose(bank16(6 + h)[:, (w * TPG + u) * P:(w * TPG + u + 1) * P],
                                                      (xstr if strings is None else strings)[:, bass.ds((i * 2 + h) * TPG + u, 1), w * P:(w + 1) * P],
                                                      ident16[:, :])
                    ins.then_inc(done, 1)

        def stack_copies(act, c, done, freed, dst):
            if c == 0:
                act.sem_inc(freed, 2)
            with act.Fori(*CHUNKS[c]) as i:
                for h in range(2):
                    act.wait_ge(done, i * 2 + h + 1)
                    nc.scalar.copy(dst[:, :, bass.ds((i * 2 + h) * GW, GW)],
                                   bank16(6 + h)[:, 0:2 * GW].rearrange("p (w n) -> p w n", w=2)).then_inc(freed, 1)

        def link(e, s, count, ins):
            count[0] += 1
            ins.then_inc(s, 1)
            e.wait_ge(s, count[0])

        def layer_norm(dve, count, ready):
            ch = lambda ins: link(dve, ln_ch, count, ins)
            ch(nc.vector.tensor_reduce(stat[:, 0, :], H[:, :, :], AX.X, ALU.add))
            ch(nc.vector.tensor_scalar(stat[:, 0, :], stat[:, 0, :], -1.0 / D, None, ALU.mult))
            ch(nc.vector.tensor_tensor(XN[:, :, :], H[:, :, :], b3(stat[:, 0, :], D), ALU.add))
            ch(nc.vector.tensor_tensor(Q2, XN[:, :, :], XN[:, :, :], ALU.mult))
            nc.vector.tensor_reduce(stat[:, 1, :], Q2, AX.X, ALU.add).then_inc(ready, 1)

        def split_x(dve, count, src, res, ready, strings=None, first=None):
            ch = lambda ins: link(dve, ln_ch, count, ins)
            for c, (lo, hi) in enumerate(CHUNKS):
                tl = slice(2 * TPG * lo, 2 * TPG * hi)
                if first is not None:
                    first(ch, tl)
                s = (xstr if strings is None else strings).rearrange("p t (a n) -> p t a n", n=D)[:, tl, :, :]
                x, r = src[:, tl, :], res[:, tl, :]
                ch(nc.vector.tensor_copy(s[:, :, 0, :], x))
                ch(nc.vector.tensor_copy(s[:, :, 3, :], s[:, :, 0, :]))
                ch(nc.vector.tensor_tensor(r, x, s[:, :, 0, :], ALU.subtract))
                ch(nc.vector.tensor_copy(s[:, :, 1, :], r))
                ch(nc.vector.tensor_tensor(r, r, s[:, :, 1, :], ALU.subtract))
                nc.vector.tensor_copy(s[:, :, 2, :], r).then_inc(ready, 1)
                dve.wait_ge(ready, c + 1)

        def normed(ch, tl):
            x = XN[:, tl, :]
            ch(nc.vector.tensor_tensor(x, x, b3(stat[:, 3, tl], D), ALU.mult))

        def rms(ch, tl):
            ch(nc.vector.tensor_tensor(Q2[:, tl, :], XN[:, tl, :], b3(stat[:, 3, tl], D), ALU.mult))

        def split_w(dve, s, count, w, st, ready, value):
            ch = lambda ins: link(dve, s, count, ins)
            ch(nc.vector.tensor_copy(st[:, 0, :], w))
            ch(nc.vector.tensor_copy(st[0:D, 1, :], st[0:D, 0, :]))
            ch(nc.vector.tensor_tensor(w, w, st[:, 0, :], ALU.subtract))
            ch(nc.vector.tensor_copy(st[:, 2, :], w))
            ch(nc.vector.tensor_tensor(w, w, st[:, 2, :], ALU.subtract))
            nc.vector.tensor_copy(st[D:P, 1, :], w[D:P, :]).then_inc(ready, 1)
            dve.wait_ge(ready, value)

        def project(pe, c, stacks, n, done, freed):
            with pe.Fori(*CHUNKS[c]) as i:
                for h in range(2):
                    pe.wait_ge(freed, i * 2 + h + 1)
                    for u in range(TPG):
                        tile = bass.ds((i * 2 + h) * GW + u * P, P)
                        for k, w in enumerate((0, 1, 0)):
                            ins = nc.tensor.matmul(PS[:, 4 + h, u * n:(u + 1) * n], W[:, w, tile], stacks[:, k, :],
                                                   start=(k == 0), stop=(k == 2))
                    ins.then_inc(done, 1)

        def project_copies(act, c, n, done, freed, dst):
            if c == 0:
                act.sem_inc(freed, 2)
            with act.Fori(*CHUNKS[c]) as i:
                for h in range(2):
                    act.wait_ge(done, i * 2 + h + 1)
                    nc.scalar.copy(dst[:, bass.ds((i * 2 + h) * TPG, TPG), :],
                                   PS[:, 4 + h, 0:TPG * n].rearrange("p (t n) -> p t n", n=n)).then_inc(freed, 1)

        def prepare_pe(pe, ready, t, kept, weights, stacks, n, done, freed, strings=None):
            for c, (lo, hi) in enumerate(CHUNKS):
                transposes(pe, c, ready, t, kept, strings)
                pe.wait_ge(kept, 2 * hi + 2)
                if c == 0:
                    pe.wait_ge(*weights)
                project(pe, c, stacks, n, done, freed)

        def prepare_act(act, t, kept, n, done, freed, dst):
            for c in range(NCH):
                stack_copies(act, c, t, kept, W)
                if dst is not None:
                    project_copies(act, c, n, done, freed, dst)


        NH, NKV, HD = 4, 2, 16
        PARTS = 6
        KR = PARTS * HD
        HH = HD // 2
        UN = TPG * NH
        QKV = A2[:, :].bitcast(F32).rearrange("p (t n) -> p t n", n=P)
        late = places(A3[:, :].bitcast(BF16), 2 * TT * NKV * (HD + 1))
        QB = [A5[:, :].rearrange("p (h n) -> p h n", h=NH), A2[:, :].rearrange("p (h n) -> p h n", h=NH)]
        KB = A1[:, :].rearrange("p (h n) -> p h n", h=NKV)
        qs_ = A0[:, 0:NT * NH * KR].rearrange("p (x a n) -> p x a n", a=PARTS, n=HD)
        ks_ = A4[:, :].bitcast(BF16)[:, 0:NT * NKV * KR].rearrange("p (x a n) -> p x a n", a=PARTS, n=HD)
        def head_steps(b, g):
            if b == 0:
                return [(c, g * 3 + c) for c in range(3)]
            return [(0, NG * 3 + g * 2), (2, NG * 3 + g * 2 + 1)]

        last_steps = NG * 5
        HCH = [(g, min(g + 3, NG)) for g in range(0, NG, 3)]
        rt = A0[:, NT * NH * KR:NT * NH * KR + 8 * 9 * 48].bitcast(F32).rearrange("p (k t h n) -> p k t h n", k=4, t=9, n=HH)
        VB = A3[:, 0:TT * NKV * (HD + 1)].rearrange("p (t h n) -> p t h n", h=NKV, n=HD + 1)
        YB = A4[:, :].rearrange("p (t n) -> p t n", n=D)
        wf = late([P, P])
        lnw = late([P, 2])
        wqkv = late([P, 3, P], BF16)
        wof = late([P, D])
        wos = late([P, 3, D], BF16)
        cs = late([P, 2, NT, HH])
        neg = late([P, P])
        neg16 = late([P, P], BF16)
        MXB = late([P, UN, NG])
        mB = late([P, UN])
        mstr = late([P, UN, 3], BF16)
        MT = late([UN, GW], BF16)
        PB = A0[:, 0:2 * UN * GW].bitcast(F32).rearrange("p (k n) -> p k n", k=UN)
        VSB = sb("VSB", [P, TPG, NKV, HD + 1])
        obr = sb("obr", [P, TPG, NH])
        b_ystr = sem("b_output_strings")
        b_in = sem("b_weights_loaded")
        b_var = sem("b_square_sums")
        b_std = sem("b_rms")
        b_w = sem("b_weight_stacks")
        b_str = sem("b_strings")
        b_t = sem("b_transposed")
        b_st = sem("b_stacks")
        b_q = sem("b_qkv_product")
        b_qe = sem("b_qkv_kept")
        b_hs = sem("b_head_strings")
        b_ht = sem("b_heads_transposed")
        b_hk = sem("b_head_stacks")
        b_one = sem("b_ones_rows")
        b_s1 = sem("b_max_scores")
        b_s1f = sem("b_max_scores_read")
        b_s2 = sem("b_scores")
        b_ex = sem("b_exponentials")
        b_sel = sem("b_causal_selected")
        b_pv = sem("b_value_products")
        b_vs = sem("b_values_staged")
        b_ot = sem("b_output_kept")
        b_ft = sem("b_output_transposed_back")
        b_o = sem("b_output_scaled")
        b_oc = sem("b_output_chain")
        b_ms = sem("b_maximum_strings")
        b_mt = sem("b_maxima_transposed")
        b_mc = sem("b_maxima_copied")
        b_mr = sem("b_maximum_rows")

        order = [(0, g) for g in range(NG)] + [(1, g) for g in reversed(range(NG))]
        before = [UN * sum(g + 1 for _, g in order[:i]) for i in range(GT + 1)]
        LAG = 2

        def b_sp(sp):
            sp.wait_ge(a_o, GT + 1)
            sp.dma_start(wf[:, :], I["wqkv"]).then_inc(b_in, 16)
            sp.dma_start(wof[:, :], I["wo"]).then_inc(b_in, 16)
            sp.dma_start(lnw[:, :], I["lnw"]).then_inc(b_in, 16)
            sp.dma_start(cs[:, :, :, :], I["rope"]).then_inc(b_in, 16)
            sp.dma_start(neg[:, :], I["neg"]).then_inc(b_in, 16)

        def b_sp_rows(sp):
            for i, (b, g) in enumerate(order):
                sp.wait_ge(b_mc, i + 1)
                for h in range(NH):
                    sp.dma_start(QB[b][KR:KR + 3, h, g * GW:(g + 1) * GW], MT[3 * h:3 * h + 3, :]).then_inc(b_mr, 16)

        def b_pe(pe):
            pe.wait_ge(a_o, GT + 1)
            prepare_pe(pe, b_str, b_t, b_st, (b_w, 1), wqkv, P, b_q, b_qe)
            def heads(b, g, c, n, bank):
                pe.wait_ge(b_hk, n + 1)
                for y in range(2):
                    for u in range(TPG):
                        if c < 2:
                            src = qs_[:, bass.ds(g * UN + u * NH + 2 * c + y, 1), :, :]
                        else:
                            src = ks_[:, bass.ds(g * TPG * NKV + u * NKV + y, 1), :, :]
                        ins = nc.tensor.transpose(bank16(bank)[0:KR, (y * TPG + u) * P:(y * TPG + u + 1) * P],
                                                  src.rearrange("p x a n -> p (x a n)"), ident16[:, :])
                ins.then_inc(b_ht, 1)

            pe.wait_ge(b_qe, GT + 2)
            for b in range(B):
                for k, (lo, hi) in enumerate(HCH):
                    pe.wait_ge(b_hs, b * len(HCH) + k + 1)
                    with pe.Fori(lo, hi) as g:
                        for c, n in head_steps(b, g):
                            heads(b, g, c, n, c)
            for g in range(NG):
                heads(1, g, 1, last_steps + g, 1 - g % 2)
            pe.wait_ge(b_hk, B * NG * 3 + 2)
            pe.wait_ge(b_one, 2)
            pe.sem_inc(b_pv, 3)

            def qk(b, g, j, h, lo, k, n2):
                pe.wait_ge(b_ex, n2 + 1)
                nc.tensor.matmul(PS[:, k % 3, lo:GW], KB[0:KR + 3, h // 2, bass.ds(b * NP + j * P, P)],
                                 QB[b][0:KR + 3, h, g * GW + lo:(g + 1) * GW], start=True, stop=True).then_inc(b_s2, 1)

            def mx(b, g, a, h, key, width, k, n1):
                pe.wait_ge(b_s1f, n1 + 1)
                nc.tensor.matmul(PS[:, 3 + k % 3, 0:width], QB[b][0:KR, h, (g * TPG + a) * P:(g * TPG + a + 1) * P],
                                 KB[0:KR, h // 2, bass.ds(b * NP + key, width)], start=True, stop=True).then_inc(b_s1, 1)

            def triple(i, m, jj, first):
                b, g = order[i]
                n2 = before[i] + jj * UN
                q0 = before[i] // NH + jj * TPG
                for k in range(UN):
                    qk(b, g, jj * TPG + k // NH, k % NH, 0, k, n2 + k)
                    if m is not None:
                        mx(*order[m], k // NH, k % NH, jj * GW, GW, k, before[m] + jj * UN + k)
                    if k == 1 and not first:
                        pvq(n2 - UN, q0 - TPG, 2, 0, False)
                    if k == 5 and first:
                        pe.wait_ge(b_ot, i + 1)
                    if k in (5, 9):
                        pvq(n2, q0, k // NH - 1, 0, first and k == 5)

            def pvq(n2, q0, u, lo, first, sel=0):
                pe.wait_ge(b_ex, n2 + 4 * u + 4 + 3)
                pe.wait_ge(b_vs, q0 + u + 1)
                if sel:
                    pe.wait_ge(b_sel, sel)
                for h in range(NH):
                    ins = nc.tensor.matmul(PS[32 * h:32 * h + HD + 1, 6, lo:GW], VSB[:, u, h // 2, :], PB[:, NH * u + h, lo:GW],
                                           start=first, stop=True, skip_group_check=True)
                ins.then_inc(b_pv, 1)

            def maxima(m, lo, hi):
                if hi > lo:
                    with pe.Fori(lo, hi) as jj:
                        for k in range(UN):
                            mx(*order[m], k // NH, k % NH, jj * GW, GW, k, before[m] + jj * UN + k)

            def diagonal(i, m):
                for k in range(UN + 4):
                    u = k // NH
                    if k < UN and i is not None:
                        b, g = order[i]
                        qk(b, g, g * TPG + u, k % NH, u * P, k, before[i] + g * UN + k)
                    if k < UN and m is not None:
                        b, g = order[m]
                        n1, kh = before[m] + g * UN + k, k % NH // 2
                        tile = g * TPG + u
                        pe.wait_ge(b_s1f, n1 + 1)
                        nc.tensor.matmul(PS[:, 3 + k % 3, 0:(u + 1) * P], QB[b][0:KR, k % NH, tile * P:(tile + 1) * P],
                                         KB[0:KR, kh, b * NP + g * GW:b * NP + g * GW + (u + 1) * P],
                                         start=True, stop=True, skip_group_check=True)
                        nc.tensor.matmul(PS[:, 3 + k % 3, u * P:(u + 1) * P], ident16[:, :], neg16[:, :],
                                         start=False, stop=True, skip_group_check=True).then_inc(b_s1, 1)
                    if k in (5, 9, 13) and i is not None:
                        b, g = order[i]
                        u = k // NH - 1
                        if g == 0 and u == 0:
                            pe.wait_ge(b_ot, i + 1)
                        pvq(before[i] + g * UN, before[i] // NH + g * TPG, u, u * P, g == 0 and u == 0, i * UN + 4 * u + 4)

            def fin(i):
                pe.wait_ge(b_ot, i + 2)
                for a in range(TPG):
                    ins = nc.tensor.transpose(PS[:, 7, a * P:(a + 1) * P], OT[:, a * P:(a + 1) * P], ident[:, :])
                ins.then_inc(b_ft, 1)

            def prep(i):
                pe.wait_ge(b_ms, i + 1)
                if i:
                    pe.wait_ge(b_mc, i)
                if i > 1:
                    pe.wait_ge(b_o, i - 1)
                for a in range(TPG):
                    ins = nc.tensor.transpose(bank16(7)[0:UN, a * P:(a + 1) * P],
                                              mstr[:, a * NH:(a + 1) * NH, :].rearrange("p h n -> p (h n)"), ident16[:, :])
                ins.then_inc(b_mt, 1)

            diagonal(None, 0)
            prep(0)
            maxima(1, 0, order[1][1])
            diagonal(None, 1)
            for i, (b, g) in enumerate(order):
                m = i + LAG if i + LAG < GT else None
                gm = order[m][1] if m is not None else 0
                both = min(g, gm)
                pe.wait_ge(b_mr, 64 * (i + 1))
                if g:
                    triple(i, m if both else None, 0, True)
                if i:
                    fin(i - 1)
                if both > 1:
                    with pe.Fori(1, both) as jj:
                        triple(i, m, jj, False)
                if g > max(both, 1):
                    with pe.Fori(max(both, 1), g) as jj:
                        triple(i, None, jj, False)
                if g:
                    pvq(before[i] + (g - 1) * UN, before[i] // NH + (g - 1) * TPG, 2, 0, False)
                if i + 1 < GT:
                    prep(i + 1)
                if m is not None:
                    maxima(m, both, gm)
                diagonal(i, m)
            fin(GT - 1)

        def b_act(act):
            act.wait_ge(b_var, 1)
            nc.scalar.activation(stat[:, 2, :], stat[:, 1, :], ACT.Sqrt, bias=epsc[:, 1:2], scale=1.0 / D).then_inc(b_std, 1)
            prepare_act(act, b_t, b_st, P, b_q, b_qe, QKV)
            act.sem_inc(b_hk, 2)
            def heads(b, g, c, n, bank):
                act.wait_ge(b_ht, n + 1)
                if c < 2:
                    dst = QB[b][0:KR, 2 * c:2 * c + 2, bass.ds(g * GW, GW)]
                else:
                    dst = KB[0:KR, :, bass.ds(b * NP + g * GW, GW)]
                nc.scalar.copy(dst, bank16(bank)[0:KR, 0:2 * GW].rearrange("p (h n) -> p h n", h=2)).then_inc(b_hk, 1)

            for b in range(B):
                for lo, hi in HCH:
                    with act.Fori(lo, hi) as g:
                        for c, n in head_steps(b, g):
                            heads(b, g, c, n, c)
            for g in range(NG):
                heads(1, g, 1, last_steps + g, 1 - g % 2)
            act.sem_inc(b_ex, 3)

            def exps(n2, q0, lo=0):
                for k in range(UN):
                    act.wait_ge(b_s2, n2 + k + 1)
                    if k % NH == 0:
                        act.wait_ge(b_pv, q0 + k // NH + 1)
                    c = k // NH * P if lo else 0
                    nc.scalar.activation(PB[:, k, c:GW], PS[:, k % 3, c:GW], ACT.Exp).then_inc(b_ex, 1)

            def prep(i):
                act.wait_ge(b_mt, i + 1)
                if i:
                    act.wait_ge(b_mr, 64 * i)
                nc.scalar.copy(MT[:, :], bank16(7)[0:UN, 0:GW]).then_inc(b_mc, 1)

            prep(0)
            for i, (b, g) in enumerate(order):
                if g:
                    with act.Fori(0, g) as jj:
                        exps(before[i] + jj * UN, before[i] // NH + jj * TPG)
                if i + 1 < GT:
                    prep(i + 1)
                exps(before[i] + g * UN, before[i] // NH + g * TPG, 1)

        def b_pool(pool):
            pool.wait_ge(b_qe, GT + 2)
            nc.gpsimd.memset(KB[96:99, 0, :], 1.0).then_inc(b_one, 1)
            nc.gpsimd.memset(KB[96:99, 1, :], 1.0).then_inc(b_one, 1)

            def stage(b, j, u, q):
                pool.wait_ge(b_one, 2)
                pool.wait_ge(b_pv, q + u + 1)
                nc.gpsimd.tensor_copy(VSB[:, u:u + 1, :, :], VB[:, bass.ds(b * NT + j + u, 1), :, :]).then_inc(b_vs, 1)

            for i, (b, g) in enumerate(order):
                q0 = before[i] // NH
                if g:
                    with pool.Fori(0, g) as jj:
                        for u in range(TPG):
                            stage(b, jj * TPG, u, q0 + jj * TPG)
                for k in range(UN):
                    if k % NH == 0:
                        stage(b, g * TPG, k // NH, q0 + g * TPG)
                    pool.wait_ge(b_ex, before[i] + g * UN + k + 4)
                    c = k // NH * P
                    v = PB[:, k, c:c + P]
                    nc.gpsimd.affine_select(out=v, in_=v, compare_op=ALU.is_ge, fill=0.0, base=0,
                                            pattern=[[1, P]], channel_multiplier=-1).then_inc(b_sel, 1)

        def b_dve(dve):
            dve.wait_ge(a_o, GT + 1)
            dve.wait_ge(b_in, 5 * 16)
            ch = lambda ins: link(dve, ln_ch, n_ln, ins)
            ch(nc.vector.tensor_copy(neg16[:, :], neg[:, :]))
            ch(nc.vector.tensor_scalar(wf[:, :], wf[:, :], lnw[:, 0:1], None, ALU.mult))
            ch(nc.vector.tensor_scalar(wf[:, 0:D], wf[:, 0:D], float(HD) ** -0.5, None, ALU.mult))
            split_w(dve, ln_ch, n_ln, wf[:, :], wqkv, b_w, 1)
            split_w(dve, ln_ch, n_ln, wof[:, :], wos, b_w, 2)
            layer_norm(dve, n_ln, ln_var)
            dve.wait_ge(ln_std, 2)
            ch(nc.vector.reciprocal(stat[:, 3, :], stat[:, 2, :]))
            normed(ch, slice(0, TT))
            ch(nc.vector.tensor_tensor(Q2, XN[:, :, :], XN[:, :, :], ALU.mult))
            nc.vector.tensor_reduce(stat[:, 1, :], Q2, AX.X, ALU.add).then_inc(b_var, 1)
            dve.wait_ge(b_std, 1)
            ch(nc.vector.reciprocal(stat[:, 3, :], stat[:, 2, :]))
            split_x(dve, n_ln, Q2, Q2, b_str, None, rms)
            ch = lambda ins: link(dve, ln_ch, n_ln, ins)
            ch(nc.vector.memset(VB[:, :, :, :], 1.0))
            dve.wait_ge(b_st, GT + 2)
            for b in range(B):
                dve.wait_ge(b_qe, (b + 1) * NG + 2)
                tb = slice(b * NT, (b + 1) * NT)
                ch(nc.vector.tensor_copy(VB[:, tb, :, 0:HD], QKV[:, tb, 96:128].rearrange("p t (h n) -> p t h n", h=NKV)))
                for c, (g0, g1) in enumerate(HCH):
                    if b:
                        dve.wait_ge(b_hk, g1 * 3 + 2)
                    t0, t1 = g0 * TPG, g1 * TPG
                    n = t1 - t0
                    v = QKV[:, b * NT + t0:b * NT + t1, 0:96].rearrange("p t (h c n) -> p t h c n", c=2, n=HH)
                    lo, hi = v[:, :, :, 0, :], v[:, :, :, 1, :]
                    co = cs[:, 0, t0:t1, :].unsqueeze(2).to_broadcast([P, n, NH + NKV, HH])
                    si = cs[:, 1, t0:t1, :].unsqueeze(2).to_broadcast([P, n, NH + NKV, HH])
                    ch(nc.vector.tensor_tensor(rt[:, 0, 0:n, :, :], lo, co, ALU.mult))
                    ch(nc.vector.tensor_tensor(rt[:, 1, 0:n, :, :], hi, si, ALU.mult))
                    ch(nc.vector.tensor_tensor(rt[:, 2, 0:n, :, :], hi, co, ALU.mult))
                    ch(nc.vector.tensor_tensor(rt[:, 3, 0:n, :, :], lo, si, ALU.mult))
                    ch(nc.vector.tensor_tensor(lo, rt[:, 0, 0:n, :, :], rt[:, 1, 0:n, :, :], ALU.subtract))
                    ch(nc.vector.tensor_tensor(hi, rt[:, 2, 0:n, :, :], rt[:, 3, 0:n, :, :], ALU.add))
                    for z, (all_, c0, nh, where) in enumerate(((qs_, 0, NH, ((0, 1, 2), (3, 4), (5,))),
                                                               (ks_, D, NKV, ((0, 3, 5), (1, 4), (2,))))):
                        st = all_[:, t0 * nh:t1 * nh, :, :]
                        x = QKV[:, b * NT + t0:b * NT + t1, c0:c0 + nh * HD].rearrange("p t (h n) -> p t h n", n=HD)
                        for part, at in enumerate(where):
                            first = st[:, :, at[0], :].rearrange("p (t h) n -> p t h n", h=nh)
                            ins = nc.vector.tensor_copy(first, x)
                            if z == 1 and part == 2:
                                ins.then_inc(b_hs, 1)
                                dve.wait_ge(b_hs, b * len(HCH) + c + 1)
                            else:
                                ch(ins)
                            for k in at[1:]:
                                ch(nc.vector.tensor_copy(st[:, :, k, :], st[:, :, at[0], :]))
                            if part < 2:
                                ch(nc.vector.tensor_tensor(x, x, first, ALU.subtract))
            dve.wait_ge(b_hk, B * NG * 3 + 2)
            dve.sem_inc(b_s1f, 3)
            dve.sem_inc(b_ot, 1)

            def reduce_max(m, k, at, n1, width):
                dve.wait_ge(b_s1, n1 + k + 1)
                nc.vector.tensor_reduce(MXB[:, k, at], PS[:, 3 + k % 3, 0:width], AX.X, ALU.max).then_inc(b_s1f, 1)

            def maxima(m, lo, hi):
                if hi > lo:
                    with dve.Fori(lo, hi) as jj:
                        for k in range(UN):
                            reduce_max(m, k, bass.ds(jj, 1), before[m] + jj * UN, GW)

            def diagonal(m):
                g = order[m][1]
                for k in range(UN):
                    reduce_max(m, k, slice(g, g + 1), before[m] + g * UN, (k // NH + 1) * P)

            def prep(i):
                g = order[i][1]
                chp = lambda ins: link(dve, ln_ch, n_ln, ins)
                dve.wait_ge(b_s1f, before[i + 1] + 3)
                chp(nc.vector.tensor_reduce(mB[:, :], MXB[:, :, 0:g + 1], AX.X, ALU.max, negate=True))
                if i:
                    dve.wait_ge(b_mt, i)
                chp(nc.vector.tensor_copy(mstr[:, :, 0], mB[:, :]))
                chp(nc.vector.tensor_tensor(mB[:, :], mB[:, :], mstr[:, :, 0], ALU.subtract))
                chp(nc.vector.tensor_copy(mstr[:, :, 1], mB[:, :]))
                chp(nc.vector.tensor_tensor(mB[:, :], mB[:, :], mstr[:, :, 1], ALU.subtract))
                nc.vector.tensor_copy(mstr[:, :, 2], mB[:, :]).then_inc(b_ms, 1)
                dve.wait_ge(b_ms, i + 1)

            def keep(i):
                dve.wait_ge(b_pv, before[i + 1] // NH + 3)
                for h in range(NH):
                    ins = nc.vector.tensor_copy(OT[32 * h:32 * h + HD + 1, :], PS[32 * h:32 * h + HD + 1, 6, 0:GW])
                ins.then_inc(b_ot, 1)

            def fin(i):
                b, g = order[i]
                t = (b * NG + g) * TPG
                O = PS[:, 7, 0:GW].rearrange("p (t h n) -> p t h n", h=NH, n=32)
                dve.wait_ge(b_ft, i + 1)
                nc.vector.reciprocal(obr[:, :, :], O[:, :, :, HD]).then_inc(b_oc, 1)
                dve.wait_ge(b_oc, i + 1)
                nc.vector.tensor_tensor(YB[:, t:t + TPG, :].rearrange("p t (h n) -> p t h n", h=NH), O[:, :, :, 0:HD],
                                        obr[:, :, :].unsqueeze(3).to_broadcast([P, TPG, NH, HD]), ALU.mult).then_inc(b_o, 1)
                dve.wait_ge(b_o, i + 1)

            diagonal(0)
            prep(0)
            maxima(1, 0, order[1][1])
            diagonal(1)
            for i, (b, g) in enumerate(order):
                m = i + LAG if i + LAG < GT else None
                gm = order[m][1] if m is not None else 0
                ahead = min(g, gm, 1)
                if i + 1 < GT:
                    prep(i + 1)
                if m is not None:
                    maxima(m, 0, ahead)
                if i:
                    fin(i - 1)
                if m is not None:
                    maxima(m, ahead, gm)
                    diagonal(m)
                keep(i)
            fin(GT - 1)
            split_x(dve, n_ln, YB, YB, b_ystr)


        b_yt = sem("b_output_transposed")
        b_yst = sem("b_output_stacks")
        b_yp = sem("b_output_product")
        b_yk = sem("b_output_added")

        def bo_pe(pe):
            prepare_pe(pe, b_ystr, b_yt, b_yst, (b_w, 2), wos, D, b_yp, b_yk)

        def bo_act(act):
            prepare_act(act, b_yt, b_yst, D, None, None, None)

        def bo_dve(dve):
            dve.sem_inc(b_yk, 2)
            with dve.Fori(0, GT // 2) as i:
                for h in range(2):
                    dve.wait_ge(b_yp, i * 2 + h + 1)
                    x = XN[:, bass.ds((i * 2 + h) * TPG, TPG), :]
                    nc.vector.tensor_tensor(x, PS[:, 4 + h, 0:TPG * D].rearrange("p (t n) -> p t n", n=D), x,
                                            ALU.add).then_inc(b_yk, 1)
            dve.wait_ge(b_yk, GT + 2)

        NE = 8
        WR = 3 * NE
        RN = 8
        S2 = A2[:, :].rearrange("p (t n) -> p t n", n=256)

        def experts(tag, HT, ring, gated, place_w, place_r, place_t, hh, raw):
            m = Stage()
            m.HT, m.ring, m.gated, m.hh = HT, ring, gated, hh
            m.PP, m.CR = (HT + 1) // 2, (ring + 1) // 2
            m.inp = sem(tag + "_weights_loaded")
            m.raw_in = sem(tag + "_selection_loaded")
            m.wst = sem(tag + "_weight_stacks")
            m.rsp = sem(tag + "_router_stacks")
            m.str = sem(tag + "_strings")
            m.xt = sem(tag + "_transposed")
            m.xw = sem(tag + "_stacks")
            m.lp = sem(tag + "_logits_product")
            m.lk = sem(tag + "_logits_kept")
            m.sh = sem(tag + "_logits_shifted")
            m.ex = sem(tag + "_logits_exponentials")
            m.ws = sem(tag + "_token_weight_strings")
            m.wt = sem(tag + "_token_weights_transposed")
            m.wk = sem(tag + "_token_weights_kept")
            m.a = sem(tag + "_hidden_product")
            m.b = sem(tag + "_hidden_second_product")
            m.s = sem(tag + "_hidden_activated")
            m.tc = sem(tag + "_hidden_chain")
            m.h = sem(tag + "_hidden_ready")
            m.o = sem(tag + "_output_products")
            m.ot = sem(tag + "_output_kept")
            m.ft = sem(tag + "_output_transposed")
            m.fc = sem(tag + "_output_chain")
            m.add = sem(tag + "_output_added")
            m.done = sem(tag + "_finished")
            m.w1 = place_w([P, 3, HT * P], BF16)
            m.w3 = place_w([P, 3, HT * P], BF16) if gated else None
            m.raw1 = raw or place_w([P, HT * P])
            m.raw3 = place_w([P, HT * P]) if gated else None
            m.w2 = place_w([P, HT, D])
            m.sel = place_w([WR, HT * P], BF16)
            m.rst = place_r([P, 3, RN], BF16)
            m.rw = sb(tag + "_router", [P, RN + 1 + RN])
            m.LG = place_r([P, TT, NE])
            m.OH = place_r([P, TT, NE])
            m.KEY = place_r([P, TT, NE])
            m.t1 = place_r([P, TT])
            m.t2 = place_r([P, TT])
            m.t3 = place_r([P, TT])
            m.WSF = place_r([P, TT * WR + P - WR], BF16)
            m.WS = m.WSF[:, 0:TT * WR].rearrange("p (t a n) -> p t a n", a=3, n=NE)
            m.WT = place_t([WR, TOK], BF16)
            return m

        def experts_weights(pool, m, sp_raw, scale=None):
            def ch(ins):
                link(pool, p_ch, n_pool, ins)

            for w, st in ((m.raw1, m.w1),) + (((m.raw3, m.w3),) if m.gated else ()):
                if scale is not None:
                    ch(nc.gpsimd.tensor_tensor(w, w, scale.to_broadcast([P, m.HT * P]), ALU.mult))
                ch(nc.gpsimd.tensor_copy(st[:, 0, :], w))
                ch(nc.gpsimd.tensor_copy(st[0:D, 1, :], st[0:D, 0, :]))
                ch(nc.gpsimd.tensor_tensor(w, w, st[:, 0, :], ALU.subtract))
                ch(nc.gpsimd.tensor_copy(st[:, 2, :], w))
                ch(nc.gpsimd.tensor_tensor(w, w, st[:, 2, :], ALU.subtract))
                ch(nc.gpsimd.tensor_copy(st[D:P, 1, :], w[D:P, :]))
            pool.sem_inc(m.wst, 1)
            pool.wait_ge(m.raw_in, 16)
            nc.gpsimd.tensor_copy(m.sel[:, :], m.raw1[0:WR, :]).then_inc(m.wst, 1)

        def experts_pe_pre(pe, m, strings):
            prepare_pe(pe, m.str, m.xt, m.xw, (m.rsp, 1), m.rst, NE, m.lp, m.lk, strings)

        def experts_act_pre(act, m):
            prepare_act(act, m.xt, m.xw, NE, m.lp, m.lk, m.LG)
            act.wait_ge(m.sh, 1)
            nc.scalar.activation(m.LG, m.LG, ACT.Exp).then_inc(m.ex, 1)

        def softmax8(dve, m, bias=None):
            ch = lambda ins: link(dve, ln_ch, n_ln, ins)
            dve.wait_ge(m.lk, GT + 2)
            if bias is not None:
                ch(nc.vector.tensor_tensor(m.LG, m.LG, bias.unsqueeze(1).to_broadcast([P, TT, NE]), ALU.add))
            ch(nc.vector.tensor_reduce(m.t1, m.LG, AX.X, ALU.max))
            nc.vector.tensor_tensor(m.LG, m.LG, b3(m.t1, NE), ALU.subtract).then_inc(m.sh, 1)
            dve.wait_ge(m.ex, 1)
            ch(nc.vector.tensor_reduce(m.t1, m.LG, AX.X, ALU.add))
            ch(nc.vector.reciprocal(m.t1, m.t1))
            ch(nc.vector.tensor_tensor(m.LG, m.LG, b3(m.t1, NE), ALU.mult))

        def first_max(dve, m, top, oh, key, tmp):
            ch = lambda ins: link(dve, ln_ch, n_ln, ins)
            ch(nc.vector.tensor_reduce(top, m.LG, AX.X, ALU.max))
            ch(nc.vector.tensor_tensor(key, m.LG, b3(top, NE), ALU.is_equal))
            ch(nc.vector.tensor_tensor(key, key, m.rw[:, RN + 1:2 * RN + 1].unsqueeze(1).to_broadcast([P, TT, NE]), ALU.mult))
            ch(nc.vector.tensor_reduce(tmp, key, AX.X, ALU.max))
            ch(nc.vector.tensor_tensor(oh, key, b3(tmp, NE), ALU.is_equal))

        def weight_strings(dve, m, w):
            ch = lambda ins: link(dve, ln_ch, n_ln, ins)
            ch(nc.vector.memset(m.WSF[:, TT * WR:], 0.0))
            ch(nc.vector.tensor_copy(m.WS[:, :, 0, :], w))
            ch(nc.vector.tensor_tensor(w, w, m.WS[:, :, 0, :], ALU.subtract))
            ch(nc.vector.tensor_copy(m.WS[:, :, 1, :], w))
            ch(nc.vector.tensor_tensor(w, w, m.WS[:, :, 1, :], ALU.subtract))
            nc.vector.tensor_copy(m.WS[:, :, 2, :], w).then_inc(m.ws, 1)

        def experts_pe(pe, m, b2s=None):
            HT, PP = m.HT, m.PP
            pe.wait_ge(m.ws, 1)
            with pe.Fori(0, GT // 2) as i:
                for h in range(2):
                    pe.wait_ge(m.wk, i * 2 + h + 1)
                    for u in range(TPG):
                        ins = nc.tensor.transpose(bank16(6 + h)[:, u * P:(u + 1) * P],
                                                  m.WSF[:, bass.ds(((i * 2 + h) * TPG + u) * WR, P)], ident16[:, :])
                    ins.then_inc(m.wt, 1)
            pe.wait_ge(m.wk, GT + 2)
            pe.wait_ge(m.wst, 2)
            pe.sem_inc(m.o, m.CR)

            def hidden(gi, h, k):
                n, ba = gi * HT + k, (h * HT + k) % 2
                tok = bass.ds(gi * GW, GW)
                pe.wait_ge(m.h, n + 1)
                for p, w in enumerate((0, 1, 0)):
                    ins = nc.tensor.matmul(PS[:, ba, 0:GW], m.w1[:, p, k * P:(k + 1) * P], W[:, w, tok],
                                           start=(p == 0), stop=(p == 2))
                ins.then_inc(m.a, 1)
                if m.gated:
                    for p, w in enumerate((0, 1, 0)):
                        nc.tensor.matmul(PS[:, 2 + ba, 0:GW], m.w3[:, p, k * P:(k + 1) * P], W[:, w, tok],
                                         start=(p == 0), stop=(p == 2))
                nc.tensor.matmul(PS[:, 4 + ba, 0:GW], m.sel[:, k * P:(k + 1) * P], m.WT[:, tok],
                                 start=True, stop=True).then_inc(m.b, 1)

            def second(gi, j):
                both = 2 * j + 1 < HT
                pe.wait_ge(m.h, gi * HT + 2 * j + both + 3)
                if j == 0:
                    pe.wait_ge(m.ot, gi + 1)
                for y in range(1 + both):
                    k = 2 * j + y
                    ins = nc.tensor.matmul(PS[y * D:(y + 1) * D, 6, 0:GW], m.w2[:, k, :], m.hh[:, k % m.ring, :],
                                           start=(j == 0), stop=True, skip_group_check=True)
                if j == PP - 1 and b2s is not None:
                    for p in range(3):
                        ins = nc.tensor.matmul(PS[:, 6, 0:GW], b2s[:, p, :], m.WT[:, bass.ds(gi * GW, GW)],
                                               start=False, stop=True, skip_group_check=True)
                ins.then_inc(m.o, 1)

            def back(gi):
                pe.wait_ge(m.ot, gi + 2)
                pe.wait_ge(m.add, gi + 1)
                for a in range(TPG):
                    ins = nc.tensor.transpose(PS[:, 7, a * P:(a + 1) * P], OT[:, a * P:(a + 1) * P], ident[:, :])
                ins.then_inc(m.ft, 1)

            rest = list(range((HT - 2) // 2, PP))
            with pe.Fori(0, GT // 2) as i:
                for h in range(2):
                    gi = i * 2 + h
                    for k in range(HT):
                        hidden(gi, h, k)
                        if h and k < len(rest):
                            second(gi - 1, rest[k])
                        if k >= 3 and k % 2 and (k - 3) // 2 not in rest:
                            second(gi, (k - 3) // 2)
                        if h and k == 5:
                            back(gi - 1)
                for j in rest:
                    second(i * 2 + 1, j)
                back(i * 2 + 1)

        def experts_act(act, m, SL, func, bias=None):
            HT, PP = m.HT, m.PP
            act.sem_inc(m.wk, 2)
            with act.Fori(0, GT // 2) as i:
                for h in range(2):
                    act.wait_ge(m.wt, i * 2 + h + 1)
                    nc.scalar.copy(m.WT[:, bass.ds((i * 2 + h) * GW, GW)], bank16(6 + h)[0:WR, 0:GW]).then_inc(m.wk, 1)
            act.sem_inc(m.ot, 1)
            act.sem_inc(m.ft, 1)

            def keep(gi):
                act.wait_ge(m.o, (gi + 1) * PP + m.CR)
                act.wait_ge(m.ft, gi + 1)
                nc.scalar.copy(OT[:, :], PS[:, 6, 0:GW]).then_inc(m.ot, 1)

            with act.Fori(0, GT // 2) as i:
                for h in range(2):
                    gi = i * 2 + h
                    for k in range(HT):
                        n, ba = gi * HT + k, (h * HT + k) % 2
                        act.wait_ge(m.a, n + 1)
                        act.wait_ge(m.h, n + 1)
                        if bias is None:
                            nc.scalar.activation(SL[:, ba, :], PS[:, ba, 0:GW], func).then_inc(m.s, 1)
                        else:
                            nc.scalar.activation(SL[:, ba, :], PS[:, ba, 0:GW], func, bias=bias[:, k:k + 1]).then_inc(m.s, 1)
                        if h and k == 2:
                            keep(gi - 1)
                keep(i * 2 + 1)

        def experts_dve(dve, m, SL, TM, dst, finish=None):
            HT, PP = m.HT, m.PP
            dve.sem_inc(m.h, 2)
            dve.sem_inc(m.add, 1)

            def add(gi):
                O = PS[:, 7, 0:GW].rearrange("p (t n) -> p t n", n=P)
                dve.wait_ge(m.ft, gi + 2)
                v = dst[:, bass.ds(gi * TPG, TPG), :]
                nc.vector.tensor_tensor(v, O[:, :, 0:D], v, ALU.add).then_inc(m.fc, 1)
                dve.wait_ge(m.fc, gi + 1)
                nc.vector.tensor_tensor(v, O[:, :, D:P], v, ALU.add).then_inc(m.add, 1)

            with dve.Fori(0, GT // 2) as i:
                for h in range(2):
                    gi = i * 2 + h
                    for k in range(HT):
                        n, ba = gi * HT + k, (h * HT + k) % 2
                        src = SL[:, ba, :]
                        dve.wait_ge(m.s, n + 1)
                        dve.wait_ge(m.b, n + 1)
                        if m.gated:
                            nc.vector.tensor_tensor(TM[:, ba, :], PS[:, 2 + ba, 0:GW], src, ALU.mult).then_inc(m.tc, 1)
                            dve.wait_ge(m.tc, n + 1)
                            src = TM[:, ba, :]
                        dve.wait_ge(m.o, gi * PP + k // 2 + 1)
                        nc.vector.tensor_tensor(m.hh[:, k % m.ring, :], PS[:, 4 + ba, 0:GW], src, ALU.mult).then_inc(m.h, 1)
                        if h and k == 6 and finish is None:
                            add(gi - 1)
                        if h and k >= 6 and finish is not None:
                            finish(gi - 1, (k - 6,))
                if finish is None:
                    add(i * 2 + 1)
                else:
                    finish(i * 2 + 1, range(10))
            dve.wait_ge(m.add, GT + 1)

        HID0 = -(-NE * int(8 / 3 * D) // P)
        pl2, pl5, pl3 = places(A2, 0), places(A5, 0), places(A3[:, :].bitcast(BF16), 0)
        f = experts("f", HID0, HID0, True, pl2, pl3, pl5, A4[:, :].rearrange("p (k n) -> p k n", n=GW), None)
        f.var, f.std = sem("f_square_sums"), sem("f_rms")
        fSL, fTM = pl5([P, 2, GW]), pl5([P, 2, GW])
        fOH2 = pl3([P, TT, NE])

        def f_sp(sp):
            sp.wait_ge(b_o, GT)
            for dst, name in ((f.raw1, "f_w1"), (f.raw3, "f_w3"), (f.w2, "f_w2")):
                sp.dma_start(dst, I[name]).then_inc(f.inp, 16)
            sp.wait_ge(f.wst, 1)
            sp.dma_start(f.raw1[0:WR, :], I["f_sel"]).then_inc(f.raw_in, 16)

        def f_pool(pool):
            pool.wait_ge(f.inp, 4 * 16)
            experts_weights(pool, f, None, f.rw[:, RN:RN + 1])

        def f_dve(dve):
            ch = lambda ins: link(dve, ln_ch, n_ln, ins)
            ch(nc.vector.tensor_tensor(Q2, XN[:, :, :], XN[:, :, :], ALU.mult))
            nc.vector.tensor_reduce(stat[:, 1, :], Q2, AX.X, ALU.add).then_inc(f.var, 1)
            dve.wait_ge(f.std, 1)
            ch(nc.vector.reciprocal(stat[:, 3, :], stat[:, 2, :]))
            dve.wait_ge(f.inp, 4 * 16)
            cr = lambda ins: link(dve, ln_ch, n_ln, ins)
            cr(nc.vector.tensor_tensor(f.rw[:, 0:RN], f.rw[:, 0:RN], f.rw[:, RN:RN + 1].to_broadcast([P, RN]), ALU.mult))
            split_w(dve, ln_ch, n_ln, f.rw[:, 0:RN], f.rst, f.rsp, 1)
            split_x(dve, n_ln, Q2, Q2, f.str, None, rms)
            softmax8(dve, f)
            first_max(dve, f, f.t1, f.OH, f.KEY, f.t3)
            cr(nc.vector.scalar_tensor_tensor(f.LG, f.OH, -2.0, f.LG, ALU.mult, ALU.add))
            first_max(dve, f, f.t2, fOH2, f.KEY, f.t3)
            cr(nc.vector.tensor_tensor(f.t3, f.t1, f.t2, ALU.add))
            cr(nc.vector.tensor_scalar(f.t3, f.t3, 1e-9, None, ALU.add))
            cr(nc.vector.reciprocal(f.t3, f.t3))
            cr(nc.vector.tensor_tensor(f.t1, f.t1, f.t3, ALU.mult))
            cr(nc.vector.tensor_tensor(f.t2, f.t2, f.t3, ALU.mult))
            cr(nc.vector.tensor_tensor(f.OH, f.OH, b3(f.t1, NE), ALU.mult))
            cr(nc.vector.tensor_tensor(fOH2, fOH2, b3(f.t2, NE), ALU.mult))
            cr(nc.vector.tensor_tensor(f.OH, f.OH, fOH2, ALU.add))
            weight_strings(dve, f, f.OH)
            experts_dve(dve, f, fSL, fTM, XN)
            nc.vector.tensor_tensor(H[:, :, :], H[:, :, :], XN[:, :, :], ALU.add).then_inc(f.done, 1)
            dve.wait_ge(f.done, 1)

        def f_act(act):
            act.wait_ge(f.var, 1)
            nc.scalar.activation(stat[:, 2, :], stat[:, 1, :], ACT.Sqrt, bias=epsc[:, 1:2], scale=1.0 / D).then_inc(f.std, 1)
            experts_act_pre(act, f)
            experts_act(act, f, fSL, ACT.Silu)

        def f_pe(pe):
            experts_pe_pre(pe, f, None)
            experts_pe(pe, f)


        SC = 64
        NC_ = NP // SC
        lam = sb("lam", [P, 5])
        sp_ = sb("ssm_parameters", [P, 24])
        s_in = sem("s_parameters_loaded")
        s_x = sem("s_exponent_ready")
        s_e = sem("s_exponentials")
        s_a = sem("s_angle_ready")
        s_sn = sem("s_sines")
        col = lambda k: sp_[:, k:k + 1]
        STEP, MAG, TH, K, XM, E, EM1, SH, SN, CO, NR, NI, LR, DEN, AL, BE, TA, TB_, AN = range(19)

        def s_parameters(dve):
            ch = lambda ins: link(dve, ln_ch, n_ln, ins)
            tt = lambda o, a, b, op: ch(nc.vector.tensor_tensor(o, a, b, op))
            ts = lambda o, a, x, op: ch(nc.vector.tensor_scalar(o, a, x, None, op))
            dve.wait_ge(s_e, 1)
            lre, lim, up, dn = lam[:, 0:1], lam[:, 1:2], lam[:, 3:4], lam[:, 4:5]
            ts(col(LR), lre, -1.0, ALU.mult)
            tt(col(LR), col(LR), lre, ALU.min)
            tt(col(MAG), col(LR), col(STEP), ALU.mult)
            nc.vector.tensor_scalar(col(XM), col(MAG), -1.0, None, ALU.max).then_inc(s_x, 1)
            dve.wait_ge(s_x, 1)
            tt(col(TH), lim, col(STEP), ALU.mult)
            ts(col(K), col(TH), 1.0 / (2 * np.pi), ALU.mult)
            ts(col(K), col(K), 1.5 * 2.0 ** 23, ALU.add)
            ts(col(K), col(K), -1.5 * 2.0 ** 23, ALU.add)
            c1 = 6.28125
            c2 = float(np.float32(np.float32((2 * np.pi - c1) * 2 ** 20).round() / 2 ** 20))
            for c in (c1, c2, 2 * np.pi - c1 - c2):
                ch(nc.vector.scalar_tensor_tensor(col(TH), col(K), -float(c), col(TH), ALU.mult, ALU.add))
            ts(col(TH), col(TH), 3.1415925, ALU.min)
            ts(col(AN), col(TH), -3.1415925, ALU.max)
            nc.vector.tensor_scalar(col(TA), col(AN), 0.5, None, ALU.mult).then_inc(s_a, 1)
            dve.wait_ge(s_a, 1)
            dve.wait_ge(s_e, 2)
            ts(col(EM1), col(XM), 1.0 / 24, ALU.mult)
            ts(col(EM1), col(EM1), 1.0 / 6, ALU.add)
            tt(col(EM1), col(EM1), col(XM), ALU.mult)
            ts(col(EM1), col(EM1), 0.5, ALU.add)
            tt(col(EM1), col(EM1), col(XM), ALU.mult)
            ts(col(EM1), col(EM1), 1.0, ALU.add)
            tt(col(EM1), col(EM1), col(XM), ALU.mult)
            ts(col(TB_), col(MAG), -0.01, ALU.is_ge)
            tt(col(EM1), col(EM1), col(TB_), ALU.mult)
            ts(col(TB_), col(TB_), -1.0, ALU.mult)
            ts(col(TB_), col(TB_), 1.0, ALU.add)
            ts(col(NR), col(E), -1.0, ALU.add)
            tt(col(NR), col(NR), col(TB_), ALU.mult)
            tt(col(EM1), col(EM1), col(NR), ALU.add)
            dve.wait_ge(s_sn, 2)
            tt(col(SH), col(SH), col(SH), ALU.mult)
            ts(col(SH), col(SH), -2.0, ALU.mult)
            ts(col(CO), col(SH), 1.0, ALU.add)
            tt(col(NR), col(E), col(SH), ALU.mult)
            tt(col(NR), col(NR), col(EM1), ALU.add)
            tt(col(NI), col(E), col(SN), ALU.mult)
            tt(col(DEN), col(LR), col(LR), ALU.mult)
            ch(nc.vector.scalar_tensor_tensor(col(DEN), lim, lim, col(DEN), ALU.mult, ALU.add))
            ch(nc.vector.reciprocal(col(DEN), col(DEN)))
            tt(col(TA), col(NR), col(LR), ALU.mult)
            ch(nc.vector.scalar_tensor_tensor(col(TA), col(NI), lim, col(TA), ALU.mult, ALU.add))
            tt(col(TA), col(TA), col(DEN), ALU.mult)
            tt(col(TB_), col(NI), col(LR), ALU.mult)
            tt(col(K), col(NR), lim, ALU.mult)
            tt(col(TB_), col(TB_), col(K), ALU.subtract)
            tt(col(TB_), col(TB_), col(DEN), ALU.mult)
            tt(col(AL), col(TB_), dn, ALU.mult)
            ch(nc.vector.scalar_tensor_tensor(col(AL), col(TA), up, col(AL), ALU.mult, ALU.add))
            tt(col(BE), col(TB_), up, ALU.mult)
            ch(nc.vector.scalar_tensor_tensor(col(BE), col(TA), dn, col(BE), ALU.mult, ALU.subtract))

        def s_parameters_act(act):
            act.wait_ge(s_in, 16)
            nc.scalar.activation(col(STEP), lam[:, 2:3], ACT.Exp).then_inc(s_e, 1)
            act.wait_ge(s_x, 1)
            nc.scalar.activation(col(E), col(MAG), ACT.Exp).then_inc(s_e, 1)
            act.wait_ge(s_a, 1)
            nc.scalar.activation(col(SN), col(AN), ACT.Sin).then_inc(s_sn, 1)
            nc.scalar.activation(col(SH), col(TA), ACT.Sin).then_inc(s_sn, 1)

        TAB = A0[:, :].bitcast(F32).rearrange("p (k n) -> p k n", k=2)
        ps3 = places(A3[:, :].bitcast(BF16), 2 * 3250)
        fin0 = ps3([P, 2, SC + 1])
        fin1 = ps3([P, 2, NC_])
        s_tab = sem("s_table_ready")

        def s_tables(pool):
            ch = lambda ins: link(pool, p_ch, n_pool, ins)

            def double(T, total):
                at = 1
                while at < total - 1:
                    m = min(at, total - 1 - at)
                    bc = lambda k: T[:, k, at:at + 1].to_broadcast([P, m])
                    c, s_ = T[:, 0, 1:1 + m], T[:, 1, 1:1 + m]
                    co, so = T[:, 0, at + 1:at + 1 + m], T[:, 1, at + 1:at + 1 + m]
                    tmp = ptmp[:, 0:m]
                    ch(nc.gpsimd.tensor_tensor(tmp, s_, bc(1), ALU.mult))
                    ch(nc.gpsimd.tensor_tensor(co, c, bc(0), ALU.mult))
                    ch(nc.gpsimd.tensor_tensor(co, co, tmp, ALU.subtract))
                    ch(nc.gpsimd.tensor_tensor(tmp, c, bc(1), ALU.mult))
                    ch(nc.gpsimd.tensor_tensor(so, s_, bc(0), ALU.mult))
                    ch(nc.gpsimd.tensor_tensor(so, so, tmp, ALU.add))
                    at += m

            for T in (fin0, fin1):
                ch(nc.gpsimd.memset(T[:, 0, 0:1], 1.0))
                ch(nc.gpsimd.memset(T[:, 1, 0:1], 0.0))
            ch(nc.gpsimd.tensor_copy(fin0[:, 0, 1:2], col(CO)))
            ch(nc.gpsimd.tensor_copy(fin0[:, 1, 1:2], col(SN)))
            double(fin0, SC + 1)
            ch(nc.gpsimd.tensor_copy(fin1[:, :, 1:2], fin0[:, :, SC:SC + 1]))
            double(fin1, NC_)
            pool.wait_ge(f.xw, GT + 2)
            for hb in range(2):
                cs_ = slice(hb * NC_ // 2, (hb + 1) * NC_ // 2)
                sh = [P, NC_ // 2, SC]
                hi = lambda k: fin1[:, k, cs_].unsqueeze(2).to_broadcast(sh)
                lo = lambda k: fin0[:, k, 0:SC].unsqueeze(1).to_broadcast(sh)
                o = lambda k: TAB[:, k, hb * NP // 2:(hb + 1) * NP // 2].rearrange("p (c j) -> p c j", j=SC)
                t = big.rearrange("p (c j) -> p c j", j=SC)
                ch(nc.gpsimd.tensor_tensor(t, hi(1), lo(1), ALU.mult))
                ch(nc.gpsimd.tensor_tensor(o(0), hi(0), lo(0), ALU.mult))
                ch(nc.gpsimd.tensor_tensor(o(0), o(0), t, ALU.subtract))
                ch(nc.gpsimd.tensor_tensor(t, hi(1), lo(0), ALU.mult))
                ch(nc.gpsimd.tensor_tensor(o(1), hi(0), lo(1), ALU.mult))
                ch(nc.gpsimd.tensor_tensor(o(1), o(1), t, ALU.add))
            pool.sem_inc(s_tab, 1)

        ptmp = sb("table_product", [P, SC])
        big = pl5([P, NP // 2])
        pa4 = places(A4[:, :].bitcast(BF16), 0)
        m1, m2, uu, zz, zc, zs = (pa4([P, 2, GW]) if k < 5 else None for k in range(6))
        pa5 = places(A3[:, :].bitcast(BF16), 0)
        zs = pa5([P, 2, GW])
        sB = pa5([P, 2, D])
        sQ = pa5([P, 2, P])
        sQr = pa5([P, P])
        sW = [pa5([P, 3, P], BF16), pa5([P, 3, P], BF16)]
        sC = pa5([P, 2, D])
        sCz = pa5([P, 2, D])
        zlast = pa5([P, 1])
        rb = pa5([P, GW])
        yt = pa5([P, 2, TPG, D])
        S = Stage()
        S.w = sem("s_weights_loaded")
        S.q = sem("s_input_weights")
        S.qt = sem("s_input_weights_transposed")
        S.ws = sem("s_weight_stacks")
        S.str = sem("s_strings")
        S.xt = sem("s_transposed")
        S.xw = sem("s_stacks")
        S.p = sem("s_input_product")
        S.pf = sem("s_input_product_read")
        S.u = sem("s_sum_ready")
        S.z = sem("s_scanned")
        S.zc = sem("s_turned_back")
        S.o = sem("s_output_product")
        S.ot = sem("s_output_kept")
        S.ft = sem("s_output_transposed")
        S.oc = sem("s_output_chain")
        S.add = sem("s_output_added")
        S.xa = sem("s_normed_added")
        S.sc = sem("s_scan_chain")

        def s_sp(sp):
            sp.wait_ge(f.done, 1)
            sp.dma_start(sB, I["s_b"]).then_inc(S.w, 16)
            sp.dma_start(sC, I["s_c"]).then_inc(S.w, 16)

        def s_dve(dve):
            layer_norm(dve, n_ln, ln_var)
            dve.wait_ge(ln_std, 3)
            link(dve, ln_ch, n_ln, nc.vector.reciprocal(stat[:, 3, :], stat[:, 2, :]))
            split_x(dve, n_ln, XN[:, :, :], Q2, S.str, S2, normed)
            ch = lambda ins: link(dve, ln_ch, n_ln, ins)
            dve.wait_ge(S.w, 2 * 16)
            dve.wait_ge(s_tab, 1)
            for k, (a, c) in enumerate(((AL, BE), (BE, AL))):
                v = sQ[:, k, 0:D]
                ch(nc.vector.tensor_scalar(v, sB[:, 0, :], col(a), None, ALU.mult))
                if k:
                    ch(nc.vector.tensor_scalar(v, v, -1.0, None, ALU.mult))
                ch(nc.vector.scalar_tensor_tensor(v, sB[:, 1, :], col(c), v, ALU.mult, ALU.add))
                ins = nc.vector.tensor_copy(sQ[:, k, D:P], v)
                ins.then_inc(S.q, 1)
            ch(nc.vector.tensor_tensor(sp_[:, 20:21], lam[:, 3:4], lam[:, 4:5], ALU.subtract))
            ch(nc.vector.tensor_scalar(sCz[:, 0, :], sC[:, 0, :], sp_[:, 20:21], None, ALU.mult))
            ch(nc.vector.tensor_scalar(sCz[:, 1, :], sC[:, 1, :], -1.0, None, ALU.mult))
            ch(nc.vector.memset(rb, 1.0))
            ch(nc.vector.tensor_scalar(rb, rb, col(E), None, ALU.mult))
            for k in range(2):
                dve.wait_ge(S.qt, k + 1)
                ch(nc.vector.tensor_copy(sQr, PS[:, k, 0:P]))
                split_w(dve, ln_ch, n_ln, sQr, sW[k], S.ws, k + 1)
            nc.vector.tensor_tensor(H[:, :, :], H[:, :, :], XN[:, :, :], ALU.add).then_inc(S.xa, 1)
            dve.wait_ge(S.xa, 1)
            dve.sem_inc(S.pf, 2)
            dve.sem_inc(S.add, 2)
            dve.sem_inc(S.sc, 1)

            def turn(gi, g, s_):
                dve.wait_ge(S.p, gi + 1)
                dve.wait_ge(S.u, gi + 1)
                t = bass.ds(g * GW, GW)
                nc.vector.tensor_tensor(m1[:, s_, :], PS[:, 2 * s_, 0:GW], TAB[:, 0, t], ALU.mult)
                nc.vector.tensor_tensor(m2[:, s_, :], PS[:, 2 * s_ + 1, 0:GW], TAB[:, 1, t], ALU.mult).then_inc(S.pf, 1)

            def scan(gi, s_, first):
                dve.wait_ge(S.u, gi + 3)
                dve.wait_ge(S.zc, gi + 1)
                dve.wait_ge(S.z, gi + 2)
                nc.vector.tensor_tensor_scan(zz[:, s_, :], rb, uu[:, s_, :], 0.0 if first else zz[:, 1 - s_, GW - 1:GW],
                                             ALU.mult, ALU.add).then_inc(S.z, 1)

            def add(gi, s_):
                O = PS[:, 6 + s_, 0:GW].rearrange("p (t n) -> p t n", n=P)
                v = H[:, bass.ds(gi * TPG, TPG), :]
                y = yt[:, s_, :, :]
                dve.wait_ge(S.ft, gi + 2)
                dve.wait_ge(S.oc, gi * 2 + 1)
                nc.vector.tensor_copy(y, O[:, :, 0:D]).then_inc(S.oc, 1)
                dve.wait_ge(S.oc, gi * 2 + 2)
                nc.vector.tensor_tensor(y, O[:, :, D:P], y, ALU.add).then_inc(S.oc, 1)
                dve.wait_ge(S.oc, gi * 2 + 3)
                nc.vector.scalar_tensor_tensor(v, y, 0.0, v, ALU.max, ALU.add).then_inc(S.add, 1)

            dve.sem_inc(S.oc, 1)
            dve.sem_inc(S.z, 2)
            for b in range(B):
                turn(b * NG, 0, b)
                turn(b * NG + 1, 1, 1 - b)
                scan(b * NG, b, True)

                def step(g, k):
                    turn(b * NG + g, g, k)
                    scan(b * NG + g - 1, 1 - k, False)
                    add(b * NG + g - 2, k)

                with dve.Fori(1, NG // 2) as i:
                    step(i * 2, b)
                    step(i * 2 + 1, 1 - b)
                step(NG - 1, b)
                scan(b * NG + NG - 1, b, False)
                add(b * NG + NG - 2, 1 - b)
                add(b * NG + NG - 1, b)
            dve.wait_ge(S.add, GT + 2)

        def s_pool(pool):
            pool.sem_inc(S.u, 2)
            pool.sem_inc(S.zc, 2)

            def sum_(gi, s_):
                pool.wait_ge(S.pf, gi + 3)
                pool.wait_ge(S.z, gi + 1)
                nc.gpsimd.tensor_tensor(uu[:, s_, :], m1[:, s_, :], m2[:, s_, :], ALU.add).then_inc(S.u, 1)

            def back(gi, g, s_):
                pool.wait_ge(S.z, gi + 3)
                pool.wait_ge(S.o, gi + 1)
                t = bass.ds(g * GW, GW)
                nc.gpsimd.tensor_tensor(zc[:, s_, :], zz[:, s_, :], TAB[:, 0, t], ALU.mult).then_inc(S.sc, 1)
                nc.gpsimd.tensor_tensor(zs[:, s_, :], zz[:, s_, :], TAB[:, 1, t], ALU.mult).then_inc(S.zc, 1)

            for b in range(B):
                sum_(b * NG, b)
                sum_(b * NG + 1, 1 - b)
                back(b * NG, 0, b)

                def step(g, k):
                    sum_(b * NG + g, k)
                    back(b * NG + g - 1, g - 1, 1 - k)

                with pool.Fori(1, NG // 2) as i:
                    step(i * 2, b)
                    step(i * 2 + 1, 1 - b)
                step(NG - 1, b)
                back(b * NG + NG - 1, NG - 1, b)

        def s_act(act):
            act.wait_ge(ln_var, 3)
            nc.scalar.activation(stat[:, 2, :], stat[:, 1, :], ACT.Sqrt, bias=epsc[:, 0:1], scale=1.0 / D).then_inc(ln_std, 1)
            prepare_act(act, S.xt, S.xw, 0, None, None, None)
            act.sem_inc(S.ft, 1)

            def keep(gi, s_):
                act.wait_ge(S.o, gi + 3)
                act.wait_ge(S.ft, gi + 1)
                nc.scalar.copy(OT[:, :], PS[:, 4 + s_, 0:GW]).then_inc(S.ot, 1)

            for b in range(B):
                keep(b * NG, b)
                with act.Fori(0, NG // 2) as i:
                    for h in range(2):
                        keep(b * NG + i * 2 + h + 1, (b + h + 1) % 2)

        def s_pe(pe):
            for c in range(NCH):
                transposes(pe, c, S.str, S.xt, S.xw, S2)
            for k in range(2):
                pe.wait_ge(S.q, k + 1)
                nc.tensor.transpose(PS[:, k, 0:P], sQ[:, k, :], ident[:, :]).then_inc(S.qt, 1)
            pe.wait_ge(S.xw, GT + 2)
            pe.wait_ge(S.ws, 2)
            pe.sem_inc(S.o, 2)

            def inp(gi, s_):
                pe.wait_ge(S.pf, gi + 1)
                for k in range(2):
                    for p_, w in enumerate((0, 1, 0)):
                        ins = nc.tensor.matmul(PS[:, 2 * s_ + k, 0:GW], sW[k][:, p_, :], W[:, w, bass.ds(gi * GW, GW)],
                                               start=(p_ == 0), stop=(p_ == 2))
                ins.then_inc(S.p, 1)

            def outp(gi, s_):
                pe.wait_ge(S.zc, gi + 3)
                for y, z in enumerate((zc, zs)):
                    ins = nc.tensor.matmul(PS[y * D:(y + 1) * D, 4 + s_, 0:GW], sCz[:, y, :], z[:, s_, :],
                                           start=True, stop=True, skip_group_check=True)
                ins.then_inc(S.o, 1)

            def fin(gi, s_):
                pe.wait_ge(S.ot, gi + 1)
                pe.wait_ge(S.add, gi + 1)
                for a in range(TPG):
                    ins = nc.tensor.transpose(PS[:, 6 + s_, a * P:(a + 1) * P], OT[:, a * P:(a + 1) * P], ident[:, :])
                ins.then_inc(S.ft, 1)

            for b in range(B):
                inp(b * NG, b)
                inp(b * NG + 1, 1 - b)

                def step(g, k):
                    inp(b * NG + g, k)
                    outp(b * NG + g - 2, k)
                    fin(b * NG + g - 2, k)

                with pe.Fori(1, NG // 2) as i:
                    step(i * 2, b)
                    step(i * 2 + 1, 1 - b)
                step(NG - 1, b)
                for g, k in ((NG - 2, 1 - b), (NG - 1, b)):
                    outp(b * NG + g, k)
                    fin(b * NG + g, k)

        HID1 = NE * F1 // P
        CAP = -(-5 * B * N // (4 * NE))
        qa5, qa0, qa3 = places(A5, 0), places(A0, 0), places(A3[:, :].bitcast(BF16), 0)
        qa4 = places(A4[:, :].bitcast(BF16), 0)
        ghh = qa4([P, 8, GW])
        gSL = qa4([P, 2, GW])
        g_ = experts("g", HID1, 8, False, qa5, qa0, qa3, ghh, None)
        gb1 = qa5([P, HID1])
        gb2 = qa5([WR, D])
        gb2s = qa5([WR, 3, P], BF16)
        gbias = qa5([P, NE])
        upto = qa5([P, P])
        ones = qa5([P, P])
        TOTT = qa0([P, NE, TT])
        SCN = qa0([P, NE, TT])
        smask = qa5([P, NE, TT])
        gy, gz, gmask = (qa0([P, TPG, D]) for _ in range(3))
        limit = qa0([P, 3])
        g_.cum = sem("g_positions_counted")
        g_oh = sem("g_choice_ready")

        def g_sp(sp):
            sp.wait_ge(f.done, 1)
            sp.wait_ge(s_tab, 1)
            for dst, name in ((g_.raw1, "g_w1"), (g_.w2, "g_w2"), (gb1, "g_b1"), (gb2, "g_b2"), (gbias, "g_bias"), (upto, "upto")):
                sp.dma_start(dst, I[name]).then_inc(g_.inp, 16)
            sp.wait_ge(g_.wst, 1)
            sp.dma_start(g_.raw1[0:WR, :], I["g_sel"]).then_inc(g_.raw_in, 16)

        def g_pool(pool):
            pool.wait_ge(g_.inp, 7 * 16)
            experts_weights(pool, g_, None)

        def g_dve(dve):
            layer_norm(dve, n_ln, ln_var)
            dve.wait_ge(ln_std, 4)
            link(dve, ln_ch, n_ln, nc.vector.reciprocal(stat[:, 3, :], stat[:, 2, :]))
            cr = lambda ins: link(dve, ln_ch, n_ln, ins)
            dve.wait_ge(g_.inp, 7 * 16)
            split_w(dve, ln_ch, n_ln, g_.rw[:, 0:RN], g_.rst, g_.rsp, 1)
            split_x(dve, n_ln, XN[:, :, :], Q2, g_.str, S2, normed)
            cr(nc.vector.memset(ones, 1.0))
            cr(nc.vector.memset(gb2s, 0.0))
            cr(nc.vector.memset(smask, 1.0))
            cr(nc.vector.memset(smask[:, :, 0:1], 0.0))
            for k in range(3):
                cr(nc.vector.tensor_copy(gb2s[:, k, 0:D], gb2))
                if k < 2:
                    cr(nc.vector.tensor_tensor(gb2, gb2, gb2s[:, k, 0:D], ALU.subtract))
            softmax8(dve, g_, gbias)
            first_max(dve, g_, g_.t1, g_.OH, g_.KEY, g_.t3)
            nc.vector.tensor_tensor(g_.OH, g_.OH, b3(valid[:, :], NE), ALU.mult).then_inc(g_oh, 1)
            dve.wait_ge(g_.cum, 1)
            for k in range(2):
                v = PS[:, 2 + k, 0:NT * NE].rearrange("p (t e) -> p e t", e=NE)
                cr(nc.vector.tensor_copy(TOTT[:, :, k * NT:(k + 1) * NT], v))
            fl = lambda a: a.rearrange("p e t -> p (e t)")
            cr(nc.vector.tensor_tensor_scan(fl(SCN), fl(smask), fl(TOTT), 0.0, ALU.mult, ALU.add))
            cr(nc.vector.tensor_tensor(SCN, SCN, TOTT, ALU.subtract))
            for k in range(2):
                tl = slice(k * NT, (k + 1) * NT)
                cr(nc.vector.tensor_tensor(g_.KEY[:, tl, :], PS[:, k, 0:NT * NE].rearrange("p (t e) -> p t e", e=NE),
                                           SCN[:, :, tl].rearrange("p e t -> p t e"), ALU.add))
            cr(nc.vector.tensor_tensor(g_.KEY, g_.KEY, g_.OH, ALU.mult))
            cr(nc.vector.tensor_reduce(g_.t2, g_.KEY, AX.X, ALU.add))
            cr(nc.vector.tensor_scalar(g_.t2, g_.t2, float(CAP), None, ALU.is_le))
            cr(nc.vector.tensor_tensor(g_.t1, g_.t1, g_.t2, ALU.mult))
            cr(nc.vector.tensor_tensor(g_.OH, g_.OH, b3(g_.t1, NE), ALU.mult))
            weight_strings(dve, g_, g_.OH)
            cr(nc.vector.memset(limit[:, 0:1], 1e4))
            cr(nc.vector.memset(limit[:, 1:2], -1e4))
            mask = gmask.bitcast(mybir.dt.uint32)
            STEPS = 9

            def finish(gi, steps):
                O = PS[:, 7, 0:GW].rearrange("p (t n) -> p t n", n=P)
                v = H[:, bass.ds(gi * TPG, TPG), :]
                for k in steps:
                    if k:
                        dve.wait_ge(g_.fc, gi * STEPS + k)
                    else:
                        dve.wait_ge(g_.ft, gi + 2)
                    if k in (4, 6, 8):
                        nc.vector.memset(limit[:, 2:3], 0.0)
                    if k == 0:
                        ins = nc.vector.tensor_copy(gy, O[:, :, 0:D])
                    elif k == 1:
                        ins = nc.vector.tensor_tensor(gy, O[:, :, D:P], gy, ALU.add)
                    elif k == 2:
                        ins = nc.vector.tensor_tensor(gmask, gy, gy, ALU.is_equal)
                    elif k == 3:
                        ins = nc.vector.memset(gz, 0.0)
                    elif k == 4:
                        ins = nc.vector.copy_predicated(gz, mask, gy)
                    elif k == 5:
                        ins = nc.vector.tensor_scalar(gmask, gz, 3.4028235e38, None, ALU.is_gt)
                    elif k == 7:
                        ins = nc.vector.tensor_scalar(gmask, gz, -3.4028235e38, None, ALU.is_lt)
                    elif k in (6, 8):
                        ins = nc.vector.copy_predicated(gz, mask, limit[:, k // 2 - 3:k // 2 - 2].unsqueeze(2).to_broadcast([P, TPG, D]))
                    else:
                        ins = nc.vector.tensor_tensor(v, gz, v, ALU.add)
                    ins.then_inc(g_.add if k == 9 else g_.fc, 1)

            experts_dve(dve, g_, gSL, None, None, finish)
            dve.sem_inc(g_.done, 1)

        def g_act(act):
            act.wait_ge(ln_var, 4)
            nc.scalar.activation(stat[:, 2, :], stat[:, 1, :], ACT.Sqrt, bias=epsc[:, 0:1], scale=1.0 / D).then_inc(ln_std, 1)
            experts_act_pre(act, g_)
            experts_act(act, g_, gSL, ACT.Relu, gb1)

        def g_pe(pe):
            experts_pe_pre(pe, g_, S2)
            pe.wait_ge(g_oh, 1)
            for m in range(2):
                for k in range(2):
                    ins = nc.tensor.matmul(PS[:, 2 * m + k, 0:NT * NE], (upto, ones)[m],
                                           g_.OH[:, k * NT:(k + 1) * NT, :].rearrange("p t e -> p (t e)"), start=True, stop=True)
            ins.then_inc(g_.cum, 1)
            experts_pe(pe, g_, gb2s)

        @block.sync
        def _(sp):
            sp.dma_start(x_pad, I["xpad"]).then_inc(t_in, 16)
            sp.dma_start(c1w[:, :], I["c1w"]).then_inc(t_in, 16)
            sp.dma_start(bnp[:, :], I["bnp"]).then_inc(t_in, 16)
            sp.dma_start(c2w, I["c2w"]).then_inc(t_in, 16)
            sp.dma_start(b2[:, :], I["b2"]).then_inc(t_in, 16)
            sp.dma_start(ident[:, :], I["ident"]).then_inc(c_in, 16)
            sp.dma_start(lam[:, :], I["lam"]).then_inc(s_in, 16)
            sp.dma_start(f.rw[:, :], I["f_r"]).then_inc(f.inp, 16)
            sp.dma_start(g_.rw[:, :], I["g_r"]).then_inc(g_.inp, 16)
            sp.dma_start(valid[:, :], I["valid"]).then_inc(c_in, 16)
            sp.dma_start(qk2[:, :, :], I["qk"]).then_inc(c_in, 16)
            sp.wait_ge(t_a, 8 * (IMG // RG))
            sp.dma_start(scratch.rearrange("b (c h) w -> (b c) (h w)", h=IMG), conv).then_inc(t_out, 16)
            sp.wait_ge(t_out, 16)
            for b in range(B):
                t0 = b * NT
                sp.dma_start(H[0:1, t0, :], I["cls"]).then_inc(h_in, 16)
                sp.dma_start(H[1:P, t0, :], scratch[b, 0:P - 1, :]).then_inc(h_in, 16)
                sp.dma_start(H[:, t0 + 1:t0 + NT - 1, :],
                             scratch[b, P - 1:P - 1 + (NT - 2) * P, :].rearrange("(t p) d -> p t d", p=P)).then_inc(h_in, 16)
                sp.dma_start(H[0:1, t0 + NT - 1, :], scratch[b, IMG * IMG - 1:IMG * IMG, :]).then_inc(h_in, 16)
                sp.dma_start(H[1:P, t0 + NT - 1, :], I["cls"].to_broadcast([P - 1, D])).then_inc(h_in, 16)
            b_sp(sp)
            b_sp_rows(sp)
            f_sp(sp)
            s_sp(sp)
            g_sp(sp)
            sp.wait_ge(g_.done, 1)
            for b in range(B):
                sp.dma_start(out[b, 0:N - 1, :].rearrange("(t p) d -> p t d", p=P), H[:, b * NT:(b + 1) * NT - 1, :]).then_inc(o_out, 16)
                sp.dma_start(out[b, N - 1:N, :], H[0:1, (b + 1) * NT - 1, :]).then_inc(o_out, 16)
            sp.wait_ge(o_out, 4 * 16)

        @block.tensor
        def _(pe):
            pe.wait_ge(t_in, 5 * 16)
            for r in range(IMG // RG):
                rows = x_pad[:, 1 + r * RG:1 + (r + 1) * RG, 1:1 + IMG]
                if r >= 2:
                    pe.wait_ge(t_ys, r - 1)
                nc.tensor.matmul(PS[0:B * CR, r % 2, :].rearrange("p (h w) -> p h w", w=IMG), c1w[:, :], rows,
                                 start=True, stop=True).then_inc(t_y, 1)
                pe.wait_ge(t_ys, r + 1)
                for k in range(TAPS):
                    n = r * TAPS + k
                    if n >= 4:
                        pe.wait_ge(t_p, n - 3)
                    nc.tensor.matmul(PS[:, 2 + n % 4, :], c2w[:, k, :], yv[:, r % 2, :],
                                     start=True, stop=True).then_inc(t_w, 1)
            pe.wait_ge(a_ch, 4)
            nc.tensor.matmul(PS[:, 2, 0:D], qkc[:, 0, :], qkc[:, 1, 0:D], start=True, stop=True).then_inc(a_m, 1)
            prepare_pe(pe, x_str, x_t, x_w, (a_ms, 1), MS, D, a_q, a_qe)
            for c in range(NCH):
                transposes(pe, c, a_qstr, a_qpt, a_qp)
            pe.wait_ge(a_qp, GT + 2)
            pe.sem_inc(a_pv, 2)

            def qk(b, g, m, k, n2):
                pe.wait_ge(a_ex, n2 + 1)
                for p, w in enumerate((0, 1, 0)):
                    ins = nc.tensor.matmul(PS[:, k % 3, 0:GW], W[:, w, bass.ds(b * NP + m * P, P)],
                                           QT[:, p, bass.ds(g * GW, GW)], start=(p == 0), stop=(p == 2))
                ins.then_inc(a_s2, 1)

            def mx(b, g, jj, u, n1):
                pe.wait_ge(a_s1f, n1 + 1)
                for p in range(2):
                    ins = nc.tensor.matmul(PS[:, 3 + u, 0:GW], QP[:, p, bass.ds((b * NG + g) * GW + u * P, P)],
                                           W[:, 0, bass.ds(b * NP + jj * GW, GW)], start=(p == 0), stop=(p == 1))
                ins.then_inc(a_s1, 1)

            def pv(n2, v, k, both, first):
                pe.wait_ge(a_ex, n2 + 4 + both)
                pe.wait_ge(a_vs, v)
                for y in range(1 + both):
                    ins = nc.tensor.matmul(PS[y * D:(y + 1) * D, 6, 0:GW], VS[:, k + y, :], PT[:, k + y, :],
                                           start=first, stop=True, skip_group_check=True)
                ins.then_inc(a_pv, 1)

            def fin(gi):
                pe.wait_ge(a_ot, gi + 2)
                for a in range(TPG):
                    ins = nc.tensor.transpose(PS[:, 7, a * P:(a + 1) * P], OT[:, a * P:(a + 1) * P], ident[:, :])
                ins.then_inc(a_ft, 1)

            def prep(gi, half, nofin=False):
                if half == 0:
                    pe.wait_ge(a_str, gi + 1)
                    if not nofin:
                        pe.wait_ge(a_o, gi)
                pe.wait_ge(a_qt, gi * 2 + half + 1)
                for w in ((0, 1), (2,))[half]:
                    for u in range(TPG):
                        o = (w % 2) * TPG + u
                        c = (0, 1, 3)[w] * D
                        ins = nc.tensor.transpose(bank16(7)[:, o * P:(o + 1) * P],
                                                  QTS[:, u, :, :].rearrange("p a n -> p (a n)")[:, c:c + P], ident16[:, :])
                ins.then_inc(a_tq, 1)

            def run(b, g, i6, n, p2, p1, first=False, last=False):
                gi = b * NG + g
                n2 = gi * NT + i6 * 6
                v0 = gi * NG + i6 * 2
                n1 = (gi + p1) * NT + i6 * 6 if p1 is not None else 0
                for k in range(n):
                    if p2:
                        qk(b, g, i6 * 6 + k, k, n2 + k)
                    if p1 is not None:
                        mx(b, g + p1, i6 * 2 + k // 3, k % 3, n1 + k)
                    if p2 and k == 1 and not first:
                        pv(n2 - 2, v0, 4, 1, False)
                    if p2 and k in (3, 5):
                        if first and k == 3:
                            pe.wait_ge(a_ot, gi + 1)
                        pv(n2 + k - 3, v0 + 1 + (k - 2) // 3, k - 3, 1, first and k == 3)
                if p2 and last:
                    pv(n2, v0 + 1, 0, 1, False)
                    pv(n2 + 2, v0 + 1, 2, 0, False)

            def step(b, g, p1, pr, before=True):
                gi = b * NG + g
                pe.wait_ge(a_qt, gi * 2 + 3)
                run(b, g, 0, 6, True, p1, first=True)
                if before:
                    fin(gi - 1)
                if pr is not None:
                    prep(gi + pr, 0)
                with pe.Fori(1, 3) as i6:
                    run(b, g, i6, 6, True, p1)
                if pr is not None:
                    prep(gi + pr, 1)
                with pe.Fori(3, 5) as i6:
                    run(b, g, i6, 6, True, p1)
                run(b, g, 5, 3, True, p1, last=True)

            for b in range(B):
                for g in range(2):
                    with pe.Fori(0, 5) as i6:
                        run(b, 0, i6, 6, False, g)
                    run(b, 0, 5, 3, False, g)
                    if g == 0:
                        prep(b * NG, 0, nofin=b == 0)
                        prep(b * NG, 1)
                step(b, 0, 2, 1, before=b > 0)
                with pe.Fori(1, NG - 2) as g:
                    step(b, g, 2, 1)
                step(b, NG - 2, None, 1)
                step(b, NG - 1, None, None)
            fin(GT - 1)
            b_pe(pe)
            bo_pe(pe)
            f_pe(pe)
            s_pe(pe)
            g_pe(pe)

        @block.scalar
        def _(act):
            s_parameters_act(act)
            act.wait_ge(t_in, 5 * 16)
            act.wait_ge(c_id, 1)
            nc.scalar.activation(bns[:, 0:1], bnp[:, 4:5], ACT.Sqrt, bias=epsc[0:B * CR, 0:1]).then_inc(t_std, 1)
            act.wait_ge(t_bn, 1)
            for r in range(IMG // RG):
                act.wait_ge(t_y, r + 1)
                if r >= 2:
                    act.wait_ge(t_w, (r - 1) * TAPS)
                nc.scalar.activation(yv[:, r % 2, :], PS[0:B * CR, r % 2, :], ACT.Relu, bias=bns[:, 3:4],
                                     scale=bns[:, 1:2]).then_inc(t_ys, 1)
            act.wait_ge(ln_var, 1)
            nc.scalar.activation(stat[:, 2, :], stat[:, 1, :], ACT.Sqrt, bias=epsc[:, 0:1], scale=1.0 / D).then_inc(ln_std, 1)
            prepare_act(act, x_t, x_w, D, a_q, a_qe, Q2)
            for c in range(NCH):
                stack_copies(act, c, a_qpt, a_qp, QP)
            act.sem_inc(a_ex, 3)
            act.sem_inc(a_qt, 1)

            def prep(gi, g, half):
                act.wait_ge(a_tq, gi * 2 + half + 1)
                ws = ((0, 2), (2, 3))[half]
                k = ws[1] - ws[0]
                nc.scalar.copy(QT[:, ws[0]:ws[1], bass.ds(g * GW, GW)],
                               bank16(7)[:, 0:k * GW].rearrange("p (w n) -> p w n", w=k)).then_inc(a_qt, 1)

            def run(gi, i6, n, need):
                for k in range(n):
                    n2 = gi * NT + i6 * 6 + k
                    act.wait_ge(a_s2, n2 + 1)
                    if k % 2 == 0:
                        act.wait_ge(a_pv, gi * NPAIR + i6 * 3 + need[k // 2] + 2)
                    nc.scalar.activation(PT[:, k, :], PS[:, k % 3, 0:GW], ACT.Exp).then_inc(a_ex, 1)

            def step(b, g, pr):
                gi = b * NG + g
                run(gi, 0, 6, (-1, 0, 0))
                if pr is not None:
                    prep(gi + pr, g + pr, 0)
                with act.Fori(1, 3) as i6:
                    run(gi, i6, 6, (-2, -1, 0))
                if pr is not None:
                    prep(gi + pr, g + pr, 1)
                with act.Fori(3, 5) as i6:
                    run(gi, i6, 6, (-2, -1, 0))
                run(gi, 5, 3, (-2, -1))

            for b in range(B):
                prep(b * NG, 0, 0)
                prep(b * NG, 0, 1)
                with act.Fori(0, NG - 2) as g:
                    step(b, g, 1)
                step(b, NG - 2, 1)
                step(b, NG - 1, None)
            act.wait_ge(ln_var, 2)
            nc.scalar.activation(stat[:, 2, :], stat[:, 1, :], ACT.Sqrt, bias=epsc[:, 0:1], scale=1.0 / D).then_inc(ln_std, 1)
            b_act(act)
            bo_act(act)
            f_act(act)
            s_act(act)
            g_act(act)

        @block.gpsimd
        def _(pool):
            for r in range(IMG // RG):
                acc = conv[:, r * 512:(r + 1) * 512]
                for k in range(1, TAPS):
                    n = r * (TAPS - 1) + k - 1
                    pool.wait_ge(t_p, r * TAPS + k + 1)
                    if n:
                        pool.wait_ge(t_a, n)
                    nc.gpsimd.tensor_tensor(acc, acc, tapp[:, n % SLOT, :], ALU.add).then_inc(t_a, 1)

            def stage(gi, b, i6, t, need):
                pool.wait_ge(x_str, NCH)
                pool.wait_ge(a_pv, gi * NPAIR + i6 * 3 + need + 2)
                j = bass.ds(b * NT + i6 * 6 + 3 * t, 3)
                nc.gpsimd.tensor_tensor(VS[:, 3 * t:3 * t + 3, :], VA[:, j, :],
                                        valid[:, j].unsqueeze(2).to_broadcast([P, TPG, D]), ALU.mult).then_inc(a_vs, 1)

            for b in range(B):
                with pool.Fori(0, NG) as g:
                    gi = b * NG + g
                    stage(gi, b, 0, 0, 0)
                    stage(gi, b, 0, 1, 0)
                    with pool.Fori(1, 5) as i6:
                        stage(gi, b, i6, 0, -1)
                        stage(gi, b, i6, 1, 0)
                    stage(gi, b, 5, 0, -1)
            b_pool(pool)
            f_pool(pool)
            s_tables(pool)
            g_pool(pool)
            s_pool(pool)

        @block.vector
        def _(dve):
            nc.vector.memset(epsc[:, 0:1], EPS)
            nc.vector.memset(epsc[:, 1:2], 1e-6)
            s_parameters(dve)
            dve.wait_ge(c_in, 3 * 16)
            nc.vector.tensor_copy(ident16[:, :], ident[:, :]).then_inc(c_id, 1)
            n_bn = [0]
            dve.wait_ge(t_std, 1)
            link(dve, t_ch, n_bn, nc.vector.reciprocal(bns[:, 0:1], bns[:, 0:1]))
            link(dve, t_ch, n_bn, nc.vector.tensor_tensor(bns[:, 1:2], bnp[:, 1:2], bns[:, 0:1], ALU.mult))
            link(dve, t_ch, n_bn, nc.vector.tensor_tensor(bns[:, 2:3], bnp[:, 0:1], bnp[:, 3:4], ALU.subtract))
            nc.vector.scalar_tensor_tensor(bns[:, 3:4], bns[:, 2:3], bns[:, 1:2], bnp[:, 2:3], ALU.mult,
                                           ALU.add).then_inc(t_bn, 1)
            for r in range(IMG // RG):
                for k in range(TAPS):
                    n = r * TAPS + k
                    m = r * (TAPS - 1) + k - 1
                    di, dj = k // 3, k % 3
                    dve.wait_ge(t_w, n + 1)
                    if k:
                        if m >= SLOT:
                            dve.wait_ge(t_a, m - SLOT + 1)
                        dst = tapp[:, m % SLOT, :]
                    else:
                        dst = conv[:, r * 512:(r + 1) * 512]
                    nc.vector.scalar_tensor_tensor(dst.rearrange("p (h w) -> p h w", w=IMG),
                                                   PS[:, 2 + n % 4, :].rearrange("p (h w) -> p h w", w=IMG), b2[:, k:k + 1],
                                                   x_pad[:, r * RG + di:r * RG + di + RG, dj:dj + IMG],
                                                   ALU.add, ALU.mult).then_inc(t_p, 1)
            n_a = [0]
            ch = lambda ins: link(dve, a_ch, n_a, ins)
            ch(nc.vector.tensor_reduce(qks[:, :], qk2[:, :, :], AX.X, ALU.add))
            ch(nc.vector.tensor_scalar(qks[:, :], qks[:, :], -1.0 / D, None, ALU.mult))
            ch(nc.vector.tensor_tensor(qkc[:, :, 0:D], qk2[:, :, :], qks[:, :].unsqueeze(2).to_broadcast([D, 2, D]), ALU.add))
            ch(nc.vector.tensor_copy(qkc[:, :, D:P], qkc[:, :, 0:D]))
            dve.wait_ge(a_m, 1)
            ch(nc.vector.tensor_scalar(mres[:, :], PS[:, 2, 0:D], float(D) ** -0.5, None, ALU.mult))
            split_w(dve, a_ch, n_a, mres[:, :], MS, a_ms, 1)
            dve.wait_ge(h_in, 10 * 16)
            layer_norm(dve, n_ln, ln_var)
            dve.wait_ge(ln_std, 1)
            link(dve, ln_ch, n_ln, nc.vector.reciprocal(stat[:, 3, :], stat[:, 2, :]))

            def a_normed(ch, tl):
                normed(ch, tl)
                ch(nc.vector.tensor_scalar(XN[:, tl, :], XN[:, tl, :], 1.0, None, ALU.add))
                ch(nc.vector.tensor_copy(VA[:, tl, :], XN[:, tl, :]))

            split_x(dve, n_ln, XN[:, :, :], Q2, x_str, None, a_normed)
            for c, (lo, hi) in enumerate(CHUNKS):
                tl = slice(2 * TPG * lo, 2 * TPG * hi)
                dve.wait_ge(a_qe, 2 * hi + 2)
                s = xstr.rearrange("p t (a n) -> p t a n", n=D)[:, tl, :, :]
                ch(nc.vector.tensor_copy(s[:, :, 0, :], Q2[:, tl, :]))
                ch(nc.vector.tensor_copy(s[:, :, 1, :], s[:, :, 0, :]))
                ch(nc.vector.tensor_tensor(XN[:, tl, :], Q2[:, tl, :], s[:, :, 0, :], ALU.subtract))
                ch(nc.vector.tensor_copy(s[:, :, 2, :], XN[:, tl, :]))
                nc.vector.tensor_copy(s[:, :, 3, :], s[:, :, 2, :]).then_inc(a_qstr, 1)

            dve.sem_inc(a_s1f, 3)
            dve.sem_inc(a_ot, 1)
            dve.sem_inc(a_o, 1)

            def maxima(gi, lo=0, hi=NG):
                with dve.Fori(lo, hi) as jj:
                    for u in range(TPG):
                        dve.wait_ge(a_s1, gi * NT + jj * TPG + u + 1)
                        nc.vector.tensor_reduce(MX[:, u, bass.ds(jj, 1)], PS[:, 3 + u, 0:GW], AX.X, ALU.max).then_inc(a_s1f, 1)

            CH = 7

            def prep(gi, g, b):
                k = [gi * CH]

                def chn(ins):
                    ins.then_inc(a_pc, 1)
                    k[0] = k[0] + 1
                    dve.wait_ge(a_pc, k[0])

                dve.wait_ge(a_s1f, (gi + 1) * NT + 3)
                chn(nc.vector.tensor_reduce(mm[:, 0, :], MX[:, :, :], AX.X, ALU.max))
                chn(nc.vector.tensor_scalar(mm[:, 1, :], mm[:, 0, :], -1.0 / D, None, ALU.mult))
                chn(nc.vector.tensor_tensor(qtm[:, :, :], Q2[:, bass.ds(gi * TPG, TPG), :],
                                            mm[:, 1, :].unsqueeze(2).to_broadcast([P, TPG, D]), ALU.add))
                dve.wait_ge(a_tq, gi * 2)
                chn(nc.vector.tensor_copy(QTS[:, :, 0:2, :], qtm[:, :, :].unsqueeze(2).to_broadcast([P, TPG, 2, D])))
                chn(nc.vector.tensor_tensor(qtm[:, :, :], qtm[:, :, :], QTS[:, :, 0, :], ALU.subtract))
                chn(nc.vector.tensor_copy(QTS[:, :, 3:5, :], qtm[:, :, :].unsqueeze(2).to_broadcast([P, TPG, 2, D])))
                chn(nc.vector.tensor_tensor(qtm[:, :, :], qtm[:, :, :], QTS[:, :, 3, :], ALU.subtract))
                nc.vector.tensor_copy(QTS[:, :, 2, :], qtm[:, :, :]).then_inc(a_str, 1)

            def keep(gi):
                dve.wait_ge(a_pv, (gi + 1) * NPAIR + 2)
                dve.wait_ge(a_ft, gi) if isinstance(gi, int) and gi else None
                nc.vector.tensor_copy(OT[:, :], PS[:, 6, 0:GW]).then_inc(a_ot, 1)

            FC = 5

            def fin(gi):
                O = PS[:, 7, 0:GW].rearrange("p (t n) -> p t n", n=P)
                k = [gi * FC]

                def chf(ins):
                    ins.then_inc(o_ch, 1)
                    k[0] = k[0] + 1
                    dve.wait_ge(o_ch, k[0])

                dve.wait_ge(a_o, gi + 1)
                dve.wait_ge(a_ft, gi + 1)
                chf(nc.vector.tensor_reduce(orec[:, :], O, AX.X, ALU.add))
                chf(nc.vector.tensor_scalar(orec[:, :], orec[:, :], 1.0 / D, None, ALU.mult))
                chf(nc.vector.reciprocal(orec[:, :], orec[:, :]))
                r = orec[:, :].unsqueeze(2).to_broadcast([P, TPG, P])
                chf(nc.vector.tensor_tensor(ot[:, :, :], O, r, ALU.mult))
                chf(nc.vector.tensor_tensor(ot[:, :, 0:D], ot[:, :, 0:D], ot[:, :, D:P], ALU.add))
                hv = H[:, bass.ds(gi * TPG, TPG), :]
                nc.vector.scalar_tensor_tensor(hv, ot[:, :, 0:D], -1.0, hv, ALU.add, ALU.add).then_inc(a_o, 1)

            def step(b, g, p1, pr, before=True):
                gi = b * NG + g
                if pr is not None:
                    prep(gi + pr, g + pr, b)
                if p1 is not None:
                    maxima(gi + p1, 0, 2)
                if before:
                    fin(gi - 1)
                if p1 is not None:
                    maxima(gi + p1, 2, NG)
                keep(gi)

            for b in range(B):
                gb = b * NG
                maxima(gb)
                prep(gb, 0, b)
                maxima(gb + 1)
                step(b, 0, 2, 1, before=b > 0)
                with dve.Fori(1, NG - 2) as g:
                    step(b, g, 2, 1)
                step(b, NG - 2, None, 1)
                step(b, NG - 1, None, None)
            fin(GT - 1)
            b_dve(dve)
            bo_dve(dve)
            f_dve(dve)
            s_dve(dve)
            g_dve(dve)


def selection(rows, tiles):
    s = np.zeros((3, 8, tiles * P), np.float32)
    for e in range(8):
        s[:, e, e * rows:(e + 1) * rows] = 1.0
    return s.reshape(24, tiles * P)


def f_layout(L, f):
    hid = int(8 / 3 * D)
    tiles = -(-8 * hid // P)
    pad = tiles * P - 8 * hid
    first = 9 - np.arange(1, 9, dtype=np.float32)
    for n in ("w1", "w3"):
        w = f("L0_ffn_" + n).reshape(8 * hid, D).T
        L["f_" + n] = np.tile(np.pad(w, ((0, 0), (0, pad))), (2, 1))
    w2 = np.pad(f("L0_ffn_w2").transpose(0, 2, 1).reshape(8 * hid, D), ((0, pad), (0, 0)))
    L["f_w2"] = w2.reshape(tiles, P, D).transpose(1, 0, 2)
    L["f_sel"] = selection(hid, tiles)
    r = np.concatenate([f("L0_ffn_router_w").T, f("L0_ffn_ln2_w")[:, None], np.tile(first, (D, 1))], axis=1)
    L["f_r"] = np.tile(r, (2, 1))


def _layout(i):
    f = lambda n: np.ascontiguousarray(np.asarray(i[n], dtype=np.float32))
    L = {}
    x = f("x").reshape(B * D, IMG, IMG)
    L["xpad"] = np.pad(x, ((0, 0), (1, 1), (1, 1)))
    w1, w2 = f("L0_tok_conv1_w"), f("L0_tok_conv2_w")
    c1 = np.zeros((B * D, B * CR), np.float32)
    c2 = np.zeros((B * CR, TAPS, B * D), np.float32)
    for b in range(B):
        c1[b * D:(b + 1) * D, b * CR:(b + 1) * CR] = w1.T
        c2[b * CR:(b + 1) * CR, :, b * D:(b + 1) * D] = w2.T[:, :, None]
    L["c1w"], L["c2w"] = c1, c2
    L["bnp"] = np.tile(np.stack([f("L0_tok_conv1_b"), f("L0_tok_bn_gamma"), f("L0_tok_bn_beta"), f("L0_tok_bn_mean"),
                                 f("L0_tok_bn_var")], axis=1), (B, 1))
    L["b2"] = np.tile(f("L0_tok_conv2_b")[None, :], (P, 1))
    L["cls"] = f("cls_tok").reshape(1, D)
    L["qk"] = np.stack([f("L0_attn_Wq"), f("L0_attn_Wk")], axis=1)
    L["ident"] = np.eye(P, dtype=np.float32)
    twice = lambda w: np.tile(w.T, (2, 1))
    L["wqkv"] = np.concatenate([twice(f("L0_ffn_wq")), twice(f("L0_ffn_wk")), twice(f("L0_ffn_wv"))], axis=1)
    L["wo"] = twice(f("L0_ffn_wo"))
    L["lnw"] = np.tile(np.stack([f("L0_ffn_ln1_w"), f("L0_ffn_ln2_w")], axis=1), (2, 1))
    inv = 1.0 / 10000.0 ** (np.arange(0, 16, 2, dtype=np.float32) / 16)
    ang = np.outer(np.arange(NP, dtype=np.float32), inv)
    L["rope"] = np.stack([np.cos(ang), np.sin(ang)]).astype(np.float32).reshape(2, NT, P, 8).transpose(2, 0, 1, 3)
    L["neg"] = np.triu(np.full((P, P), BIG), 1).astype(np.float32)
    t = (np.arange(TT)[None, :] % NT) * P + np.arange(P)[:, None]
    f_layout(L, f)
    tiles = 8 * F1 // P
    L["g_w1"] = np.tile(f("L1_ffn_w1").transpose(1, 0, 2).reshape(D, 8 * F1), (2, 1))
    L["g_w2"] = f("L1_ffn_w2").reshape(tiles, P, D).transpose(1, 0, 2)
    L["g_b1"] = f("L1_ffn_b1").reshape(tiles, P).T
    L["g_b2"] = np.tile(f("L1_ffn_b2"), (3, 1))
    L["g_bias"] = np.tile(f("L1_ffn_gate_b")[None, :], (P, 1))
    L["g_sel"] = selection(F1, tiles)
    L["g_r"] = np.tile(np.concatenate([f("L1_ffn_gate_w"), np.zeros((D, 1), np.float32),
                                       np.tile(8 - np.arange(8, dtype=np.float32), (D, 1))], axis=1), (2, 1))
    L["upto"] = np.triu(np.ones((P, P), np.float32))
    up = np.repeat([1.0, 0.0], D).astype(np.float32)
    lam = [np.tile(f("L1_attn_" + n), 2) for n in ("Lambda_re", "Lambda_im", "log_step")]
    L["lam"] = np.stack(lam + [up, 1 - up], axis=1)
    L["s_b"] = np.tile(np.stack([f("L1_attn_B_re"), f("L1_attn_B_im")], axis=1), (2, 1, 1))
    cr, ci = f("L1_attn_C_re").T, f("L1_attn_C_im").T
    L["s_c"] = np.stack([np.concatenate([cr, ci]), np.concatenate([ci, cr])], axis=1)
    L["valid"] = (t < N).astype(np.float32)
    return {k: np.ascontiguousarray(v) for k, v in L.items()}


def kernel(**inputs):
    import concourse.bacc as _bacc
    from concourse import mybir as _mybir
    from concourse.bass_utils import run_bass_kernel_spmd as _run

    nc = _bacc.Bacc("TRN2", target_bir_lowering=False, num_devices=1)
    arrays = {"in_" + k: v for k, v in _layout(inputs).items()}
    I = {k[3:]: nc.dram_tensor(k, v.shape, _mybir.dt.from_np(v.dtype), kind="ExternalInput").ap() for k, v in arrays.items()}
    out = nc.dram_tensor("out_h", (B, N, D), _mybir.dt.float32, kind="ExternalOutput").ap()
    tower(nc, I, out)
    r = _run(nc, [arrays], core_ids=[0])
    return r.results[0]["out_h"]
```

```python
from contextlib import ExitStack

import numpy as np

import concourse.bass as bass
from concourse import mybir

F32 = mybir.dt.float32
BF16 = mybir.dt.bfloat16
ALU = mybir.AluOpType
ACT = mybir.ActivationFunctionType
AX = mybir.AxisListType

P = 128
B = 2
D = 64
IMG = 64
TAPS = 9
CR = 16
N = IMG * IMG + 1
TPG = 3
GW = TPG * P
NG = -(-N // GW)
NT = NG * TPG
NP = NT * P
GT = B * NG
TT = B * NT
TOK = B * NP
EPS = 1e-5
BIG = -1e30
F1 = 256


class Stage:
    pass


def tower(nc, I, out):
    ctx = ExitStack()
    with ctx:
        def sb(name, shape, dt=F32):
            return ctx.enter_context(nc.sbuf_tensor(name, shape, dt))

        def sem(name):
            return ctx.enter_context(nc.semaphore(name))

        scratch = nc.dram_tensor("tokens_scratch", (B, IMG * IMG, D), F32, kind="Internal").ap()

        PS = ctx.enter_context(nc.psum_tensor("PS", [P, 8, 512], F32))

        def bank16(k):
            return PS[:, k, :].bitcast(BF16)

        H = sb("H", [P, TT, D])
        XN = sb("XN", [P, TT, D])
        stat = sb("stat", [P, 4, TT])
        A0 = sb("A0", [P, TT * 256], BF16)
        A1 = sb("A1", [P, 2 * TOK], BF16)
        A2 = sb("A2", [P, 2 * TOK], BF16)
        A3 = sb("A3", [P, TT * 65])
        A4 = sb("A4", [P, TT * D])
        ident = sb("ident", [P, P])
        ident16 = sb("ident16", [P, P], BF16)
        valid = sb("valid", [P, TT])
        epsc = sb("epsc", [P, 2])

        xstr = A0[:, :].rearrange("p (t n) -> p t n", n=256)
        W = A1[:, :].rearrange("p (w n) -> p w n", w=2)

        A5 = sb("A5", [P, 4 * NP], BF16)

        def places(arena, start):
            at = [start]

            def place(shape, dt=F32):
                n = int(np.prod(shape[1:])) * (2 if dt is F32 else 1)
                at[0] += at[0] % 2
                v = arena[0:shape[0], at[0]:at[0] + n]
                at[0] += n
                assert at[0] <= arena.shape[1], (at[0], arena.shape)
                v = v.bitcast(F32) if dt is F32 else v
                names = "abcd"[:len(shape) - 1]
                if len(shape) > 2:
                    v = v.rearrange("p (%s) -> p %s" % (" ".join(names), " ".join(names)), **dict(zip(names[1:], shape[2:])))
                return v
            return place

        early = places(A5, 0)
        n_ln = [0]
        n_pool = [0]
        p_ch = sem("pool_chain")

        c_in = sem("constants_loaded")
        c_id = sem("ident16_ready")

        block = ctx.enter_context(nc.Block())

        x_pad = A1[:, 0:2 * 66 * 66].bitcast(F32).rearrange("p (h w) -> p h w", w=66)
        conv = A2[:, 0:2 * IMG * IMG].bitcast(F32)
        c1w = early([P, B * CR])
        bnp = early([B * CR, 5])
        bns = early([B * CR, 4])
        c2w = A3[:, 0:TAPS * P].rearrange("p (k n) -> p k n", k=TAPS)
        cx = places(XN[:, :, :].rearrange("p t n -> p (t n)").bitcast(BF16), 0)
        c2s = cx([P, 2, TAPS, P], BF16)
        ys = cx([P, 2, 512], BF16)
        y2 = cx([B * CR, 512], BF16)
        yr = cx([B * CR, 512])
        t_x0 = sem("first_rows_loaded")
        t_cw = sem("tap_weights_ready")
        t_r1 = sem("conv1_first_rest")
        t_y2 = sem("conv1_second_part")
        t_r2 = sem("conv1_second_rest")
        t_y3 = sem("conv1_parts")
        b2 = early([P, TAPS])
        yv = early([B * CR, 2, 512])
        tapp = early([P, 3, 512])
        t_in = sem("conv_inputs_loaded")
        t_std = sem("bn_std")
        t_bn = sem("bn_folded")
        t_y = sem("conv1_product")
        t_ys = sem("conv1_relu")
        t_w = sem("dynamic_weights")
        t_p = sem("tap_product")
        t_a = sem("tap_added")
        t_out = sem("conv_stored")
        h_in = sem("tokens_loaded")

        RG = 8
        SLOT = 3

        ln_ch = sem("vector_chain")
        ln_var = sem("ln_variance")
        ln_std = sem("ln_std")
        x_str = sem("x_strings")
        x_t = sem("x_transposed")
        x_w = sem("x_stacks")

        qk2 = early([D, 2, D])
        qkc = early([D, 2, P])
        qks = early([D, 2])
        MS = early([P, 3, D], BF16)
        mres = early([P, D])
        VA = XN
        qrest = A3[:, 0:TT * D].rearrange("p (t n) -> p t n", n=D)
        Q2 = A4[:, :].rearrange("p (t n) -> p t n", n=D)
        QP = A2[:, :].rearrange("p (w n) -> p w n", w=2)
        QT = A0[:, 0:3 * NP].rearrange("p (w n) -> p w n", w=3)
        MX = early([P, TPG, NG])
        mm = early([P, 2, TPG])
        qtm = early([P, TPG, D])
        QTS = early([P, TPG, 5, D], BF16)
        PT = early([P, 6, GW])
        VS = early([P, 6, D])
        OT = sb("OT", [P, GW])
        NPAIR = (NT + 1) // 2
        orec = early([P, TPG])
        ot = early([P, TPG, P])
        a_m = sem("a_projection_matrix")
        a_ms = sem("a_projection_stacks")
        a_ch = sem("a_chain")
        a_q = sem("a_queries_product")
        a_qe = sem("a_queries_kept")
        a_qstr = sem("a_query_strings")
        a_qpt = sem("a_query_transposed")
        a_qp = sem("a_query_stacks")
        a_s1 = sem("a_max_scores")
        a_s1f = sem("a_max_scores_read")
        a_str = sem("a_shifted_strings")
        a_tq = sem("a_shifted_transposed")
        a_qt = sem("a_shifted_stacks")
        a_s2 = sem("a_scores")
        a_ex = sem("a_exponentials")
        a_pv = sem("a_value_products")
        a_vs = sem("a_values_staged")
        a_ot = sem("a_output_kept")
        a_ft = sem("a_output_transposed")
        a_o = sem("a_output_added")
        a_pc = sem("a_prep_chain")
        o_out = sem("output_stored")
        o_ch = sem("a_output_chain")


        def b3(ap, n):
            return ap.unsqueeze(2).to_broadcast([P, ap.shape[1], n])

        CHUNKS = [(0, 2), (2, 5), (5, 8), (8, GT // 2)]
        NCH = len(CHUNKS)

        def transposes(pe, c, ready, done, freed, strings=None):
            pe.wait_ge(ready, c + 1)
            pe.wait_ge(c_id, 1)
            with pe.Fori(*CHUNKS[c]) as i:
                for h in range(2):
                    pe.wait_ge(freed, i * 2 + h + 1)
                    for w in range(2):
                        for u in range(TPG):
                            ins = nc.tensor.transpose(bank16(6 + h)[:, (w * TPG + u) * P:(w * TPG + u + 1) * P],
                                                      (xstr if strings is None else strings)[:, bass.ds((i * 2 + h) * TPG + u, 1),
                                                                                             w * P:(w + 1) * P],
                                                      ident16[:, :])
                    ins.then_inc(done, 1)

        def stack_copies(act, c, done, freed, dst):
            if c == 0:
                act.sem_inc(freed, 2)
            with act.Fori(*CHUNKS[c]) as i:
                for h in range(2):
                    act.wait_ge(done, i * 2 + h + 1)
                    nc.scalar.copy(dst[:, :, bass.ds((i * 2 + h) * GW, GW)],
                                   bank16(6 + h)[:, 0:2 * GW].rearrange("p (w n) -> p w n", w=2)).then_inc(freed, 1)

        def link(e, s, count, ins):
            count[0] += 1
            ins.then_inc(s, 1)
            e.wait_ge(s, count[0])

        chunk_tiles = [slice(2 * TPG * lo, 2 * TPG * hi) for lo, hi in CHUNKS]
        NORM_A, NORM_B, NORM_B2, NORM_F, NORM_S, NORM_G = range(6)
        EV = NCH + 1

        def square_sums(dve, which, first):
            for tl in chunk_tiles:
                if first is None:
                    dve.sem_inc(ln_var, 1)
                else:
                    first(tl).then_inc(ln_var, 1)
            for c, tl in enumerate(chunk_tiles):
                dve.wait_ge(ln_std, which * EV + c + 1)
                ins = nc.vector.tensor_reduce(stat[:, 1, tl], Q2[:, tl, :], AX.X, ALU.add)
            ins.then_inc(ln_var, 1)
            dve.wait_ge(ln_std, (which + 1) * EV)
            link(dve, ln_ch, n_ln, nc.vector.reciprocal(stat[:, 3, :], stat[:, 2, :]))

        def square_sums_act(act, which, eps):
            for c, tl in enumerate(chunk_tiles):
                act.wait_ge(ln_var, which * EV + c + 1)
                nc.scalar.activation(Q2[:, tl, :], XN[:, tl, :], ACT.Square).then_inc(ln_std, 1)
            act.wait_ge(ln_var, (which + 1) * EV)
            nc.scalar.activation(stat[:, 2, :], stat[:, 1, :], ACT.Sqrt, bias=epsc[:, eps:eps + 1], scale=1.0 / D).then_inc(ln_std, 1)

        def layer_norm(dve, which):
            ch = lambda ins: link(dve, ln_ch, n_ln, ins)

            def centred(tl):
                ch(nc.vector.tensor_reduce(stat[:, 0, tl], H[:, tl, :], AX.X, ALU.add))
                ch(nc.vector.tensor_scalar(stat[:, 0, tl], stat[:, 0, tl], -1.0 / D, None, ALU.mult))
                return nc.vector.tensor_tensor(XN[:, tl, :], H[:, tl, :], b3(stat[:, 0, tl], D), ALU.add)

            square_sums(dve, which, centred)

        def split_x(dve, count, src, res, ready, strings=None, first=None):
            ch = lambda ins: link(dve, ln_ch, count, ins)
            for c, (lo, hi) in enumerate(CHUNKS):
                tl = slice(2 * TPG * lo, 2 * TPG * hi)
                if first is not None:
                    first(ch, tl)
                s = (xstr if strings is None else strings).rearrange("p t (a n) -> p t a n", n=D)[:, tl, :, :]
                x, r = src[:, tl, :], res[:, tl, :]
                ch(nc.vector.tensor_copy(s[:, :, 0, :], x))
                ch(nc.vector.tensor_copy(s[:, :, 3, :], s[:, :, 0, :]))
                ch(nc.vector.tensor_tensor(r, x, s[:, :, 0, :], ALU.subtract))
                ch(nc.vector.tensor_copy(s[:, :, 1, :], r))
                ch(nc.vector.tensor_tensor(r, r, s[:, :, 1, :], ALU.subtract))
                nc.vector.tensor_copy(s[:, :, 2, :], r).then_inc(ready, 1)
                dve.wait_ge(ready, c + 1)

        def normed(ch, tl):
            x = XN[:, tl, :]
            ch(nc.vector.tensor_tensor(x, x, b3(stat[:, 3, tl], D), ALU.mult))

        def rms(ch, tl):
            ch(nc.vector.tensor_tensor(Q2[:, tl, :], XN[:, tl, :], b3(stat[:, 3, tl], D), ALU.mult))

        def split_w(dve, s, count, w, st, ready, value):
            ch = lambda ins: link(dve, s, count, ins)
            ch(nc.vector.tensor_copy(st[:, 0, :], w))
            ch(nc.vector.tensor_copy(st[0:D, 1, :], st[0:D, 0, :]))
            ch(nc.vector.tensor_tensor(w, w, st[:, 0, :], ALU.subtract))
            ch(nc.vector.tensor_copy(st[:, 2, :], w))
            ch(nc.vector.tensor_tensor(w, w, st[:, 2, :], ALU.subtract))
            nc.vector.tensor_copy(st[D:P, 1, :], w[D:P, :]).then_inc(ready, 1)
            dve.wait_ge(ready, value)

        def project(pe, c, stacks, n, done, freed):
            with pe.Fori(*CHUNKS[c]) as i:
                for h in range(2):
                    pe.wait_ge(freed, i * 2 + h + 1)
                    for u in range(TPG):
                        tile = bass.ds((i * 2 + h) * GW + u * P, P)
                        for k, w in enumerate((0, 1, 0)):
                            ins = nc.tensor.matmul(PS[:, 4 + h, u * n:(u + 1) * n], W[:, w, tile], stacks[:, k, :],
                                                   start=(k == 0), stop=(k == 2))
                    ins.then_inc(done, 1)

        def project_copies(act, c, n, done, freed, dst):
            if c == 0:
                act.sem_inc(freed, 2)
            with act.Fori(*CHUNKS[c]) as i:
                for h in range(2):
                    act.wait_ge(done, i * 2 + h + 1)
                    nc.scalar.copy(dst[:, bass.ds((i * 2 + h) * TPG, TPG), :],
                                   PS[:, 4 + h, 0:TPG * n].rearrange("p (t n) -> p t n", n=n)).then_inc(freed, 1)

        def prepare_pe(pe, ready, t, kept, weights, stacks, n, done, freed, strings=None):
            for c, (lo, hi) in enumerate(CHUNKS):
                transposes(pe, c, ready, t, kept, strings)
                pe.wait_ge(kept, 2 * hi + 2)
                if c == 0:
                    pe.wait_ge(*weights)
                project(pe, c, stacks, n, done, freed)

        def prepare_act(act, t, kept, n, done, freed, dst):
            for c in range(NCH):
                stack_copies(act, c, t, kept, W)
                if dst is not None:
                    project_copies(act, c, n, done, freed, dst)


        NH, NKV, HD = 4, 2, 16
        PARTS = 6
        KR = PARTS * HD
        HH = HD // 2
        UN = TPG * NH
        QKV = A2[:, :].bitcast(F32).rearrange("p (t n) -> p t n", n=P)
        late = places(A3[:, :].bitcast(BF16), 2 * TT * NKV * (HD + 1))
        QB = [A5[:, :].rearrange("p (h n) -> p h n", h=NH), A2[:, :].rearrange("p (h n) -> p h n", h=NH)]
        KB = A1[:, :].rearrange("p (h n) -> p h n", h=NKV)
        qs_ = A0[:, 0:NT * NH * KR].rearrange("p (x a n) -> p x a n", a=PARTS, n=HD)
        ks_ = A4[:, :].bitcast(BF16)[:, 0:NT * NKV * KR].rearrange("p (x a n) -> p x a n", a=PARTS, n=HD)
        def head_steps(b, g):
            if b == 0:
                return [(c, g * 3 + c) for c in range(3)]
            return [(0, NG * 3 + g * 2), (2, NG * 3 + g * 2 + 1)]

        last_steps = NG * 5
        HCH = [(g, min(g + 3, NG)) for g in range(0, NG, 3)]
        rt = A0[:, NT * NH * KR:NT * NH * KR + 8 * 9 * 48].bitcast(F32).rearrange("p (k t h n) -> p k t h n", k=4, t=9, n=HH)
        VB = A3[:, 0:TT * NKV * (HD + 1)].rearrange("p (t h n) -> p t h n", h=NKV, n=HD + 1)
        YB = A4[:, :].rearrange("p (t n) -> p t n", n=D)
        wf = late([P, P])
        lnw = late([P, 2])
        wqkv = late([P, 3, P], BF16)
        wof = late([P, D])
        wos = late([P, 3, D], BF16)
        cs = late([P, 2, NT, HH])
        neg = late([P, P])
        neg16 = late([P, P], BF16)
        MXB = late([P, UN, NG])
        mB = late([P, UN])
        mstr = late([P, UN, 3], BF16)
        MT = late([UN, GW], BF16)
        PB = A0[:, 0:2 * UN * GW].bitcast(F32).rearrange("p (k n) -> p k n", k=UN)
        VSB = sb("VSB", [P, TPG, NKV, HD + 1])
        obr = sb("obr", [P, TPG, NH])
        b_ystr = sem("b_output_strings")
        b_in = sem("b_weights_loaded")
        b_w = sem("b_weight_stacks")
        b_str = sem("b_strings")
        b_t = sem("b_transposed")
        b_st = sem("b_stacks")
        b_q = sem("b_qkv_product")
        b_qe = sem("b_qkv_kept")
        b_hs = sem("b_head_strings")
        b_ht = sem("b_heads_transposed")
        b_hk = sem("b_head_stacks")
        b_one = sem("b_ones_rows")
        b_s1 = sem("b_max_scores")
        b_s1f = sem("b_max_scores_read")
        b_s2 = sem("b_scores")
        b_ex = sem("b_exponentials")
        b_sel = sem("b_causal_selected")
        b_pv = sem("b_value_products")
        b_vs = sem("b_values_staged")
        b_ot = sem("b_output_kept")
        b_ft = sem("b_output_transposed_back")
        b_o = sem("b_output_scaled")
        b_oc = sem("b_output_chain")
        b_ms = sem("b_maximum_strings")
        b_mt = sem("b_maxima_transposed")
        b_mc = sem("b_maxima_copied")
        b_mr = sem("b_maximum_rows")

        order = [(0, g) for g in range(NG)] + [(1, g) for g in reversed(range(NG))]
        before = [UN * sum(g + 1 for _, g in order[:i]) for i in range(GT + 1)]
        LAG = 2

        def b_sp(sp):
            sp.wait_ge(a_o, GT + 1)
            sp.dma_start(wf[:, :], I["wqkv"]).then_inc(b_in, 16)
            sp.dma_start(wof[:, :], I["wo"]).then_inc(b_in, 16)
            sp.dma_start(lnw[:, :], I["lnw"]).then_inc(b_in, 16)
            sp.dma_start(cs[:, :, :, :], I["rope"]).then_inc(b_in, 16)
            sp.dma_start(neg[:, :], I["neg"]).then_inc(b_in, 16)

        def b_sp_rows(sp):
            for i, (b, g) in enumerate(order):
                sp.wait_ge(b_mc, i + 1)
                for h in range(NH):
                    sp.dma_start(QB[b][KR:KR + 3, h, g * GW:(g + 1) * GW], MT[3 * h:3 * h + 3, :]).then_inc(b_mr, 16)

        def b_pe(pe):
            pe.wait_ge(a_o, GT + 1)
            prepare_pe(pe, b_str, b_t, b_st, (b_w, 1), wqkv, P, b_q, b_qe)
            def heads(b, g, c, n, bank):
                pe.wait_ge(b_hk, n + 1)
                for y in range(2):
                    for u in range(TPG):
                        if c < 2:
                            src = qs_[:, bass.ds(g * UN + u * NH + 2 * c + y, 1), :, :]
                        else:
                            src = ks_[:, bass.ds(g * TPG * NKV + u * NKV + y, 1), :, :]
                        ins = nc.tensor.transpose(bank16(bank)[0:KR, (y * TPG + u) * P:(y * TPG + u + 1) * P],
                                                  src.rearrange("p x a n -> p (x a n)"), ident16[:, :])
                ins.then_inc(b_ht, 1)

            pe.wait_ge(b_qe, GT + 2)
            for b in range(B):
                for k, (lo, hi) in enumerate(HCH):
                    pe.wait_ge(b_hs, b * len(HCH) + k + 1)
                    with pe.Fori(lo, hi) as g:
                        for c, n in head_steps(b, g):
                            heads(b, g, c, n, c)
            for g in range(NG):
                heads(1, g, 1, last_steps + g, 1 - g % 2)
            pe.wait_ge(b_hk, B * NG * 3 + 2)
            pe.wait_ge(b_one, 2)
            pe.sem_inc(b_pv, 3)

            def qk(b, g, j, h, lo, k, n2):
                pe.wait_ge(b_ex, n2 + 1)
                nc.tensor.matmul(PS[:, k % 3, lo:GW], KB[0:KR + 3, h // 2, bass.ds(b * NP + j * P, P)],
                                 QB[b][0:KR + 3, h, g * GW + lo:(g + 1) * GW], start=True, stop=True).then_inc(b_s2, 1)

            def mx(b, g, a, h, key, width, k, n1):
                pe.wait_ge(b_s1f, n1 + 1)
                nc.tensor.matmul(PS[:, 3 + k % 3, 0:width], QB[b][0:KR, h, (g * TPG + a) * P:(g * TPG + a + 1) * P],
                                 KB[0:KR, h // 2, bass.ds(b * NP + key, width)], start=True, stop=True).then_inc(b_s1, 1)

            def triple(i, m, jj, first):
                b, g = order[i]
                n2 = before[i] + jj * UN
                q0 = before[i] // NH + jj * TPG
                for k in range(UN):
                    qk(b, g, jj * TPG + k // NH, k % NH, 0, k, n2 + k)
                    if m is not None:
                        mx(*order[m], k // NH, k % NH, jj * GW, GW, k, before[m] + jj * UN + k)
                    if k == 1 and not first:
                        pvq(n2 - UN, q0 - TPG, 2, 0, False)
                    if k == 5 and first:
                        pe.wait_ge(b_ot, i + 1)
                    if k in (5, 9):
                        pvq(n2, q0, k // NH - 1, 0, first and k == 5)

            def pvq(n2, q0, u, lo, first, sel=0):
                pe.wait_ge(b_ex, n2 + 4 * u + 4 + 3)
                pe.wait_ge(b_vs, q0 + u + 1)
                if sel:
                    pe.wait_ge(b_sel, sel)
                for h in range(NH):
                    ins = nc.tensor.matmul(PS[32 * h:32 * h + HD + 1, 6, lo:GW], VSB[:, u, h // 2, :], PB[:, NH * u + h, lo:GW],
                                           start=first, stop=True, skip_group_check=True)
                ins.then_inc(b_pv, 1)

            def maxima(m, lo, hi):
                if hi > lo:
                    with pe.Fori(lo, hi) as jj:
                        for k in range(UN):
                            mx(*order[m], k // NH, k % NH, jj * GW, GW, k, before[m] + jj * UN + k)

            def diagonal(i, m):
                for k in range(UN + 4):
                    u = k // NH
                    if k < UN and i is not None:
                        b, g = order[i]
                        qk(b, g, g * TPG + u, k % NH, u * P, k, before[i] + g * UN + k)
                    if k < UN and m is not None:
                        b, g = order[m]
                        n1, kh = before[m] + g * UN + k, k % NH // 2
                        tile = g * TPG + u
                        pe.wait_ge(b_s1f, n1 + 1)
                        nc.tensor.matmul(PS[:, 3 + k % 3, 0:(u + 1) * P], QB[b][0:KR, k % NH, tile * P:(tile + 1) * P],
                                         KB[0:KR, kh, b * NP + g * GW:b * NP + g * GW + (u + 1) * P],
                                         start=True, stop=True, skip_group_check=True)
                        nc.tensor.matmul(PS[:, 3 + k % 3, u * P:(u + 1) * P], ident16[:, :], neg16[:, :],
                                         start=False, stop=True, skip_group_check=True).then_inc(b_s1, 1)
                    if k in (5, 9, 13) and i is not None:
                        b, g = order[i]
                        u = k // NH - 1
                        if g == 0 and u == 0:
                            pe.wait_ge(b_ot, i + 1)
                        pvq(before[i] + g * UN, before[i] // NH + g * TPG, u, u * P, g == 0 and u == 0, i * UN + 4 * u + 4)

            def fin(i):
                pe.wait_ge(b_ot, i + 2)
                for a in range(TPG):
                    ins = nc.tensor.transpose(PS[:, 7, a * P:(a + 1) * P], OT[:, a * P:(a + 1) * P], ident[:, :])
                ins.then_inc(b_ft, 1)

            def prep(i):
                pe.wait_ge(b_ms, i + 1)
                if i:
                    pe.wait_ge(b_mc, i)
                if i > 1:
                    pe.wait_ge(b_o, i - 1)
                for a in range(TPG):
                    ins = nc.tensor.transpose(bank16(7)[0:UN, a * P:(a + 1) * P],
                                              mstr[:, a * NH:(a + 1) * NH, :].rearrange("p h n -> p (h n)"), ident16[:, :])
                ins.then_inc(b_mt, 1)

            diagonal(None, 0)
            prep(0)
            maxima(1, 0, order[1][1])
            diagonal(None, 1)
            for i, (b, g) in enumerate(order):
                m = i + LAG if i + LAG < GT else None
                gm = order[m][1] if m is not None else 0
                both = min(g, gm)
                pe.wait_ge(b_mr, 64 * (i + 1))
                if g:
                    triple(i, m if both else None, 0, True)
                if i:
                    fin(i - 1)
                if both > 1:
                    with pe.Fori(1, both) as jj:
                        triple(i, m, jj, False)
                if g > max(both, 1):
                    with pe.Fori(max(both, 1), g) as jj:
                        triple(i, None, jj, False)
                if g:
                    pvq(before[i] + (g - 1) * UN, before[i] // NH + (g - 1) * TPG, 2, 0, False)
                if i + 1 < GT:
                    prep(i + 1)
                if m is not None:
                    maxima(m, both, gm)
                diagonal(i, m)
            fin(GT - 1)

        def b_act(act):
            square_sums_act(act, NORM_B2, 1)
            prepare_act(act, b_t, b_st, P, b_q, b_qe, QKV)
            act.sem_inc(b_hk, 2)
            def heads(b, g, c, n, bank):
                act.wait_ge(b_ht, n + 1)
                if c < 2:
                    dst = QB[b][0:KR, 2 * c:2 * c + 2, bass.ds(g * GW, GW)]
                else:
                    dst = KB[0:KR, :, bass.ds(b * NP + g * GW, GW)]
                nc.scalar.copy(dst, bank16(bank)[0:KR, 0:2 * GW].rearrange("p (h n) -> p h n", h=2)).then_inc(b_hk, 1)

            for b in range(B):
                for lo, hi in HCH:
                    with act.Fori(lo, hi) as g:
                        for c, n in head_steps(b, g):
                            heads(b, g, c, n, c)
            for g in range(NG):
                heads(1, g, 1, last_steps + g, 1 - g % 2)
            act.sem_inc(b_ex, 3)

            def exps(n2, q0, lo=0):
                for k in range(UN):
                    act.wait_ge(b_s2, n2 + k + 1)
                    if k % NH == 0:
                        act.wait_ge(b_pv, q0 + k // NH + 1)
                    c = k // NH * P if lo else 0
                    nc.scalar.activation(PB[:, k, c:GW], PS[:, k % 3, c:GW], ACT.Exp).then_inc(b_ex, 1)

            def prep(i):
                act.wait_ge(b_mt, i + 1)
                if i:
                    act.wait_ge(b_mr, 64 * i)
                nc.scalar.copy(MT[:, :], bank16(7)[0:UN, 0:GW]).then_inc(b_mc, 1)

            prep(0)
            for i, (b, g) in enumerate(order):
                if g:
                    with act.Fori(0, g) as jj:
                        exps(before[i] + jj * UN, before[i] // NH + jj * TPG)
                if i + 1 < GT:
                    prep(i + 1)
                exps(before[i] + g * UN, before[i] // NH + g * TPG, 1)

        def b_pool(pool):
            pool.wait_ge(b_qe, GT + 2)
            nc.gpsimd.memset(KB[96:99, 0, :], 1.0).then_inc(b_one, 1)
            nc.gpsimd.memset(KB[96:99, 1, :], 1.0).then_inc(b_one, 1)

            def stage(b, j, u, q):
                pool.wait_ge(b_one, 2)
                pool.wait_ge(b_pv, q + u + 1)
                nc.gpsimd.tensor_copy(VSB[:, u:u + 1, :, :], VB[:, bass.ds(b * NT + j + u, 1), :, :]).then_inc(b_vs, 1)

            for i, (b, g) in enumerate(order):
                q0 = before[i] // NH
                if g:
                    with pool.Fori(0, g) as jj:
                        for u in range(TPG):
                            stage(b, jj * TPG, u, q0 + jj * TPG)
                for k in range(UN):
                    if k % NH == 0:
                        stage(b, g * TPG, k // NH, q0 + g * TPG)
                    pool.wait_ge(b_ex, before[i] + g * UN + k + 4)
                    c = k // NH * P
                    v = PB[:, k, c:c + P]
                    nc.gpsimd.affine_select(out=v, in_=v, compare_op=ALU.is_ge, fill=0.0, base=0,
                                            pattern=[[1, P]], channel_multiplier=-1).then_inc(b_sel, 1)

        def b_dve(dve):
            dve.wait_ge(a_o, GT + 1)
            dve.wait_ge(b_in, 5 * 16)
            ch = lambda ins: link(dve, ln_ch, n_ln, ins)
            ch(nc.vector.tensor_copy(neg16[:, :], neg[:, :]))
            ch(nc.vector.tensor_scalar(wf[:, :], wf[:, :], lnw[:, 0:1], None, ALU.mult))
            ch(nc.vector.tensor_scalar(wf[:, 0:D], wf[:, 0:D], float(HD) ** -0.5, None, ALU.mult))
            split_w(dve, ln_ch, n_ln, wf[:, :], wqkv, b_w, 1)
            split_w(dve, ln_ch, n_ln, wof[:, :], wos, b_w, 2)
            layer_norm(dve, NORM_B)
            square_sums(dve, NORM_B2, lambda tl: nc.vector.tensor_tensor(XN[:, tl, :], XN[:, tl, :], b3(stat[:, 3, tl], D), ALU.mult))
            split_x(dve, n_ln, Q2, Q2, b_str, None, rms)
            ch = lambda ins: link(dve, ln_ch, n_ln, ins)
            ch(nc.vector.memset(VB[:, :, :, :], 1.0))
            dve.wait_ge(b_st, GT + 2)
            for b in range(B):
                dve.wait_ge(b_qe, (b + 1) * NG + 2)
                tb = slice(b * NT, (b + 1) * NT)
                ch(nc.vector.tensor_copy(VB[:, tb, :, 0:HD], QKV[:, tb, 96:128].rearrange("p t (h n) -> p t h n", h=NKV)))
                for c, (g0, g1) in enumerate(HCH):
                    if b:
                        dve.wait_ge(b_hk, g1 * 3 + 2)
                    t0, t1 = g0 * TPG, g1 * TPG
                    n = t1 - t0
                    v = QKV[:, b * NT + t0:b * NT + t1, 0:96].rearrange("p t (h c n) -> p t h c n", c=2, n=HH)
                    lo, hi = v[:, :, :, 0, :], v[:, :, :, 1, :]
                    co = cs[:, 0, t0:t1, :].unsqueeze(2).to_broadcast([P, n, NH + NKV, HH])
                    si = cs[:, 1, t0:t1, :].unsqueeze(2).to_broadcast([P, n, NH + NKV, HH])
                    ch(nc.vector.tensor_tensor(rt[:, 0, 0:n, :, :], lo, co, ALU.mult))
                    ch(nc.vector.tensor_tensor(rt[:, 1, 0:n, :, :], hi, si, ALU.mult))
                    ch(nc.vector.tensor_tensor(rt[:, 2, 0:n, :, :], hi, co, ALU.mult))
                    ch(nc.vector.tensor_tensor(rt[:, 3, 0:n, :, :], lo, si, ALU.mult))
                    ch(nc.vector.tensor_tensor(lo, rt[:, 0, 0:n, :, :], rt[:, 1, 0:n, :, :], ALU.subtract))
                    ch(nc.vector.tensor_tensor(hi, rt[:, 2, 0:n, :, :], rt[:, 3, 0:n, :, :], ALU.add))
                    for z, (all_, c0, nh, where) in enumerate(((qs_, 0, NH, ((0, 1, 2), (3, 4), (5,))),
                                                               (ks_, D, NKV, ((0, 3, 5), (1, 4), (2,))))):
                        st = all_[:, t0 * nh:t1 * nh, :, :]
                        x = QKV[:, b * NT + t0:b * NT + t1, c0:c0 + nh * HD].rearrange("p t (h n) -> p t h n", n=HD)
                        for part, at in enumerate(where):
                            first = st[:, :, at[0], :].rearrange("p (t h) n -> p t h n", h=nh)
                            ins = nc.vector.tensor_copy(first, x)
                            if z == 1 and part == 2:
                                ins.then_inc(b_hs, 1)
                                dve.wait_ge(b_hs, b * len(HCH) + c + 1)
                            else:
                                ch(ins)
                            for k in at[1:]:
                                ch(nc.vector.tensor_copy(st[:, :, k, :], st[:, :, at[0], :]))
                            if part < 2:
                                ch(nc.vector.tensor_tensor(x, x, first, ALU.subtract))
            dve.wait_ge(b_hk, B * NG * 3 + 2)
            dve.sem_inc(b_s1f, 3)
            dve.sem_inc(b_ot, 1)

            def reduce_max(m, k, at, n1, width):
                dve.wait_ge(b_s1, n1 + k + 1)
                nc.vector.tensor_reduce(MXB[:, k, at], PS[:, 3 + k % 3, 0:width], AX.X, ALU.max).then_inc(b_s1f, 1)

            def maxima(m, lo, hi):
                if hi > lo:
                    with dve.Fori(lo, hi) as jj:
                        for k in range(UN):
                            reduce_max(m, k, bass.ds(jj, 1), before[m] + jj * UN, GW)

            def diagonal(m):
                g = order[m][1]
                for k in range(UN):
                    reduce_max(m, k, slice(g, g + 1), before[m] + g * UN, (k // NH + 1) * P)

            def prep(i, steps):
                g = order[i][1]
                for k in steps:
                    if k == 0:
                        dve.wait_ge(b_s1f, before[i + 1] + 3)
                        ins = nc.vector.tensor_reduce(mB[:, :], MXB[:, :, 0:g + 1], AX.X, ALU.max, negate=True)
                    else:
                        dve.wait_ge(ln_ch, n_ln[0])
                        if k == 1 and i:
                            dve.wait_ge(b_mt, i)
                        if k % 2:
                            ins = nc.vector.tensor_copy(mstr[:, :, k // 2], mB[:, :])
                        else:
                            ins = nc.vector.tensor_tensor(mB[:, :], mB[:, :], mstr[:, :, k // 2 - 1], ALU.subtract)
                    if k < 5:
                        n_ln[0] += 1
                    ins.then_inc(ln_ch if k < 5 else b_ms, 1)

            def keep(i):
                dve.wait_ge(b_pv, before[i + 1] // NH + 3)
                nc.vector.tensor_copy(OT[:, :], PS[:, 6, 0:GW]).then_inc(b_ot, 1)

            def fin(i):
                b, g = order[i]
                t = (b * NG + g) * TPG
                O = PS[:, 7, 0:GW].rearrange("p (t h n) -> p t h n", h=NH, n=32)
                dve.wait_ge(b_ft, i + 1)
                nc.vector.reciprocal(obr[:, :, :], O[:, :, :, HD]).then_inc(b_oc, 1)
                dve.wait_ge(b_oc, i + 1)
                nc.vector.tensor_tensor(YB[:, t:t + TPG, :].rearrange("p t (h n) -> p t h n", h=NH), O[:, :, :, 0:HD],
                                        obr[:, :, :].unsqueeze(3).to_broadcast([P, TPG, NH, HD]), ALU.mult).then_inc(b_o, 1)
                dve.wait_ge(b_o, i + 1)

            diagonal(0)
            prep(0, range(6))
            maxima(1, 0, order[1][1])
            diagonal(1)
            for i, (b, g) in enumerate(order):
                m = i + LAG if i + LAG < GT else None
                gm = order[m][1] if m is not None else 0
                ahead = min(g, gm, 1)
                if ahead:
                    for k in range(UN):
                        if k < 6:
                            prep(i + 1, (k,))
                        if k == 0:
                            dve.wait_ge(ln_ch, n_ln[0])
                        reduce_max(m, k, slice(0, 1), before[m], GW)
                elif i + 1 < GT:
                    prep(i + 1, range(6))
                if i:
                    fin(i - 1)
                if m is not None:
                    maxima(m, ahead, gm)
                    diagonal(m)
                keep(i)
            fin(GT - 1)
            split_x(dve, n_ln, YB, YB, b_ystr)


        b_yt = sem("b_output_transposed")
        b_yst = sem("b_output_stacks")
        b_yp = sem("b_output_product")
        b_yk = sem("b_output_added")

        def bo_pe(pe):
            prepare_pe(pe, b_ystr, b_yt, b_yst, (b_w, 2), wos, D, b_yp, b_yk)

        def bo_act(act):
            prepare_act(act, b_yt, b_yst, D, None, None, None)

        def bo_dve(dve):
            dve.sem_inc(b_yk, 2)
            with dve.Fori(0, GT // 2) as i:
                for h in range(2):
                    dve.wait_ge(b_yp, i * 2 + h + 1)
                    x = XN[:, bass.ds((i * 2 + h) * TPG, TPG), :]
                    nc.vector.tensor_tensor(x, PS[:, 4 + h, 0:TPG * D].rearrange("p (t n) -> p t n", n=D), x,
                                            ALU.add).then_inc(b_yk, 1)
            dve.wait_ge(b_yk, GT + 2)

        NE = 8
        WR = 3 * NE
        RN = 8
        S2 = A2[:, :].rearrange("p (t n) -> p t n", n=256)

        def experts(tag, HT, ring, gated, place_w, place_r, place_t, hh, raw):
            m = Stage()
            m.HT, m.ring, m.gated, m.hh = HT, ring, gated, hh
            m.PP, m.CR = (HT + 1) // 2, (ring + 1) // 2
            m.inp = sem(tag + "_weights_loaded")
            m.raw_in = sem(tag + "_selection_loaded")
            m.wst = sem(tag + "_weight_stacks")
            m.rsp = sem(tag + "_router_stacks")
            m.str = sem(tag + "_strings")
            m.xt = sem(tag + "_transposed")
            m.xw = sem(tag + "_stacks")
            m.lp = sem(tag + "_logits_product")
            m.lk = sem(tag + "_logits_kept")
            m.sh = sem(tag + "_logits_shifted")
            m.ex = sem(tag + "_logits_exponentials")
            m.ws = sem(tag + "_token_weight_strings")
            m.wt = sem(tag + "_token_weights_transposed")
            m.wk = sem(tag + "_token_weights_kept")
            m.a = sem(tag + "_hidden_product")
            m.b = sem(tag + "_hidden_second_product")
            m.s = sem(tag + "_hidden_activated")
            m.tc = sem(tag + "_hidden_chain") if gated else None
            m.h = sem(tag + "_hidden_ready")
            m.o = sem(tag + "_output_products")
            m.ot = sem(tag + "_output_kept")
            m.ft = sem(tag + "_output_transposed")
            m.fc = sem(tag + "_output_chain")
            m.add = sem(tag + "_output_added")
            m.done = sem(tag + "_finished")
            m.w1 = place_w([P, 3, HT * P], BF16)
            m.w3 = place_w([P, 3, HT * P], BF16) if gated else None
            m.raw1 = raw or place_w([P, HT * P])
            m.raw3 = place_w([P, HT * P]) if gated else None
            m.w2 = place_w([P, HT, D])
            m.sel = place_w([P, HT * P], BF16)
            m.rst = sb(tag + "_router_parts", [P, 3, RN], BF16)
            m.rw = sb(tag + "_router", [P, RN + 1 + RN])
            m.LG = place_r([P, TT, NE])
            m.OH = place_r([P, TT, NE])
            m.KEY = place_r([P, TT, NE])
            m.t1 = place_r([P, TT])
            m.t2 = place_r([P, TT])
            m.t3 = place_r([P, TT])
            m.WSF = place_r([P, TT * WR + P - WR], BF16)
            m.WS = m.WSF[:, 0:TT * WR].rearrange("p (t a n) -> p t a n", a=3, n=NE)
            m.WT = place_t([P, TOK], BF16)
            return m

        def experts_weights(pool, m, scale=None):
            def ch(ins):
                link(pool, p_ch, n_pool, ins)

            for w, st in ((m.raw1, m.w1),) + (((m.raw3, m.w3),) if m.gated else ()):
                if scale is not None:
                    ch(nc.gpsimd.tensor_tensor(w, w, scale.to_broadcast([P, m.HT * P]), ALU.mult))
                ch(nc.gpsimd.tensor_copy(st[:, 0, :], w))
                ch(nc.gpsimd.tensor_copy(st[0:D, 1, :], st[0:D, 0, :]))
                ch(nc.gpsimd.tensor_tensor(w, w, st[:, 0, :], ALU.subtract))
                ch(nc.gpsimd.tensor_copy(st[:, 2, :], w))
                ch(nc.gpsimd.tensor_tensor(w, w, st[:, 2, :], ALU.subtract))
                ch(nc.gpsimd.tensor_copy(st[D:P, 1, :], w[D:P, :]))
            pool.sem_inc(m.wst, 1)
            pool.wait_ge(m.raw_in, 16)
            nc.gpsimd.tensor_copy(m.sel[:, :], m.raw1).then_inc(m.wst, 1)

        def experts_pe_pre(pe, m, strings):
            prepare_pe(pe, m.str, m.xt, m.xw, (m.rsp, 1), m.rst, NE, m.lp, m.lk, strings)

        def experts_act_pre(act, m):
            prepare_act(act, m.xt, m.xw, NE, m.lp, m.lk, m.LG)
            act.wait_ge(m.sh, 1)
            nc.scalar.activation(m.LG, m.LG, ACT.Exp).then_inc(m.ex, 1)

        def softmax8(dve, m, bias=None):
            ch = lambda ins: link(dve, ln_ch, n_ln, ins)
            dve.wait_ge(m.lk, GT + 2)
            if bias is not None:
                ch(nc.vector.tensor_tensor(m.LG, m.LG, bias.unsqueeze(1).to_broadcast([P, TT, NE]), ALU.add))
            ch(nc.vector.tensor_reduce(m.t1, m.LG, AX.X, ALU.max))
            nc.vector.tensor_tensor(m.LG, m.LG, b3(m.t1, NE), ALU.subtract).then_inc(m.sh, 1)
            dve.wait_ge(m.ex, 1)
            ch(nc.vector.tensor_reduce(m.t1, m.LG, AX.X, ALU.add))
            ch(nc.vector.reciprocal(m.t1, m.t1))
            ch(nc.vector.tensor_tensor(m.LG, m.LG, b3(m.t1, NE), ALU.mult))

        def first_max(dve, m, top, oh, key, tmp):
            ch = lambda ins: link(dve, ln_ch, n_ln, ins)
            ch(nc.vector.tensor_reduce(top, m.LG, AX.X, ALU.max))
            ch(nc.vector.tensor_tensor(key, m.LG, b3(top, NE), ALU.is_equal))
            ch(nc.vector.tensor_tensor(key, key, m.rw[:, RN + 1:2 * RN + 1].unsqueeze(1).to_broadcast([P, TT, NE]), ALU.mult))
            ch(nc.vector.tensor_reduce(tmp, key, AX.X, ALU.max))
            ch(nc.vector.tensor_tensor(oh, key, b3(tmp, NE), ALU.is_equal))

        def weight_strings(dve, m, w):
            ch = lambda ins: link(dve, ln_ch, n_ln, ins)
            ch(nc.vector.memset(m.WSF[:, TT * WR:], 0.0))
            ch(nc.vector.tensor_copy(m.WS[:, :, 0, :], w))
            ch(nc.vector.tensor_tensor(w, w, m.WS[:, :, 0, :], ALU.subtract))
            ch(nc.vector.tensor_copy(m.WS[:, :, 1, :], w))
            ch(nc.vector.tensor_tensor(w, w, m.WS[:, :, 1, :], ALU.subtract))
            nc.vector.tensor_copy(m.WS[:, :, 2, :], w).then_inc(m.ws, 1)

        def experts_pe(pe, m, b2s=None):
            HT, PP = m.HT, m.PP
            pe.wait_ge(m.ws, 1)
            with pe.Fori(0, GT // 2) as i:
                for h in range(2):
                    pe.wait_ge(m.wk, i * 2 + h + 1)
                    for u in range(TPG):
                        ins = nc.tensor.transpose(bank16(6 + h)[:, u * P:(u + 1) * P],
                                                  m.WSF[:, bass.ds(((i * 2 + h) * TPG + u) * WR, P)], ident16[:, :])
                    ins.then_inc(m.wt, 1)
            pe.wait_ge(m.wk, GT + 2)
            pe.wait_ge(m.wst, 2)
            pe.sem_inc(m.o, m.CR)

            def hidden(gi, h, k):
                n, ba = gi * HT + k, (h * HT + k) % 2
                tok = bass.ds(gi * GW, GW)
                pe.wait_ge(m.h, n + 1)
                for p, w in enumerate((0, 1, 0)):
                    ins = nc.tensor.matmul(PS[:, ba, 0:GW], m.w1[:, p, k * P:(k + 1) * P], W[:, w, tok],
                                           start=(p == 0), stop=(p == 2))
                ins.then_inc(m.a, 1)
                if m.gated:
                    for p, w in enumerate((0, 1, 0)):
                        nc.tensor.matmul(PS[:, 2 + ba, 0:GW], m.w3[:, p, k * P:(k + 1) * P], W[:, w, tok],
                                         start=(p == 0), stop=(p == 2))
                nc.tensor.matmul(PS[:, 4 + ba, 0:GW], m.sel[:, k * P:(k + 1) * P], m.WT[:, tok],
                                 start=True, stop=True).then_inc(m.b, 1)

            def second(gi, j):
                both = 2 * j + 1 < HT
                pe.wait_ge(m.h, gi * HT + 2 * j + both + 3)
                if j == 0:
                    pe.wait_ge(m.ot, gi + 1)
                for y in range(1 + both):
                    k = 2 * j + y
                    ins = nc.tensor.matmul(PS[y * D:(y + 1) * D, 6, 0:GW], m.w2[:, k, :], m.hh[:, k % m.ring, :],
                                           start=(j == 0), stop=True, skip_group_check=True)
                if j == PP - 1 and b2s is not None:
                    for p in range(3):
                        ins = nc.tensor.matmul(PS[:, 6, 0:GW], b2s[:, p, :], m.WT[:, bass.ds(gi * GW, GW)],
                                               start=False, stop=True, skip_group_check=True)
                ins.then_inc(m.o, 1)

            def back(gi):
                pe.wait_ge(m.ot, gi + 2)
                pe.wait_ge(m.add, gi + 1)
                for a in range(TPG):
                    ins = nc.tensor.transpose(PS[:, 7, a * P:(a + 1) * P], OT[:, a * P:(a + 1) * P], ident[:, :])
                ins.then_inc(m.ft, 1)

            rest = list(range((HT - 2) // 2, PP))
            with pe.Fori(0, GT // 2) as i:
                for h in range(2):
                    gi = i * 2 + h
                    for k in range(HT):
                        hidden(gi, h, k)
                        if h and k < len(rest):
                            second(gi - 1, rest[k])
                        if k >= 3 and k % 2 and (k - 3) // 2 not in rest:
                            second(gi, (k - 3) // 2)
                        if h and k == 5:
                            back(gi - 1)
                for j in rest:
                    second(i * 2 + 1, j)
                back(i * 2 + 1)

        def experts_act(act, m, SL, func, bias=None):
            HT, PP = m.HT, m.PP
            act.sem_inc(m.wk, 2)
            with act.Fori(0, GT // 2) as i:
                for h in range(2):
                    act.wait_ge(m.wt, i * 2 + h + 1)
                    nc.scalar.copy(m.WT[:, bass.ds((i * 2 + h) * GW, GW)], bank16(6 + h)[:, 0:GW]).then_inc(m.wk, 1)
            act.sem_inc(m.ot, 1)
            act.sem_inc(m.ft, 1)

            def keep(gi):
                act.wait_ge(m.o, (gi + 1) * PP + m.CR)
                act.wait_ge(m.ft, gi + 1)
                nc.scalar.copy(OT[:, :], PS[:, 6, 0:GW]).then_inc(m.ot, 1)

            with act.Fori(0, GT // 2) as i:
                for h in range(2):
                    gi = i * 2 + h
                    for k in range(HT):
                        n, ba = gi * HT + k, (h * HT + k) % 2
                        act.wait_ge(m.a, n + 1)
                        act.wait_ge(m.h, n + 1)
                        if bias is None:
                            nc.scalar.activation(SL[:, ba, :], PS[:, ba, 0:GW], func).then_inc(m.s, 1)
                        else:
                            nc.scalar.activation(SL[:, ba, :], PS[:, ba, 0:GW], func, bias=bias[:, k:k + 1]).then_inc(m.s, 1)
                        if h and k == 2:
                            keep(gi - 1)
                keep(i * 2 + 1)

        def experts_dve(dve, m, SL, TM, dst, finish=None):
            HT, PP = m.HT, m.PP
            dve.sem_inc(m.h, 2)
            dve.sem_inc(m.add, 1)

            def add(gi):
                O = PS[:, 7, 0:GW].rearrange("p (t n) -> p t n", n=P)
                dve.wait_ge(m.ft, gi + 2)
                v = dst[:, bass.ds(gi * TPG, TPG), :]
                nc.vector.tensor_tensor(v, O[:, :, 0:D], v, ALU.add).then_inc(m.fc, 1)
                dve.wait_ge(m.fc, gi + 1)
                nc.vector.tensor_tensor(v, O[:, :, D:P], v, ALU.add).then_inc(m.add, 1)

            with dve.Fori(0, GT // 2) as i:
                for h in range(2):
                    gi = i * 2 + h
                    for k in range(HT):
                        n, ba = gi * HT + k, (h * HT + k) % 2
                        src = SL[:, ba, :]
                        dve.wait_ge(m.s, n + 1)
                        dve.wait_ge(m.b, n + 1)
                        if m.gated:
                            nc.vector.tensor_tensor(TM[:, ba, :], PS[:, 2 + ba, 0:GW], src, ALU.mult).then_inc(m.tc, 1)
                            dve.wait_ge(m.tc, n + 1)
                            src = TM[:, ba, :]
                        dve.wait_ge(m.o, gi * PP + k // 2 + 1)
                        nc.vector.tensor_tensor(m.hh[:, k % m.ring, :], PS[:, 4 + ba, 0:GW], src, ALU.mult).then_inc(m.h, 1)
                        if h and k == 6 and finish is None:
                            add(gi - 1)
                        if h and k >= 6 and finish is not None:
                            finish(gi - 1, (k - 6,))
                if finish is None:
                    add(i * 2 + 1)
                else:
                    finish(i * 2 + 1, range(10))
            dve.wait_ge(m.add, GT + 1)

        HID0 = -(-NE * int(8 / 3 * D) // P)
        pl2, pl5, pl3 = places(A2, 0), places(A5, 0), places(A3[:, :].bitcast(BF16), 0)
        f = experts("f", HID0, HID0, True, pl2, pl3, pl5, A4[:, :].rearrange("p (k n) -> p k n", n=GW), None)
        fSL, fTM = pl5([P, 2, GW]), pl5([P, 2, GW])
        fOH2 = pl3([P, TT, NE])

        def f_sp(sp):
            sp.wait_ge(b_o, GT)
            for dst, name in ((f.raw1, "f_w1"), (f.raw3, "f_w3"), (f.w2, "f_w2")):
                sp.dma_start(dst, I[name]).then_inc(f.inp, 16)
            sp.wait_ge(f.wst, 1)
            sp.dma_start(f.raw1, I["f_sel"]).then_inc(f.raw_in, 16)

        def f_pool(pool):
            pool.wait_ge(f.inp, 3 * 16)
            pool.wait_ge(f.rsp, 1)
            experts_weights(pool, f, f.rw[:, RN:RN + 1])

        def f_dve(dve):
            ch = lambda ins: link(dve, ln_ch, n_ln, ins)
            square_sums(dve, NORM_F, None)
            cr = lambda ins: link(dve, ln_ch, n_ln, ins)
            split_x(dve, n_ln, Q2, Q2, f.str, None, rms)
            softmax8(dve, f)
            first_max(dve, f, f.t1, f.OH, f.KEY, f.t3)
            cr(nc.vector.scalar_tensor_tensor(f.LG, f.OH, -2.0, f.LG, ALU.mult, ALU.add))
            first_max(dve, f, f.t2, fOH2, f.KEY, f.t3)
            cr(nc.vector.tensor_tensor(f.t3, f.t1, f.t2, ALU.add))
            cr(nc.vector.tensor_scalar(f.t3, f.t3, 1e-9, None, ALU.add))
            cr(nc.vector.reciprocal(f.t3, f.t3))
            cr(nc.vector.tensor_tensor(f.t1, f.t1, f.t3, ALU.mult))
            cr(nc.vector.tensor_tensor(f.t2, f.t2, f.t3, ALU.mult))
            cr(nc.vector.tensor_tensor(f.OH, f.OH, b3(f.t1, NE), ALU.mult))
            cr(nc.vector.tensor_tensor(fOH2, fOH2, b3(f.t2, NE), ALU.mult))
            cr(nc.vector.tensor_tensor(f.OH, f.OH, fOH2, ALU.add))
            weight_strings(dve, f, f.OH)
            experts_dve(dve, f, fSL, fTM, XN)
            nc.vector.tensor_tensor(H[:, :, :], H[:, :, :], XN[:, :, :], ALU.add).then_inc(f.done, 1)
            dve.wait_ge(f.done, 1)

        def f_act(act):
            square_sums_act(act, NORM_F, 1)
            experts_act_pre(act, f)
            experts_act(act, f, fSL, ACT.Silu)

        def f_pe(pe):
            experts_pe_pre(pe, f, None)
            experts_pe(pe, f)


        SC = 64
        NC_ = NP // SC
        lam = sb("lam", [P, 5])
        sp_ = sb("ssm_parameters", [P, 24])
        s_in = sem("s_parameters_loaded")
        s_x = sem("s_exponent_ready")
        s_e = sem("s_exponentials")
        s_a = sem("s_angle_ready")
        s_sn = sem("s_sines")
        col = lambda k: sp_[:, k:k + 1]
        STEP, MAG, TH, K, XM, E, EM1, SH, SN, CO, NR, NI, LR, DEN, AL, BE, TA, TB_, AN = range(19)

        def s_parameters(dve):
            ch = lambda ins: link(dve, ln_ch, n_ln, ins)
            tt = lambda o, a, b, op: ch(nc.vector.tensor_tensor(o, a, b, op))
            ts = lambda o, a, x, op: ch(nc.vector.tensor_scalar(o, a, x, None, op))
            dve.wait_ge(s_e, 1)
            lre, lim, up, dn = lam[:, 0:1], lam[:, 1:2], lam[:, 3:4], lam[:, 4:5]
            ts(col(LR), lre, -1.0, ALU.mult)
            tt(col(LR), col(LR), lre, ALU.min)
            tt(col(MAG), col(LR), col(STEP), ALU.mult)
            nc.vector.tensor_scalar(col(XM), col(MAG), -1.0, None, ALU.max).then_inc(s_x, 1)
            dve.wait_ge(s_x, 1)
            tt(col(TH), lim, col(STEP), ALU.mult)
            ts(col(K), col(TH), 1.0 / (2 * np.pi), ALU.mult)
            ts(col(K), col(K), 1.5 * 2.0 ** 23, ALU.add)
            ts(col(K), col(K), -1.5 * 2.0 ** 23, ALU.add)
            c1 = 6.28125
            c2 = float(np.float32(np.float32((2 * np.pi - c1) * 2 ** 20).round() / 2 ** 20))
            for c in (c1, c2, 2 * np.pi - c1 - c2):
                ch(nc.vector.scalar_tensor_tensor(col(TH), col(K), -float(c), col(TH), ALU.mult, ALU.add))
            ts(col(TH), col(TH), 3.1415925, ALU.min)
            ts(col(AN), col(TH), -3.1415925, ALU.max)
            nc.vector.tensor_scalar(col(TA), col(AN), 0.5, None, ALU.mult).then_inc(s_a, 1)
            dve.wait_ge(s_a, 1)
            dve.wait_ge(s_e, 2)
            ts(col(EM1), col(XM), 1.0 / 24, ALU.mult)
            ts(col(EM1), col(EM1), 1.0 / 6, ALU.add)
            tt(col(EM1), col(EM1), col(XM), ALU.mult)
            ts(col(EM1), col(EM1), 0.5, ALU.add)
            tt(col(EM1), col(EM1), col(XM), ALU.mult)
            ts(col(EM1), col(EM1), 1.0, ALU.add)
            tt(col(EM1), col(EM1), col(XM), ALU.mult)
            ts(col(TB_), col(MAG), -0.01, ALU.is_ge)
            tt(col(EM1), col(EM1), col(TB_), ALU.mult)
            ts(col(TB_), col(TB_), -1.0, ALU.mult)
            ts(col(TB_), col(TB_), 1.0, ALU.add)
            ts(col(NR), col(E), -1.0, ALU.add)
            tt(col(NR), col(NR), col(TB_), ALU.mult)
            tt(col(EM1), col(EM1), col(NR), ALU.add)
            dve.wait_ge(s_sn, 2)
            tt(col(SH), col(SH), col(SH), ALU.mult)
            ts(col(SH), col(SH), -2.0, ALU.mult)
            ts(col(CO), col(SH), 1.0, ALU.add)
            tt(col(NR), col(E), col(SH), ALU.mult)
            tt(col(NR), col(NR), col(EM1), ALU.add)
            tt(col(NI), col(E), col(SN), ALU.mult)
            tt(col(DEN), col(LR), col(LR), ALU.mult)
            ch(nc.vector.scalar_tensor_tensor(col(DEN), lim, lim, col(DEN), ALU.mult, ALU.add))
            ch(nc.vector.reciprocal(col(DEN), col(DEN)))
            tt(col(TA), col(NR), col(LR), ALU.mult)
            ch(nc.vector.scalar_tensor_tensor(col(TA), col(NI), lim, col(TA), ALU.mult, ALU.add))
            tt(col(TA), col(TA), col(DEN), ALU.mult)
            tt(col(TB_), col(NI), col(LR), ALU.mult)
            tt(col(K), col(NR), lim, ALU.mult)
            tt(col(TB_), col(TB_), col(K), ALU.subtract)
            tt(col(TB_), col(TB_), col(DEN), ALU.mult)
            tt(col(AL), col(TB_), dn, ALU.mult)
            ch(nc.vector.scalar_tensor_tensor(col(AL), col(TA), up, col(AL), ALU.mult, ALU.add))
            tt(col(BE), col(TB_), up, ALU.mult)
            ch(nc.vector.scalar_tensor_tensor(col(BE), col(TA), dn, col(BE), ALU.mult, ALU.subtract))

        def s_parameters_act(act):
            act.wait_ge(s_in, 16)
            nc.scalar.activation(col(STEP), lam[:, 2:3], ACT.Exp).then_inc(s_e, 1)
            act.wait_ge(s_x, 1)
            nc.scalar.activation(col(E), col(MAG), ACT.Exp).then_inc(s_e, 1)
            act.wait_ge(s_a, 1)
            nc.scalar.activation(col(SN), col(AN), ACT.Sin).then_inc(s_sn, 1)
            nc.scalar.activation(col(SH), col(TA), ACT.Sin).then_inc(s_sn, 1)

        TAB = A0[:, :].bitcast(F32).rearrange("p (k n) -> p k n", k=2)
        ps3 = places(A3[:, :].bitcast(BF16), 2 * 3250)
        fin0 = ps3([P, 2, SC + 1])
        fin1 = ps3([P, 2, NC_])
        s_tab = sem("s_table_ready")

        def s_tables(pool):
            ch = lambda ins: link(pool, p_ch, n_pool, ins)

            def double(T, total):
                at = 1
                while at < total - 1:
                    m = min(at, total - 1 - at)
                    bc = lambda k: T[:, k, at:at + 1].to_broadcast([P, m])
                    c, s_ = T[:, 0, 1:1 + m], T[:, 1, 1:1 + m]
                    co, so = T[:, 0, at + 1:at + 1 + m], T[:, 1, at + 1:at + 1 + m]
                    tmp = ptmp[:, 0:m]
                    ch(nc.gpsimd.tensor_tensor(tmp, s_, bc(1), ALU.mult))
                    ch(nc.gpsimd.tensor_tensor(co, c, bc(0), ALU.mult))
                    ch(nc.gpsimd.tensor_tensor(co, co, tmp, ALU.subtract))
                    ch(nc.gpsimd.tensor_tensor(tmp, c, bc(1), ALU.mult))
                    ch(nc.gpsimd.tensor_tensor(so, s_, bc(0), ALU.mult))
                    ch(nc.gpsimd.tensor_tensor(so, so, tmp, ALU.add))
                    at += m

            for T in (fin0, fin1):
                ch(nc.gpsimd.memset(T[:, 0, 0:1], 1.0))
                ch(nc.gpsimd.memset(T[:, 1, 0:1], 0.0))
            ch(nc.gpsimd.tensor_copy(fin0[:, 0, 1:2], col(CO)))
            ch(nc.gpsimd.tensor_copy(fin0[:, 1, 1:2], col(SN)))
            double(fin0, SC + 1)
            ch(nc.gpsimd.tensor_copy(fin1[:, :, 1:2], fin0[:, :, SC:SC + 1]))
            double(fin1, NC_)
            pool.wait_ge(f.xw, GT + 2)
            for hb in range(2):
                cs_ = slice(hb * NC_ // 2, (hb + 1) * NC_ // 2)
                sh = [P, NC_ // 2, SC]
                hi = lambda k: fin1[:, k, cs_].unsqueeze(2).to_broadcast(sh)
                lo = lambda k: fin0[:, k, 0:SC].unsqueeze(1).to_broadcast(sh)
                o = lambda k: TAB[:, k, hb * NP // 2:(hb + 1) * NP // 2].rearrange("p (c j) -> p c j", j=SC)
                t = big.rearrange("p (c j) -> p c j", j=SC)
                ch(nc.gpsimd.tensor_tensor(t, hi(1), lo(1), ALU.mult))
                ch(nc.gpsimd.tensor_tensor(o(0), hi(0), lo(0), ALU.mult))
                ch(nc.gpsimd.tensor_tensor(o(0), o(0), t, ALU.subtract))
                ch(nc.gpsimd.tensor_tensor(t, hi(1), lo(0), ALU.mult))
                ch(nc.gpsimd.tensor_tensor(o(1), hi(0), lo(1), ALU.mult))
                ch(nc.gpsimd.tensor_tensor(o(1), o(1), t, ALU.add))
            pool.sem_inc(s_tab, 1)

        ptmp = sb("table_product", [P, SC])
        big = pl5([P, NP // 2])
        pa4 = places(A4[:, :].bitcast(BF16), 0)
        m1, m2, uu, zz, zc, zs = (pa4([P, 2, GW]) if k < 5 else None for k in range(6))
        pa5 = places(A3[:, :].bitcast(BF16), 0)
        zs = pa5([P, 2, GW])
        sB = pa5([P, 2, D])
        sQ = pa5([P, 2, P])
        sQr = pa5([P, P])
        sW = [pa5([P, 3, P], BF16), pa5([P, 3, P], BF16)]
        sC = pa5([P, 2, D])
        sCz = pa5([P, 2, D])
        rb = pa5([P, GW])
        yt = pa5([P, 2, TPG, D])
        S = Stage()
        S.w = sem("s_weights_loaded")
        S.q = sem("s_input_weights")
        S.qt = sem("s_input_weights_transposed")
        S.ws = sem("s_weight_stacks")
        S.str = sem("s_strings")
        S.xt = sem("s_transposed")
        S.xw = sem("s_stacks")
        S.p = sem("s_input_product")
        S.pf = sem("s_input_product_read")
        S.u = sem("s_sum_ready")
        S.z = sem("s_scanned")
        S.zc = sem("s_turned_back")
        S.o = sem("s_output_product")
        S.ot = sem("s_output_kept")
        S.ft = sem("s_output_transposed")
        S.oc = sem("s_output_chain")
        S.add = sem("s_output_added")

        def s_sp(sp):
            sp.wait_ge(f.done, 1)
            sp.dma_start(sB, I["s_b"]).then_inc(S.w, 16)
            sp.dma_start(sC, I["s_c"]).then_inc(S.w, 16)

        def s_dve(dve):
            layer_norm(dve, NORM_S)
            split_x(dve, n_ln, XN[:, :, :], Q2, S.str, S2, normed)
            ch = lambda ins: link(dve, ln_ch, n_ln, ins)
            dve.wait_ge(S.w, 2 * 16)
            dve.wait_ge(s_tab, 1)
            for k, (a, c) in enumerate(((AL, BE), (BE, AL))):
                v = sQ[:, k, 0:D]
                ch(nc.vector.tensor_scalar(v, sB[:, 0, :], col(a), None, ALU.mult))
                if k:
                    ch(nc.vector.tensor_scalar(v, v, -1.0, None, ALU.mult))
                ch(nc.vector.scalar_tensor_tensor(v, sB[:, 1, :], col(c), v, ALU.mult, ALU.add))
                ins = nc.vector.tensor_copy(sQ[:, k, D:P], v)
                ins.then_inc(S.q, 1)
            ch(nc.vector.tensor_tensor(sp_[:, 20:21], lam[:, 3:4], lam[:, 4:5], ALU.subtract))
            ch(nc.vector.tensor_scalar(sCz[:, 0, :], sC[:, 0, :], sp_[:, 20:21], None, ALU.mult))
            ch(nc.vector.tensor_scalar(sCz[:, 1, :], sC[:, 1, :], -1.0, None, ALU.mult))
            ch(nc.vector.memset(rb, 1.0))
            ch(nc.vector.tensor_scalar(rb, rb, col(E), None, ALU.mult))
            for k in range(2):
                dve.wait_ge(S.qt, k + 1)
                ch(nc.vector.tensor_copy(sQr, PS[:, k, 0:P]))
                split_w(dve, ln_ch, n_ln, sQr, sW[k], S.ws, k + 1)
            ch(nc.vector.tensor_tensor(H[:, :, :], H[:, :, :], XN[:, :, :], ALU.add))
            dve.sem_inc(S.pf, 2)
            dve.sem_inc(S.u, 2)
            dve.sem_inc(S.add, 2)

            def turn(gi, g, s_):
                dve.wait_ge(S.p, gi + 1)
                dve.wait_ge(S.u, gi + 1)
                t = bass.ds(g * GW, GW)
                nc.vector.tensor_tensor(m1[:, s_, :], PS[:, 2 * s_, 0:GW], TAB[:, 0, t], ALU.mult)
                nc.vector.tensor_tensor(m2[:, s_, :], PS[:, 2 * s_ + 1, 0:GW], TAB[:, 1, t], ALU.mult).then_inc(S.pf, 1)

            def sum_(gi, s_):
                dve.wait_ge(S.pf, gi + 3)
                dve.wait_ge(S.z, gi + 1)
                nc.vector.tensor_tensor(uu[:, s_, :], m1[:, s_, :], m2[:, s_, :], ALU.add).then_inc(S.u, 1)

            def scan(gi, s_, first):
                dve.wait_ge(S.u, gi + 3)
                dve.wait_ge(S.zc, gi + 1)
                dve.wait_ge(S.z, gi + 2)
                nc.vector.tensor_tensor_scan(zz[:, s_, :], rb, uu[:, s_, :], 0.0 if first else zz[:, 1 - s_, GW - 1:GW],
                                             ALU.mult, ALU.add).then_inc(S.z, 1)

            def add(gi, s_):
                O = PS[:, 6 + s_, 0:GW].rearrange("p (t n) -> p t n", n=P)
                v = H[:, bass.ds(gi * TPG, TPG), :]
                y = yt[:, s_, :, :]
                dve.wait_ge(S.ft, gi + 2)
                dve.wait_ge(S.oc, gi * 2 + 1)
                nc.vector.tensor_copy(y, O[:, :, 0:D]).then_inc(S.oc, 1)
                dve.wait_ge(S.oc, gi * 2 + 2)
                nc.vector.tensor_tensor(y, O[:, :, D:P], y, ALU.add).then_inc(S.oc, 1)
                dve.wait_ge(S.oc, gi * 2 + 3)
                nc.vector.scalar_tensor_tensor(v, y, 0.0, v, ALU.max, ALU.add).then_inc(S.add, 1)

            dve.sem_inc(S.oc, 1)
            dve.sem_inc(S.z, 2)
            for b in range(B):
                turn(b * NG, 0, b)
                sum_(b * NG, b)
                turn(b * NG + 1, 1, 1 - b)
                scan(b * NG, b, True)
                sum_(b * NG + 1, 1 - b)

                def step(g, k):
                    turn(b * NG + g, g, k)
                    scan(b * NG + g - 1, 1 - k, False)
                    sum_(b * NG + g, k)
                    add(b * NG + g - 2, k)

                with dve.Fori(1, NG // 2) as i:
                    step(i * 2, b)
                    step(i * 2 + 1, 1 - b)
                step(NG - 1, b)
                scan(b * NG + NG - 1, b, False)
                add(b * NG + NG - 2, 1 - b)
                add(b * NG + NG - 1, b)
            dve.wait_ge(S.add, GT + 2)

        def s_pool(pool):
            pool.sem_inc(S.zc, 2)

            def back(gi, g, s_):
                pool.wait_ge(S.z, gi + 3)
                pool.wait_ge(S.o, gi + 1)
                t = bass.ds(g * GW, GW)
                nc.gpsimd.tensor_tensor(zc[:, s_, :], zz[:, s_, :], TAB[:, 0, t], ALU.mult)
                nc.gpsimd.tensor_tensor(zs[:, s_, :], zz[:, s_, :], TAB[:, 1, t], ALU.mult).then_inc(S.zc, 1)

            for b in range(B):
                back(b * NG, 0, b)

                def step(g, k):
                    back(b * NG + g - 1, g - 1, 1 - k)

                with pool.Fori(1, NG // 2) as i:
                    step(i * 2, b)
                    step(i * 2 + 1, 1 - b)
                step(NG - 1, b)
                back(b * NG + NG - 1, NG - 1, b)

        def s_act(act):
            square_sums_act(act, NORM_S, 0)
            prepare_act(act, S.xt, S.xw, 0, None, None, None)
            act.sem_inc(S.ft, 1)

            def keep(gi, s_):
                act.wait_ge(S.o, gi + 3)
                act.wait_ge(S.ft, gi + 1)
                nc.scalar.copy(OT[:, :], PS[:, 4 + s_, 0:GW]).then_inc(S.ot, 1)

            for b in range(B):
                keep(b * NG, b)
                with act.Fori(0, NG // 2) as i:
                    for h in range(2):
                        keep(b * NG + i * 2 + h + 1, (b + h + 1) % 2)

        def s_pe(pe):
            for c in range(NCH):
                transposes(pe, c, S.str, S.xt, S.xw, S2)
            for k in range(2):
                pe.wait_ge(S.q, k + 1)
                nc.tensor.transpose(PS[:, k, 0:P], sQ[:, k, :], ident[:, :]).then_inc(S.qt, 1)
            pe.wait_ge(S.xw, GT + 2)
            pe.wait_ge(S.ws, 2)
            pe.sem_inc(S.o, 2)

            def inp(gi, s_):
                pe.wait_ge(S.pf, gi + 1)
                for k in range(2):
                    for p_, w in enumerate((0, 1, 0)):
                        ins = nc.tensor.matmul(PS[:, 2 * s_ + k, 0:GW], sW[k][:, p_, :], W[:, w, bass.ds(gi * GW, GW)],
                                               start=(p_ == 0), stop=(p_ == 2))
                ins.then_inc(S.p, 1)

            def outp(gi, s_):
                pe.wait_ge(S.zc, gi + 3)
                for y, z in enumerate((zc, zs)):
                    ins = nc.tensor.matmul(PS[y * D:(y + 1) * D, 4 + s_, 0:GW], sCz[:, y, :], z[:, s_, :],
                                           start=True, stop=True, skip_group_check=True)
                ins.then_inc(S.o, 1)

            def fin(gi, s_):
                pe.wait_ge(S.ot, gi + 1)
                pe.wait_ge(S.add, gi + 1)
                for a in range(TPG):
                    ins = nc.tensor.transpose(PS[:, 6 + s_, a * P:(a + 1) * P], OT[:, a * P:(a + 1) * P], ident[:, :])
                ins.then_inc(S.ft, 1)

            for b in range(B):
                inp(b * NG, b)
                inp(b * NG + 1, 1 - b)

                def step(g, k):
                    inp(b * NG + g, k)
                    outp(b * NG + g - 2, k)
                    fin(b * NG + g - 2, k)

                with pe.Fori(1, NG // 2) as i:
                    step(i * 2, b)
                    step(i * 2 + 1, 1 - b)
                step(NG - 1, b)
                for g, k in ((NG - 2, 1 - b), (NG - 1, b)):
                    outp(b * NG + g, k)
                    fin(b * NG + g, k)

        HID1 = NE * F1 // P
        CAP = -(-5 * B * N // (4 * NE))
        qa5, qa0, qa3 = places(A5, 0), places(A0, 0), places(A3[:, :].bitcast(BF16), 0)
        qa4 = places(A4[:, :].bitcast(BF16), 0)
        ghh = qa4([P, 8, GW])
        gSL = qa4([P, 2, GW])
        g_ = experts("g", HID1, 8, False, qa5, qa0, qa3, ghh, None)
        gb1 = qa5([P, HID1])
        gb2 = qa5([WR, D])
        gb2s = qa5([P, 3, P], BF16)
        gbias = qa5([P, NE])
        upto = qa5([P, P])
        ones = qa5([P, P])
        TOTT = qa0([P, NE, TT])
        SCN = qa0([P, NE, TT])
        smask = qa5([P, NE, TT])
        gy, gz, gmask = (qa0([P, TPG, D]) for _ in range(3))
        limit = qa0([P, 3])
        g_.cum = sem("g_positions_counted")
        g_oh = sem("g_choice_ready")

        def g_sp(sp):
            sp.wait_ge(f.done, 1)
            sp.wait_ge(s_tab, 1)
            for dst, name in ((g_.raw1, "g_w1"), (g_.w2, "g_w2"), (gb1, "g_b1"), (gb2, "g_b2"), (gbias, "g_bias"), (upto, "upto")):
                sp.dma_start(dst, I[name]).then_inc(g_.inp, 16)
            sp.wait_ge(g_.wst, 1)
            sp.dma_start(g_.raw1, I["g_sel"]).then_inc(g_.raw_in, 16)

        def g_pool(pool):
            pool.wait_ge(g_.inp, 6 * 16)
            experts_weights(pool, g_)

        def g_dve(dve):
            layer_norm(dve, NORM_G)
            cr = lambda ins: link(dve, ln_ch, n_ln, ins)
            dve.wait_ge(g_.inp, 6 * 16)
            split_x(dve, n_ln, XN[:, :, :], Q2, g_.str, S2, normed)
            cr(nc.vector.memset(ones, 1.0))
            cr(nc.vector.memset(gb2s, 0.0))
            cr(nc.vector.memset(smask, 1.0))
            cr(nc.vector.memset(smask[:, :, 0:1], 0.0))
            for k in range(3):
                cr(nc.vector.tensor_copy(gb2s[0:WR, k, 0:D], gb2))
                if k < 2:
                    cr(nc.vector.tensor_tensor(gb2, gb2, gb2s[0:WR, k, 0:D], ALU.subtract))
            softmax8(dve, g_, gbias)
            first_max(dve, g_, g_.t1, g_.OH, g_.KEY, g_.t3)
            nc.vector.tensor_tensor(g_.OH, g_.OH, b3(valid[:, :], NE), ALU.mult).then_inc(g_oh, 1)
            dve.wait_ge(g_.cum, 1)
            for k in range(2):
                v = PS[:, 2 + k, 0:NT * NE].rearrange("p (t e) -> p e t", e=NE)
                cr(nc.vector.tensor_copy(TOTT[:, :, k * NT:(k + 1) * NT], v))
            fl = lambda a: a.rearrange("p e t -> p (e t)")
            cr(nc.vector.tensor_tensor_scan(fl(SCN), fl(smask), fl(TOTT), 0.0, ALU.mult, ALU.add))
            cr(nc.vector.tensor_tensor(SCN, SCN, TOTT, ALU.subtract))
            for k in range(2):
                tl = slice(k * NT, (k + 1) * NT)
                cr(nc.vector.tensor_tensor(g_.KEY[:, tl, :], PS[:, k, 0:NT * NE].rearrange("p (t e) -> p t e", e=NE),
                                           SCN[:, :, tl].rearrange("p e t -> p t e"), ALU.add))
            cr(nc.vector.tensor_tensor(g_.KEY, g_.KEY, g_.OH, ALU.mult))
            cr(nc.vector.tensor_reduce(g_.t2, g_.KEY, AX.X, ALU.add))
            cr(nc.vector.tensor_scalar(g_.t2, g_.t2, float(CAP), None, ALU.is_le))
            cr(nc.vector.tensor_tensor(g_.t1, g_.t1, g_.t2, ALU.mult))
            cr(nc.vector.tensor_tensor(g_.OH, g_.OH, b3(g_.t1, NE), ALU.mult))
            weight_strings(dve, g_, g_.OH)
            cr(nc.vector.memset(limit[:, 0:1], 1e4))
            cr(nc.vector.memset(limit[:, 1:2], -1e4))
            mask = gmask.bitcast(mybir.dt.uint32)
            STEPS = 9

            def finish(gi, steps):
                O = PS[:, 7, 0:GW].rearrange("p (t n) -> p t n", n=P)
                v = H[:, bass.ds(gi * TPG, TPG), :]
                for k in steps:
                    if k:
                        dve.wait_ge(g_.fc, gi * STEPS + k)
                    else:
                        dve.wait_ge(g_.ft, gi + 2)
                    if k in (4, 6, 8):
                        nc.vector.memset(limit[:, 2:3], 0.0)
                    if k == 0:
                        ins = nc.vector.tensor_copy(gy, O[:, :, 0:D])
                    elif k == 1:
                        ins = nc.vector.tensor_tensor(gy, O[:, :, D:P], gy, ALU.add)
                    elif k == 2:
                        ins = nc.vector.tensor_tensor(gmask, gy, gy, ALU.is_equal)
                    elif k == 3:
                        ins = nc.vector.memset(gz, 0.0)
                    elif k == 4:
                        ins = nc.vector.copy_predicated(gz, mask, gy)
                    elif k == 5:
                        ins = nc.vector.tensor_scalar(gmask, gz, 3.4028235e38, None, ALU.is_gt)
                    elif k == 7:
                        ins = nc.vector.tensor_scalar(gmask, gz, -3.4028235e38, None, ALU.is_lt)
                    elif k in (6, 8):
                        ins = nc.vector.copy_predicated(gz, mask, limit[:, k // 2 - 3:k // 2 - 2].unsqueeze(2).to_broadcast([P, TPG, D]))
                    else:
                        ins = nc.vector.tensor_tensor(v, gz, v, ALU.add)
                    ins.then_inc(g_.add if k == 9 else g_.fc, 1)

            experts_dve(dve, g_, gSL, None, None, finish)
            dve.sem_inc(g_.done, 1)

        def g_act(act):
            square_sums_act(act, NORM_G, 0)
            experts_act_pre(act, g_)
            experts_act(act, g_, gSL, ACT.Relu, gb1)

        def g_pe(pe):
            experts_pe_pre(pe, g_, S2)
            pe.wait_ge(g_oh, 1)
            for m in range(2):
                for k in range(2):
                    ins = nc.tensor.matmul(PS[:, 2 * m + k, 0:NT * NE], (upto, ones)[m],
                                           g_.OH[:, k * NT:(k + 1) * NT, :].rearrange("p t e -> p (t e)"), start=True, stop=True)
            ins.then_inc(g_.cum, 1)
            experts_pe(pe, g_, gb2s)

        @block.sync
        def _(sp):
            sp.dma_start(lam[:, :], I["lam"]).then_inc(s_in, 16)
            sp.dma_start(bnp[:, :], I["bnp"]).then_inc(t_x0, 16)
            sp.dma_start(c1w[:, :], I["c1w"]).then_inc(t_x0, 16)
            sp.dma_start(c2w, I["c2w"]).then_inc(t_x0, 16)
            sp.dma_start(x_pad[:, 0:2 * RG + 2, :], I["xpad"][:, 0:2 * RG + 2, :]).then_inc(t_x0, 16)
            sp.dma_start(b2[:, :], I["b2"]).then_inc(t_x0, 16)
            sp.dma_start(x_pad[:, 2 * RG + 2:, :], I["xpad"][:, 2 * RG + 2:, :]).then_inc(t_in, 16)
            sp.dma_start(ident[:, :], I["ident"]).then_inc(c_in, 16)
            sp.dma_start(f.rw[:, :], I["f_r"]).then_inc(c_in, 16)
            sp.dma_start(g_.rw[:, :], I["g_r"]).then_inc(c_in, 16)
            sp.dma_start(valid[:, :], I["valid"]).then_inc(c_in, 16)
            sp.dma_start(qk2[:, :, :], I["qk"]).then_inc(c_in, 16)
            sp.wait_ge(t_a, 8 * (IMG // RG))
            sp.dma_start(scratch.rearrange("b (c h) w -> (b c) (h w)", h=IMG), conv).then_inc(t_out, 16)
            sp.wait_ge(t_out, 16)
            for b in range(B):
                t0 = b * NT
                sp.dma_start(H[0:1, t0, :], I["cls"]).then_inc(h_in, 16)
                sp.dma_start(H[1:P, t0, :], scratch[b, 0:P - 1, :]).then_inc(h_in, 16)
                sp.dma_start(H[:, t0 + 1:t0 + NT - 1, :],
                             scratch[b, P - 1:P - 1 + (NT - 2) * P, :].rearrange("(t p) d -> p t d", p=P)).then_inc(h_in, 16)
                sp.dma_start(H[0:1, t0 + NT - 1, :], scratch[b, IMG * IMG - 1:IMG * IMG, :]).then_inc(h_in, 16)
                sp.dma_start(H[1:P, t0 + NT - 1, :], I["cls"].to_broadcast([P - 1, D])).then_inc(h_in, 16)
            b_sp(sp)
            b_sp_rows(sp)
            f_sp(sp)
            s_sp(sp)
            g_sp(sp)
            sp.wait_ge(g_.done, 1)
            for b in range(B):
                sp.dma_start(out[b, 0:N - 1, :].rearrange("(t p) d -> p t d", p=P), H[:, b * NT:(b + 1) * NT - 1, :]).then_inc(o_out, 16)
                sp.dma_start(out[b, N - 1:N, :], H[0:1, (b + 1) * NT - 1, :]).then_inc(o_out, 16)
            sp.wait_ge(o_out, 4 * 16)

        @block.tensor
        def _(pe):
            pe.wait_ge(t_x0, 5 * 16)

            def conv1(r):
                if r == 2:
                    pe.wait_ge(t_in, 16)
                if r >= 2:
                    pe.wait_ge(t_ys, r - 1)
                nc.tensor.matmul(PS[0:B * CR, r % 2, :].rearrange("p (h w) -> p h w", w=IMG), c1w[:, :],
                                 x_pad[:, 1 + r * RG:1 + (r + 1) * RG, 1:1 + IMG], start=True, stop=True).then_inc(t_y, 1)

            conv1(0)
            conv1(1)
            pe.wait_ge(t_cw, 1)
            for r in range(IMG // RG):
                pe.wait_ge(t_y3, r + 1)
                for k in range(TAPS):
                    n = r * TAPS + k
                    if n >= 4:
                        pe.wait_ge(t_p, n - 3)
                    for w in range(2):
                        ins = nc.tensor.matmul(PS[:, 2 + n % 4, :], c2s[:, w, k, :], ys[:, r % 2, :],
                                               start=(w == 0), stop=(w == 1))
                    ins.then_inc(t_w, 1)
                if r + 2 < IMG // RG:
                    conv1(r + 2)
            pe.wait_ge(a_ch, 4)
            nc.tensor.matmul(PS[:, 2, 0:D], qkc[:, 0, :], qkc[:, 1, 0:D], start=True, stop=True).then_inc(a_m, 1)
            prepare_pe(pe, x_str, x_t, x_w, (a_ms, 1), MS, D, a_q, a_qe)
            for c in range(NCH):
                transposes(pe, c, a_qstr, a_qpt, a_qp)
            pe.wait_ge(a_qp, GT + 2)
            pe.sem_inc(a_pv, 2)

            def qk(b, g, m, k, n2):
                pe.wait_ge(a_ex, n2 + 1)
                for p, w in enumerate((0, 1, 0)):
                    ins = nc.tensor.matmul(PS[:, k % 3, 0:GW], W[:, w, bass.ds(b * NP + m * P, P)],
                                           QT[:, p, bass.ds(g * GW, GW)], start=(p == 0), stop=(p == 2))
                ins.then_inc(a_s2, 1)

            def mx(b, g, jj, u, n1):
                pe.wait_ge(a_s1f, n1 + 1)
                for p in range(2):
                    ins = nc.tensor.matmul(PS[:, 3 + u, 0:GW], QP[:, p, bass.ds((b * NG + g) * GW + u * P, P)],
                                           W[:, 0, bass.ds(b * NP + jj * GW, GW)], start=(p == 0), stop=(p == 1))
                ins.then_inc(a_s1, 1)

            def pv(n2, v, k, both, first):
                pe.wait_ge(a_ex, n2 + 4 + both)
                pe.wait_ge(a_vs, v)
                for y in range(1 + both):
                    ins = nc.tensor.matmul(PS[y * D:(y + 1) * D, 6, 0:GW], VS[:, k + y, :], PT[:, k + y, :],
                                           start=first, stop=True, skip_group_check=True)
                ins.then_inc(a_pv, 1)

            def fin(gi):
                pe.wait_ge(a_ot, gi + 2)
                for a in range(TPG):
                    ins = nc.tensor.transpose(PS[:, 7, a * P:(a + 1) * P], OT[:, a * P:(a + 1) * P], ident[:, :])
                ins.then_inc(a_ft, 1)

            def prep(gi, half, nofin=False):
                if half == 0:
                    pe.wait_ge(a_str, gi + 1)
                    if not nofin:
                        pe.wait_ge(a_o, gi)
                pe.wait_ge(a_qt, gi * 2 + half + 1)
                for w in ((0, 1), (2,))[half]:
                    for u in range(TPG):
                        o = (w % 2) * TPG + u
                        c = (0, 1, 3)[w] * D
                        ins = nc.tensor.transpose(bank16(7)[:, o * P:(o + 1) * P],
                                                  QTS[:, u, :, :].rearrange("p a n -> p (a n)")[:, c:c + P], ident16[:, :])
                ins.then_inc(a_tq, 1)

            def run(b, g, i6, n, p2, m, first=False, last=False):
                gi = b * NG + g
                n2 = gi * NT + i6 * 6
                v0 = gi * NG + i6 * 2
                n1 = (m[0] * NG + m[1]) * NT + i6 * 6 if m is not None else 0
                for k in range(n):
                    if p2:
                        qk(b, g, i6 * 6 + k, k, n2 + k)
                    if m is not None:
                        mx(*m, i6 * 2 + k // 3, k % 3, n1 + k)
                    if p2 and k == 1 and not first:
                        pv(n2 - 2, v0, 4, 1, False)
                    if p2 and k in (3, 5):
                        if first and k == 3:
                            pe.wait_ge(a_ot, gi + 1)
                        pv(n2 + k - 3, v0 + 1 + (k - 2) // 3, k - 3, 1, first and k == 3)
                if p2 and last:
                    pv(n2, v0 + 1, 0, 1, False)
                    pv(n2 + 2, v0 + 1, 2, 0, False)

            def step(b, g, m, pr, before=True):
                gi = b * NG + g
                pe.wait_ge(a_qt, gi * 2 + 3)
                run(b, g, 0, 6, True, m, first=True)
                if before:
                    fin(gi - 1)
                if pr:
                    prep(gi + 1, 0)
                with pe.Fori(1, 3) as i6:
                    run(b, g, i6, 6, True, m)
                if pr:
                    prep(gi + 1, 1)
                with pe.Fori(3, 5) as i6:
                    run(b, g, i6, 6, True, m)
                run(b, g, 5, 3, True, m, last=True)

            for g in range(2):
                with pe.Fori(0, 5) as i6:
                    run(0, 0, i6, 6, False, (0, g))
                run(0, 0, 5, 3, False, (0, g))
                if g == 0:
                    prep(0, 0, nofin=True)
                    prep(0, 1)
            for b in range(B):
                more = b + 1 < B
                step(b, 0, (b, 2), True, before=b > 0)
                with pe.Fori(1, NG - 2) as g:
                    step(b, g, (b, g + 2), True)
                step(b, NG - 2, (b + 1, 0) if more else None, True)
                step(b, NG - 1, (b + 1, 1) if more else None, more)
            fin(GT - 1)
            b_pe(pe)
            bo_pe(pe)
            f_pe(pe)
            s_pe(pe)
            g_pe(pe)

        @block.scalar
        def _(act):
            s_parameters_act(act)
            act.wait_ge(t_x0, 5 * 16)
            act.wait_ge(c_id, 1)
            nc.scalar.activation(bns[:, 0:1], bnp[:, 4:5], ACT.Sqrt, bias=epsc[0:B * CR, 0:1]).then_inc(t_std, 1)
            act.wait_ge(t_bn, 1)
            Q = B * CR
            for r in range(IMG // RG):
                act.wait_ge(t_y, r + 1)
                if r >= 2:
                    act.wait_ge(t_w, (r - 1) * TAPS)
                for dst in (yv[:, r % 2, :], ys[0:Q, r % 2, :], ys[3 * Q:4 * Q, r % 2, :]):
                    ins = nc.scalar.activation(dst, PS[0:Q, r % 2, :], ACT.Relu, bias=bns[:, 3:4], scale=bns[:, 1:2])
                ins.then_inc(t_ys, 1)
                act.wait_ge(t_r1, r + 1)
                nc.scalar.copy(y2[:, :], yr[:, :])
                nc.scalar.copy(ys[Q:2 * Q, r % 2, :], yr[:, :]).then_inc(t_y2, 1)
                act.wait_ge(t_r2, r + 1)
                nc.scalar.copy(ys[2 * Q:3 * Q, r % 2, :], yr[:, :]).then_inc(t_y3, 1)
            square_sums_act(act, NORM_A, 0)
            prepare_act(act, x_t, x_w, D, a_q, a_qe, Q2)
            for c in range(NCH):
                stack_copies(act, c, a_qpt, a_qp, QP)
            act.sem_inc(a_ex, 3)
            act.sem_inc(a_qt, 1)

            def prep(gi, g, half):
                act.wait_ge(a_tq, gi * 2 + half + 1)
                ws = ((0, 2), (2, 3))[half]
                k = ws[1] - ws[0]
                nc.scalar.copy(QT[:, ws[0]:ws[1], bass.ds(g * GW, GW)],
                               bank16(7)[:, 0:k * GW].rearrange("p (w n) -> p w n", w=k)).then_inc(a_qt, 1)

            def run(gi, i6, n, need):
                for k in range(n):
                    n2 = gi * NT + i6 * 6 + k
                    act.wait_ge(a_s2, n2 + 1)
                    if k % 2 == 0:
                        act.wait_ge(a_pv, gi * NPAIR + i6 * 3 + need[k // 2] + 2)
                    nc.scalar.activation(PT[:, k, :], PS[:, k % 3, 0:GW], ACT.Exp).then_inc(a_ex, 1)

            def step(b, g, column):
                gi = b * NG + g
                run(gi, 0, 6, (-1, 0, 0))
                if column is not None:
                    prep(gi + 1, column, 0)
                with act.Fori(1, 3) as i6:
                    run(gi, i6, 6, (-2, -1, 0))
                if column is not None:
                    prep(gi + 1, column, 1)
                with act.Fori(3, 5) as i6:
                    run(gi, i6, 6, (-2, -1, 0))
                run(gi, 5, 3, (-2, -1))

            prep(0, 0, 0)
            prep(0, 0, 1)
            for b in range(B):
                with act.Fori(0, NG - 2) as g:
                    step(b, g, g + 1)
                step(b, NG - 2, NG - 1)
                step(b, NG - 1, 0 if b + 1 < B else None)
            square_sums_act(act, NORM_B, 0)
            b_act(act)
            bo_act(act)
            f_act(act)
            s_act(act)
            g_act(act)

        @block.gpsimd
        def _(pool):
            for r in range(IMG // RG):
                acc = conv[:, r * 512:(r + 1) * 512]
                for k in range(1, TAPS):
                    n = r * (TAPS - 1) + k - 1
                    pool.wait_ge(t_p, r * TAPS + k + 1)
                    if n:
                        pool.wait_ge(t_a, n)
                    nc.gpsimd.tensor_tensor(acc, acc, tapp[:, n % SLOT, :], ALU.add).then_inc(t_a, 1)

            def stage(gi, b, i6, t, need):
                pool.wait_ge(x_str, NCH)
                pool.wait_ge(a_pv, gi * NPAIR + i6 * 3 + need + 2)
                j = bass.ds(b * NT + i6 * 6 + 3 * t, 3)
                nc.gpsimd.tensor_tensor(VS[:, 3 * t:3 * t + 3, :], VA[:, j, :],
                                        valid[:, j].unsqueeze(2).to_broadcast([P, TPG, D]), ALU.mult).then_inc(a_vs, 1)

            for b in range(B):
                with pool.Fori(0, NG) as g:
                    gi = b * NG + g
                    stage(gi, b, 0, 0, 0)
                    stage(gi, b, 0, 1, 0)
                    with pool.Fori(1, 5) as i6:
                        stage(gi, b, i6, 0, -1)
                        stage(gi, b, i6, 1, 0)
                    stage(gi, b, 5, 0, -1)
            b_pool(pool)
            f_pool(pool)
            s_tables(pool)
            g_pool(pool)
            s_pool(pool)

        @block.vector
        def _(dve):
            nc.vector.memset(epsc[:, 0:1], EPS)
            nc.vector.memset(epsc[:, 1:2], 1e-6)
            s_parameters(dve)
            dve.wait_ge(c_in, 5 * 16)
            nc.vector.tensor_copy(ident16[:, :], ident[:, :]).then_inc(c_id, 1)
            dve.wait_ge(t_std, 1)
            link(dve, ln_ch, n_ln, nc.vector.reciprocal(bns[:, 0:1], bns[:, 0:1]))
            link(dve, ln_ch, n_ln, nc.vector.tensor_tensor(bns[:, 1:2], bnp[:, 1:2], bns[:, 0:1], ALU.mult))
            link(dve, ln_ch, n_ln, nc.vector.tensor_tensor(bns[:, 2:3], bnp[:, 0:1], bnp[:, 3:4], ALU.subtract))
            nc.vector.scalar_tensor_tensor(bns[:, 3:4], bns[:, 2:3], bns[:, 1:2], bnp[:, 2:3], ALU.mult,
                                           ALU.add).then_inc(t_bn, 1)
            cw = lambda ins: link(dve, ln_ch, n_ln, ins)
            dve.wait_ge(t_x0, 5 * 16)
            Q = B * CR
            A_, B_ = c2s[:, 0, :, :], c2s[:, 1, :, :]
            cw(nc.vector.memset(B_, 0.0))
            cw(nc.vector.tensor_copy(A_, c2w))
            cw(nc.vector.tensor_tensor(c2w, c2w, A_, ALU.subtract))
            cw(nc.vector.tensor_copy(A_[3 * Q:, :, :], c2w[3 * Q:, :, :]))
            cw(nc.vector.tensor_copy(B_[Q:2 * Q, :, :], c2w[Q:2 * Q, :, :]))
            cw(nc.vector.tensor_copy(B_[0:Q, :, :], c2w[0:Q, :, :]))
            cw(nc.vector.tensor_tensor(c2w[0:Q, :, :], c2w[0:Q, :, :], B_[0:Q, :, :], ALU.subtract))
            nc.vector.tensor_copy(B_[0:Q, :, :], c2w[0:Q, :, :]).then_inc(t_cw, 1)

            def routers():
                cw(nc.vector.tensor_tensor(f.rw[:, 0:RN], f.rw[:, 0:RN], f.rw[:, RN:RN + 1].to_broadcast([P, RN]), ALU.mult))
                split_w(dve, ln_ch, n_ln, f.rw[:, 0:RN], f.rst, f.rsp, 1)
                split_w(dve, ln_ch, n_ln, g_.rw[:, 0:RN], g_.rst, g_.rsp, 1)


            def rest1(r):
                dve.wait_ge(t_ys, r + 1)
                if r:
                    dve.wait_ge(t_y3, r)
                nc.vector.tensor_tensor(yr[:, :], yv[:, r % 2, :], ys[0:Q, r % 2, :], ALU.subtract).then_inc(t_r1, 1)

            def rest2(r):
                dve.wait_ge(t_y2, r + 1)
                nc.vector.tensor_tensor(yr[:, :], yr[:, :], y2[:, :], ALU.subtract).then_inc(t_r2, 1)

            rest1(0)
            rest2(0)
            for r in range(IMG // RG):
                for k in range(TAPS):
                    n = r * TAPS + k
                    m = r * (TAPS - 1) + k - 1
                    di, dj = k // 3, k % 3
                    dve.wait_ge(t_w, n + 1)
                    if n == 2 * TAPS:
                        dve.wait_ge(t_in, 16)
                    if k:
                        if m >= SLOT:
                            dve.wait_ge(t_a, m - SLOT + 1)
                        dst = tapp[:, m % SLOT, :]
                    else:
                        dst = conv[:, r * 512:(r + 1) * 512]
                    nc.vector.scalar_tensor_tensor(dst.rearrange("p (h w) -> p h w", w=IMG),
                                                   PS[:, 2 + n % 4, :].rearrange("p (h w) -> p h w", w=IMG), b2[:, k:k + 1],
                                                   x_pad[:, r * RG + di:r * RG + di + RG, dj:dj + IMG],
                                                   ALU.add, ALU.mult).then_inc(t_p, 1)
                    if r + 1 < IMG // RG and k == 2:
                        rest1(r + 1)
                    if r + 1 < IMG // RG and k == 6:
                        rest2(r + 1)
            n_a = [0]
            ch = lambda ins: link(dve, a_ch, n_a, ins)
            ch(nc.vector.tensor_reduce(qks[:, :], qk2[:, :, :], AX.X, ALU.add))
            ch(nc.vector.tensor_scalar(qks[:, :], qks[:, :], -1.0 / D, None, ALU.mult))
            ch(nc.vector.tensor_tensor(qkc[:, :, 0:D], qk2[:, :, :], qks[:, :].unsqueeze(2).to_broadcast([D, 2, D]), ALU.add))
            ch(nc.vector.tensor_copy(qkc[:, :, D:P], qkc[:, :, 0:D]))
            dve.wait_ge(a_m, 1)
            ch(nc.vector.tensor_scalar(mres[:, :], PS[:, 2, 0:D], float(D) ** -0.5, None, ALU.mult))
            split_w(dve, a_ch, n_a, mres[:, :], MS, a_ms, 1)
            routers()
            dve.wait_ge(h_in, 10 * 16)
            layer_norm(dve, NORM_A)

            def a_normed(ch, tl):
                normed(ch, tl)
                ch(nc.vector.tensor_scalar(XN[:, tl, :], XN[:, tl, :], 1.0, None, ALU.add))

            split_x(dve, n_ln, XN[:, :, :], Q2, x_str, None, a_normed)
            for c, (lo, hi) in enumerate(CHUNKS):
                tl = slice(2 * TPG * lo, 2 * TPG * hi)
                dve.wait_ge(a_qe, 2 * hi + 2)
                s = xstr.rearrange("p t (a n) -> p t a n", n=D)[:, tl, :, :]
                ch(nc.vector.tensor_copy(s[:, :, 0, :], Q2[:, tl, :]))
                ch(nc.vector.tensor_copy(s[:, :, 1, :], s[:, :, 0, :]))
                ch(nc.vector.tensor_tensor(qrest[:, tl, :], Q2[:, tl, :], s[:, :, 0, :], ALU.subtract))
                ch(nc.vector.tensor_copy(s[:, :, 2, :], qrest[:, tl, :]))
                nc.vector.tensor_copy(s[:, :, 3, :], s[:, :, 2, :]).then_inc(a_qstr, 1)

            dve.sem_inc(a_s1f, 3)
            dve.sem_inc(a_ot, 1)
            dve.sem_inc(a_o, 1)

            def maxima(gi, lo=0, hi=NG):
                with dve.Fori(lo, hi) as jj:
                    for u in range(TPG):
                        dve.wait_ge(a_s1, gi * NT + jj * TPG + u + 1)
                        nc.vector.tensor_reduce(MX[:, u, bass.ds(jj, 1)], PS[:, 3 + u, 0:GW], AX.X, ALU.max).then_inc(a_s1f, 1)

            CH = 7

            def prep(gi, g, b):
                k = [gi * CH]

                def chn(ins):
                    ins.then_inc(a_pc, 1)
                    k[0] = k[0] + 1
                    dve.wait_ge(a_pc, k[0])

                dve.wait_ge(a_s1f, (gi + 1) * NT + 3)
                chn(nc.vector.tensor_reduce(mm[:, 0, :], MX[:, :, :], AX.X, ALU.max))
                chn(nc.vector.tensor_scalar(mm[:, 1, :], mm[:, 0, :], -1.0 / D, None, ALU.mult))
                chn(nc.vector.tensor_tensor(qtm[:, :, :], Q2[:, bass.ds(gi * TPG, TPG), :],
                                            mm[:, 1, :].unsqueeze(2).to_broadcast([P, TPG, D]), ALU.add))
                dve.wait_ge(a_tq, gi * 2)
                chn(nc.vector.tensor_copy(QTS[:, :, 0:2, :], qtm[:, :, :].unsqueeze(2).to_broadcast([P, TPG, 2, D])))
                chn(nc.vector.tensor_tensor(qtm[:, :, :], qtm[:, :, :], QTS[:, :, 0, :], ALU.subtract))
                chn(nc.vector.tensor_copy(QTS[:, :, 3:5, :], qtm[:, :, :].unsqueeze(2).to_broadcast([P, TPG, 2, D])))
                chn(nc.vector.tensor_tensor(qtm[:, :, :], qtm[:, :, :], QTS[:, :, 3, :], ALU.subtract))
                nc.vector.tensor_copy(QTS[:, :, 2, :], qtm[:, :, :]).then_inc(a_str, 1)

            def keep(gi):
                dve.wait_ge(a_pv, (gi + 1) * NPAIR + 2)
                nc.vector.tensor_copy(OT[:, :], PS[:, 6, 0:GW]).then_inc(a_ot, 1)

            FC = 5

            def fin(gi):
                O = PS[:, 7, 0:GW].rearrange("p (t n) -> p t n", n=P)
                k = [gi * FC]

                def chf(ins):
                    ins.then_inc(o_ch, 1)
                    k[0] = k[0] + 1
                    dve.wait_ge(o_ch, k[0])

                dve.wait_ge(a_o, gi + 1)
                dve.wait_ge(a_ft, gi + 1)
                chf(nc.vector.tensor_reduce(orec[:, :], O, AX.X, ALU.add))
                chf(nc.vector.tensor_scalar(orec[:, :], orec[:, :], 1.0 / D, None, ALU.mult))
                chf(nc.vector.reciprocal(orec[:, :], orec[:, :]))
                r = orec[:, :].unsqueeze(2).to_broadcast([P, TPG, P])
                chf(nc.vector.tensor_tensor(ot[:, :, :], O, r, ALU.mult))
                chf(nc.vector.tensor_tensor(ot[:, :, 0:D], ot[:, :, 0:D], ot[:, :, D:P], ALU.add))
                hv = H[:, bass.ds(gi * TPG, TPG), :]
                nc.vector.scalar_tensor_tensor(hv, ot[:, :, 0:D], -1.0, hv, ALU.add, ALU.add).then_inc(a_o, 1)

            def step(b, g, p1, pr, before=True):
                gi = b * NG + g
                if pr is not None:
                    prep(gi + pr, g + pr, b)
                if p1 is not None:
                    maxima(gi + p1, 0, 2)
                if before:
                    fin(gi - 1)
                if p1 is not None:
                    maxima(gi + p1, 2, NG)
                keep(gi)

            maxima(0)
            prep(0, 0, 0)
            maxima(1)
            for b in range(B):
                more = b + 1 < B
                step(b, 0, 2, 1, before=b > 0)
                with dve.Fori(1, NG - 2) as g:
                    step(b, g, 2, 1)
                step(b, NG - 2, 2 if more else None, 1)
                step(b, NG - 1, 2 if more else None, 1 if more else None)
            fin(GT - 1)
            b_dve(dve)
            bo_dve(dve)
            f_dve(dve)
            s_dve(dve)
            g_dve(dve)


def selection(rows, tiles):
    s = np.zeros((3, 8, tiles * P), np.float32)
    for e in range(8):
        s[:, e, e * rows:(e + 1) * rows] = 1.0
    return np.pad(s.reshape(24, tiles * P), ((0, P - 24), (0, 0)))


def f_layout(L, f):
    hid = int(8 / 3 * D)
    tiles = -(-8 * hid // P)
    pad = tiles * P - 8 * hid
    first = 9 - np.arange(1, 9, dtype=np.float32)
    for n in ("w1", "w3"):
        w = f("L0_ffn_" + n).reshape(8 * hid, D).T
        L["f_" + n] = np.tile(np.pad(w, ((0, 0), (0, pad))), (2, 1))
    w2 = np.pad(f("L0_ffn_w2").transpose(0, 2, 1).reshape(8 * hid, D), ((0, pad), (0, 0)))
    L["f_w2"] = w2.reshape(tiles, P, D).transpose(1, 0, 2)
    L["f_sel"] = selection(hid, tiles)
    r = np.concatenate([f("L0_ffn_router_w").T, f("L0_ffn_ln2_w")[:, None], np.tile(first, (D, 1))], axis=1)
    L["f_r"] = np.tile(r, (2, 1))


def _layout(i):
    f = lambda n: np.ascontiguousarray(np.asarray(i[n], dtype=np.float32))
    L = {}
    x = f("x").reshape(B * D, IMG, IMG)
    L["xpad"] = np.pad(x, ((0, 0), (1, 1), (1, 1)))
    w1, w2 = f("L0_tok_conv1_w"), f("L0_tok_conv2_w")
    c1 = np.zeros((B * D, B * CR), np.float32)
    c2 = np.zeros((P, TAPS, B * D), np.float32)
    for b in range(B):
        c1[b * D:(b + 1) * D, b * CR:(b + 1) * CR] = w1.T
        for q in range(4):
            c2[(q * B + b) * CR:(q * B + b + 1) * CR, :, b * D:(b + 1) * D] = w2.T[:, :, None]
    L["c1w"], L["c2w"] = c1, c2
    L["bnp"] = np.tile(np.stack([f("L0_tok_conv1_b"), f("L0_tok_bn_gamma"), f("L0_tok_bn_beta"), f("L0_tok_bn_mean"),
                                 f("L0_tok_bn_var")], axis=1), (B, 1))
    L["b2"] = np.tile(f("L0_tok_conv2_b")[None, :], (P, 1))
    L["cls"] = f("cls_tok").reshape(1, D)
    L["qk"] = np.stack([f("L0_attn_Wq"), f("L0_attn_Wk")], axis=1)
    L["ident"] = np.eye(P, dtype=np.float32)
    twice = lambda w: np.tile(w.T, (2, 1))
    L["wqkv"] = np.concatenate([twice(f("L0_ffn_wq")), twice(f("L0_ffn_wk")), twice(f("L0_ffn_wv"))], axis=1)
    L["wo"] = twice(f("L0_ffn_wo"))
    L["lnw"] = np.tile(np.stack([f("L0_ffn_ln1_w"), f("L0_ffn_ln2_w")], axis=1), (2, 1))
    inv = 1.0 / 10000.0 ** (np.arange(0, 16, 2, dtype=np.float32) / 16)
    ang = np.outer(np.arange(NP, dtype=np.float32), inv)
    L["rope"] = np.stack([np.cos(ang), np.sin(ang)]).astype(np.float32).reshape(2, NT, P, 8).transpose(2, 0, 1, 3)
    L["neg"] = np.triu(np.full((P, P), BIG), 1).astype(np.float32)
    t = (np.arange(TT)[None, :] % NT) * P + np.arange(P)[:, None]
    f_layout(L, f)
    tiles = 8 * F1 // P
    L["g_w1"] = np.tile(f("L1_ffn_w1").transpose(1, 0, 2).reshape(D, 8 * F1), (2, 1))
    L["g_w2"] = f("L1_ffn_w2").reshape(tiles, P, D).transpose(1, 0, 2)
    L["g_b1"] = f("L1_ffn_b1").reshape(tiles, P).T
    L["g_b2"] = np.tile(f("L1_ffn_b2"), (3, 1))
    L["g_bias"] = np.tile(f("L1_ffn_gate_b")[None, :], (P, 1))
    L["g_sel"] = selection(F1, tiles)
    L["g_r"] = np.tile(np.concatenate([f("L1_ffn_gate_w"), np.zeros((D, 1), np.float32),
                                       np.tile(8 - np.arange(8, dtype=np.float32), (D, 1))], axis=1), (2, 1))
    L["upto"] = np.triu(np.ones((P, P), np.float32))
    up = np.repeat([1.0, 0.0], D).astype(np.float32)
    lam = [np.tile(f("L1_attn_" + n), 2) for n in ("Lambda_re", "Lambda_im", "log_step")]
    L["lam"] = np.stack(lam + [up, 1 - up], axis=1)
    L["s_b"] = np.tile(np.stack([f("L1_attn_B_re"), f("L1_attn_B_im")], axis=1), (2, 1, 1))
    cr, ci = f("L1_attn_C_re").T, f("L1_attn_C_im").T
    L["s_c"] = np.stack([np.concatenate([cr, ci]), np.concatenate([ci, cr])], axis=1)
    L["valid"] = (t < N).astype(np.float32)
    return {k: np.ascontiguousarray(v) for k, v in L.items()}


def kernel(**inputs):
    import concourse.bacc as _bacc
    from concourse import mybir as _mybir
    from concourse.bass_utils import run_bass_kernel_spmd as _run

    nc = _bacc.Bacc("TRN2", target_bir_lowering=False, num_devices=1)
    arrays = {"in_" + k: v for k, v in _layout(inputs).items()}
    I = {k[3:]: nc.dram_tensor(k, v.shape, _mybir.dt.from_np(v.dtype), kind="ExternalInput").ap() for k, v in arrays.items()}
    out = nc.dram_tensor("out_h", (B, N, D), _mybir.dt.float32, kind="ExternalOutput").ap()
    tower(nc, I, out)
    r = _run(nc, [arrays], core_ids=[0])
    return r.results[0]["out_h"]
```
